# Optimizing a Trainium2 kernel written in Bass

```python
import numpy as np
import jax
import jax.numpy as jnp

def _softmax(x, axis=-1):
    return jax.nn.softmax(x, axis=axis)

def _gelu(x):
    return jax.nn.gelu(x, approximate=True)

def _silu(x):
    return jax.nn.silu(x)

def _sigmoid(x):
    return jax.nn.sigmoid(x)

def _layernorm(x, axis=-1, eps=1e-05):
    m = jnp.mean(x, axis=axis, keepdims=True)
    v = jnp.var(x, axis=axis, keepdims=True)
    return (x - m) / jnp.sqrt(v + eps)

def _scatter_add(tgt, idx, src, axis=0):
    return tgt.at[idx].add(src)

def _segment_sum(src, seg, n):
    return jax.ops.segment_sum(src, seg, n)
kernel_name = 'mk_gnn_ffn_d1_gnn_r8_8d056e'

def setup_inputs(seed: int=0):
    np.random.seed(seed)
    _w = jnp.asarray

    def _rec_inputs():
        import jax
        import jax.numpy as jnp
        _gk = jax.random.key(seed)
        x = -0.0006008 + 1.001 * jax.random.normal(jax.random.fold_in(_gk, 1), (6250, 256), jnp.float32)
        src = jax.random.randint(jax.random.fold_in(_gk, 2), (100000,), 0, 6250, jnp.int32)
        dst = jnp.minimum((6250 * jax.random.uniform(jax.random.fold_in(_gk, 3), (100000,)) ** 2.0).astype(jnp.int32), 49999)
        _o = jnp.argsort(dst, stable=True)
        src = src[_o]
        dst = dst[_o]
        edge_attr_3 = 0.000857669 + 1.0001 * jax.random.normal(jax.random.fold_in(_gk, 11), (100000, 3), jnp.float32)
        edge_attr_50 = 2.43349e-05 + 1.00019 * jax.random.normal(jax.random.fold_in(_gk, 12), (100000, 50), jnp.float32)
        return (x, src, dst, edge_attr_3, edge_attr_50)
    x, src, dst, edge_attr_3, edge_attr_50 = _rec_inputs()

    def _L0_gnn_setup():
        import jax, jax.numpy as jnp
        import numpy as np
        CUTOFF = 2.0
        LOG2 = float(np.log(2.0))

        def ssp(x):
            return jax.nn.softplus(x) - LOG2
        key = jax.random.key(seed)
        ks = jax.random.split(key, 12)
        N, E, H, F, G = (1250, 40000, 256, 256, 50)
        x = jax.random.normal(ks[0], (N, H), dtype=jnp.float32)
        edge_index = jax.random.randint(ks[1], (2, E), 0, N, dtype=jnp.int64)
        edge_weight = jax.random.normal(ks[2], (E, 3), dtype=jnp.float32)
        edge_attr = jax.random.normal(ks[3], (E, G), dtype=jnp.float32)
        s = lambda fan_in: 1.0 / np.sqrt(fan_in)
        mlp_w1 = jax.random.uniform(ks[4], (G, F), jnp.float32, -s(G), s(G))
        mlp_b1 = jax.random.uniform(ks[5], (F,), jnp.float32, -s(G), s(G))
        mlp_w2 = jax.random.uniform(ks[6], (F, F), jnp.float32, -s(F), s(F))
        mlp_b2 = jax.random.uniform(ks[7], (F,), jnp.float32, -s(F), s(F))
        lin1_w = jax.random.uniform(ks[8], (H, F), jnp.float32, -s(H), s(H))
        lin2_w = jax.random.uniform(ks[9], (F, H), jnp.float32, -s(F), s(F))
        lin2_b = jax.random.uniform(ks[10], (H,), jnp.float32, -s(F), s(F))
        return {'x': x, 'edge_index': edge_index, 'edge_weight': edge_weight, 'edge_attr': edge_attr, 'mlp_w1': mlp_w1, 'mlp_b1': mlp_b1, 'mlp_w2': mlp_w2, 'mlp_b2': mlp_b2, 'lin1_w': lin1_w, 'lin2_w': lin2_w, 'lin2_b': lin2_b}
    _L0_gnn_all = _L0_gnn_setup()
    _L0_gnn_in = {k: v for k, v in _L0_gnn_all.items() if k in ('mlp_w1', 'mlp_b1', 'mlp_w2', 'mlp_b2', 'lin1_w', 'lin2_w', 'lin2_b')}
    del _L0_gnn_all

    def _L0_ffn_setup():
        import jax, jax.numpy as jnp
        import numpy as np
        B, K, D = (512, 16, 256)
        E = 32
        H = int(D * 0.25)
        key = jax.random.key(seed)
        ks = jax.random.split(key, 7)
        d_rs = D ** (-0.5)
        h_rs = H ** (-0.5)
        x = jax.random.normal(ks[0], (B, K, D), dtype=jnp.float32)
        router_w = jax.random.uniform(ks[1], (E, D), jnp.float32, -d_rs, d_rs)
        router_b = jax.random.uniform(ks[2], (E,), jnp.float32, -d_rs, d_rs)
        W1 = jax.random.uniform(ks[3], (E, D, H), jnp.float32, -h_rs, h_rs)
        b1 = jax.random.uniform(ks[4], (E, H), jnp.float32, -h_rs, h_rs)
        W2 = jax.random.uniform(ks[5], (E, H, D), jnp.float32, -d_rs, d_rs)
        b2 = jax.random.uniform(ks[6], (E, D), jnp.float32, -d_rs, d_rs)
        return {'x': x, 'router_w': router_w, 'router_b': router_b, 'W1': W1, 'b1': b1, 'W2': W2, 'b2': b2}
    _L0_ffn_all = _L0_ffn_setup()
    _L0_ffn_in = {k: v for k, v in _L0_ffn_all.items() if k in ('router_w', 'router_b', 'W1', 'b1', 'W2', 'b2')}
    del _L0_ffn_all
    return {'x': x, 'src': src, 'dst': dst, 'edge_attr_3': edge_attr_3, 'edge_attr_50': edge_attr_50, 'L0_gnn_mlp_w1': _L0_gnn_in['mlp_w1'], 'L0_gnn_mlp_b1': _L0_gnn_in['mlp_b1'], 'L0_gnn_mlp_w2': _L0_gnn_in['mlp_w2'], 'L0_gnn_mlp_b2': _L0_gnn_in['mlp_b2'], 'L0_gnn_lin1_w': _L0_gnn_in['lin1_w'], 'L0_gnn_lin2_w': _L0_gnn_in['lin2_w'], 'L0_gnn_lin2_b': _L0_gnn_in['lin2_b'], 'L0_ffn_router_w': _L0_ffn_in['router_w'], 'L0_ffn_router_b': _L0_ffn_in['router_b'], 'L0_ffn_W1': _L0_ffn_in['W1'], 'L0_ffn_b1': _L0_ffn_in['b1'], 'L0_ffn_W2': _L0_ffn_in['W2'], 'L0_ffn_b2': _L0_ffn_in['b2']}

def reference(x, src, dst, edge_attr_3, edge_attr_50, L0_gnn_mlp_w1, L0_gnn_mlp_b1, L0_gnn_mlp_w2, L0_gnn_mlp_b2, L0_gnn_lin1_w, L0_gnn_lin2_w, L0_gnn_lin2_b, L0_ffn_router_w, L0_ffn_router_b, L0_ffn_W1, L0_ffn_b1, L0_ffn_W2, L0_ffn_b2):
    import jax
    import jax.numpy as jnp

    def _L0_gnn_ref(x, edge_index, edge_weight, edge_attr, mlp_w1, mlp_b1, mlp_w2, mlp_b2, lin1_w, lin2_w, lin2_b):
        import jax, jax.numpy as jnp
        import numpy as np
        CUTOFF = 2.0
        LOG2 = float(np.log(2.0))

        def ssp(x):
            return jax.nn.softplus(x) - LOG2
        N = x.shape[0]
        distances = jnp.linalg.norm(edge_weight, axis=1)
        C = 0.5 * (jnp.cos(distances * jnp.pi / CUTOFF) + 1.0)
        C = C * (distances <= CUTOFF)
        W = ssp(edge_attr @ mlp_w1 + mlp_b1) @ mlp_w2 + mlp_b2
        W = W * C[:, None]
        i, j = (edge_index[0], edge_index[1])
        messages = W * (x[j] @ lin1_w)
        agg = jax.ops.segment_sum(messages, i, num_segments=N)
        h = ssp(agg @ lin2_w + lin2_b)
        return x + h

    def _L0_ffn_ref(x, router_w, router_b, W1, b1, W2, b2):
        import jax, jax.numpy as jnp
        import numpy as np
        B, K, D = (512, 16, 256)
        E = 32
        H = int(D * 0.25)
        xf = x.reshape(-1, D)
        logits = xf @ router_w.T + router_b
        idx = jnp.argmax(logits, axis=-1)
        w1t = jnp.take(W1, idx, axis=0)
        h = jnp.einsum('nd,ndh->nh', xf, w1t) + jnp.take(b1, idx, axis=0)
        h = jax.nn.relu(h)
        w2t = jnp.take(W2, idx, axis=0)
        out = jnp.einsum('nh,nhd->nd', h, w2t) + jnp.take(b2, idx, axis=0)
        out = jax.nn.relu(out)
        return out.reshape(x.shape)
    edge_index = jnp.stack([src, dst])
    x = x + _L0_gnn_ref(_layernorm(x, axis=-1), edge_index, edge_attr_3, edge_attr_50, L0_gnn_mlp_w1, L0_gnn_mlp_b1, L0_gnn_mlp_w2, L0_gnn_mlp_b2, L0_gnn_lin1_w, L0_gnn_lin2_w, L0_gnn_lin2_b)
    x = x + _L0_ffn_ref(_layernorm(x, axis=-1)[None], L0_ffn_router_w, L0_ffn_router_b, L0_ffn_W1, L0_ffn_b1, L0_ffn_W2, L0_ffn_b2)[0]
    return x

_drawn_inputs = setup_inputs


def setup_inputs(seed=0):
    import zlib

    import numpy as np

    out = dict(_drawn_inputs(seed))
    spreads = {}
    factors = {'edge_attr_3': 11.556,
     'L0_gnn_mlp_b1': 53.311,
     'L0_gnn_mlp_b2': 41.797,
     'L0_gnn_lin2_b': 29.818,
     'L0_ffn_b1': 64.0,
     'L0_ffn_b2': 27.267,
     'edge_attr_50': 7.102,
     'L0_gnn_mlp_w1': 7.127,
     'L0_gnn_mlp_w2': 5.16,
     'L0_gnn_lin1_w': 4.062,
     'L0_gnn_lin2_w': 4.1,
     'L0_ffn_router_w': 3.578,
     'L0_ffn_router_b': 8.0,
     'L0_ffn_W1': 5.033,
     'L0_ffn_W2': 3.98}
    for name, (base, spread) in spreads.items():
        noise = np.random.default_rng([zlib.crc32(name.encode()), seed]).standard_normal(out[name].shape)
        drawn = base * np.exp(spread * noise) if base else spread * noise
        out[name] = jnp.asarray(drawn.astype(out[name].dtype))
    for name, factor in factors.items():
        out[name] = (out[name] * factor).astype(out[name].dtype)
    return out
```

```python
import math
from contextlib import ExitStack

import concourse.bass as bass
import concourse.mybir as mybir

P = 128


class Step:
    def __init__(self, q, r, u, count):
        self.q, self.r, self.u, self.count = q, r, u, count

    def __add__(self, d):
        return Step(self.q + (self.r + d) // self.u, (self.r + d) % self.u, self.u, self.count)

    @property
    def n(self):
        return self.q * self.u + self.r

    @property
    def slot(self):
        return self.r % 2

    @property
    def turn(self):
        return self.q * (self.u // 2) + self.r // 2

    def there(self):
        return not isinstance(self.q, int) or 0 <= self.n < self.count


def run_steps(eng, body, first, end, u, count):
    turns = (count - 1) // u
    for n in range(first, u):
        body(Step(n // u, n % u, u, count))
    with eng.Fori(1, turns) as q:
        for r in range(u):
            body(Step(q, r, u, count))
    for n in range(turns * u, end):
        body(Step(n // u, n % u, u, count))


def wait_apart(eng, semaphore, value, passed):
    if not isinstance(value, int) or value > 0:
        eng.wait_ge(semaphore, value)
        eng.sem_inc(passed, 1)


def wait(eng, semaphore, value):
    if not isinstance(value, int) or value > 0:
        eng.wait_ge(semaphore, value)


def gnn_moe(nc, x, src, dst, edge3, edge50, mlp_w1, mlp_b1, mlp_w2, mlp_b2, lin1_w, lin2_w, lin2_b,
            router_w, router_b, ffn_w1, ffn_b1, ffn_w2, ffn_b2, out):
    F32, F32R, BF16, I32 = mybir.dt.float32, mybir.dt.float32r, mybir.dt.bfloat16, mybir.dt.int32
    ALU, ACT, AX = mybir.AluOpType, mybir.ActivationFunctionType, mybir.AxisListType
    ds = bass.ds

    N, D = x.shape
    E, G = edge50.shape
    NX, _, H = ffn_w1.shape
    KC = D // P
    NT = -(-N // P)
    NLAST = N - (NT - 1) * P
    J = 4
    SE = J * P
    NS = -(-E // SE)
    U = 4
    LASTE = E - (NS - 1) * SE
    RB = 2
    RH = NS // RB
    FULL = (NS - 1) % RH
    DUMMY = N
    PADROW = N + P
    TR = -(-(PADROW + 1) // P) * P
    ET = NX + (N - NX) // P
    CAP = 40.0
    LN2 = math.log(2.0)
    EPS = 1e-5
    CUTOFF = 2.0
    assert NS == RB * RH and NS % U == 0 and LASTE % J == 0 and NT % 2 == 1 and ET % 2 == 0 and H < P

    z_dram = nc.dram_tensor("z_rows", [NT * P, D], F32).ap()
    dig_dram = nc.dram_tensor("src_digits", [2, NS * SE], BF16).ap()
    agg_dram = [nc.dram_tensor(f"agg_table{j}", [TR, D], F32).ap() for j in range(J)]
    xs_dram = nc.dram_tensor("sorted_rows", [ET * P, D], F32).ap()
    ys_dram = nc.dram_tensor("sorted_results", [ET * P, D], F32).ap()
    ZW = 2560
    assert (TR * D // P) % ZW == 0 and (ET * D) % ZW == 0

    ctx = ExitStack()
    with ctx:
        def sb(name, shape, dt=F32):
            return ctx.enter_context(nc.sbuf_tensor(name, shape, dt))

        def sem(name):
            return ctx.enter_context(nc.semaphore(name))

        x_sb = sb("x_sb", [P, NT, D])
        xf_sb = sb("xf_sb", [P, NT, D])
        ident = sb("ident", [P, P])
        ident_r = sb("ident_r", [P, P], F32R)
        upper = sb("upper", [P, P])
        upper_bf = sb("upper_bf", [P, P], BF16)
        ones_bf = sb("ones_bf", [P, P], BF16)
        ones_row = sb("ones_row", [1, P])
        ones_r = sb("ones_r", [33, P], F32R)
        neg_ln2 = sb("neg_ln2", [P, 1])
        dummy = sb("dummy_rows", [P, 1])
        digit_w = sb("digit_w", [2, P], BF16)
        w1_in = sb("w1_in", [P, D])
        w1_hh = sb("w1_hh", [P, D], F32R)
        w1_lo = sb("w1_lo", [G, D], F32R)
        w1_res = sb("w1_res", [G, D])
        b1_col = sb("b1_col", [P, KC])
        w2_sb = sb("w2_sb", [P, KC, D])
        b2_row = sb("b2_row", [1, D])
        b2_hl = sb("b2_hl", [33, D], F32R)
        lin1_sb = sb("lin1_sb", [P, KC, D])
        lin2_sb = sb("lin2_sb", [P, KC, D])
        lin2b_row = sb("lin2b_row", [1, D])
        rw_in = sb("rw_in", [NX, D])
        rwT = sb("rwT", [P, KC, NX])
        rb_row = sb("rb_row", [1, NX])
        stats = sb("stats", [P, NT, 6])
        mean = sb("mean", [P, NT])
        rstd = sb("rstd", [P, NT])
        tmp_n = sb("tmp_n", [P, NT])
        xn = sb("xn", [P, 2, D])
        xT = sb("xT", [P, 2, D])
        rowbuf = sb("rowbuf", [P, 2, D])
        cols = sb("cols", [P, NS, 4 * J])

        PS = ctx.enter_context(nc.psum_tensor("PS", [P, 8, 512], F32))

        w_in = sem("w_in")
        e_in = sem("e_in")
        zero_rdy = sem("zero_rdy")
        filled = sem("filled")
        consts = sem("consts")
        pool_passed = sem("pool_passed")
        pchain = sem("pchain")
        chain = sem("chain")
        chain2 = sem("chain2")
        st_rdy = sem("st_rdy")
        res_rdy = sem("res_rdy")
        xn_rdy = sem("xn_rdy")
        xnt_done = sem("xnt_done")
        xT_rdy = sem("xT_rdy")
        mmz_done = sem("mmz_done")
        zb_rdy = sem("zb_rdy")
        z_out = [sem(f"z_out{b}") for b in range(2)]
        sq_ask = sem("sq_ask")
        sq_rdy = sem("sq_rdy")
        pv_ask = sem("pv_ask")
        pv_rdy = sem("pv_rdy")
        prow_rdy = sem("prow_rdy")
        pt_done = sem("pt_done")
        pt_free = sem("pt_free")
        dig_rdy = sem("dig_rdy")
        dig_out = sem("dig_out")
        wprep = sem("wprep")
        wprep_mm = sem("wprep_mm")
        prep_done = sem("prep_done")

        def node_row(a, n):
            return a[:, ds(n, 1), :].rearrange("p a d -> p (a d)")

        def norm_bulk(vec, link, count):
            me, mo = stats[:, :, 1], stats[:, :, 4]
            link(nc.vector.tensor_tensor(mean[:], me, mo, ALU.add))
            link(nc.vector.tensor_tensor(tmp_n[:], me, mo, ALU.subtract))
            link(nc.vector.tensor_scalar(mean[:], mean[:], 0.5, None, ALU.mult))
            link(nc.vector.scalar_tensor_tensor(out=tmp_n[:], in0=tmp_n[:], scalar=0.25, in1=tmp_n[:],
                                                op0=ALU.mult, op1=ALU.mult))
            link(nc.vector.tensor_tensor(rstd[:], stats[:, :, 2], stats[:, :, 5], ALU.add))
            link(nc.vector.scalar_tensor_tensor(out=tmp_n[:], in0=rstd[:], scalar=1.0 / D, in1=tmp_n[:],
                                                op0=ALU.mult, op1=ALU.add))
            nc.vector.tensor_scalar(tmp_n[:], tmp_n[:], EPS, None, ALU.add).then_inc(sq_ask, 1)
            vec.wait_ge(sq_rdy, count)
            link(nc.vector.reciprocal(rstd[:], rstd[:]))

        part1 = ExitStack()
        with part1:
            def sb1(name, shape, dt=F32):
                return part1.enter_context(nc.sbuf_tensor(name, shape, dt))

            a_in = sb1("a_in", [P, U, J * G])
            a_hl = sb1("a_hl", [P, 2, J, P], F32R)
            aT = sb1("aT", [P, 2, SE], F32R)
            digits = sb1("digits", [2, U, SE], BF16)
            dstc = sb1("dstc", [P, U, J], I32)
            sel = sb1("sel", [P, U, 3 * J])
            capped = sb1("capped", [P, KC, SE])
            hT = sb1("hT", [P, 2, KC, SE])
            zg = sb1("zg", [P, U, J, D])
            msg = sb1("msg", [P, 2, J, D])
            same = sb1("same", [P, U, J, P])
            later = sb1("later", [P, 2, J])
            tab_f = sb1("tab_f", [P, 2, J])
            tabc = sb1("tabc", [P, U, J], I32)
            summed = xf_sb[:].rearrange("p t d -> p (t d)")[:, NT * D - U * J * D:].rearrange(
                "p (u j d) -> p u j d", u=U, j=J)

            r_int = zg[0:RH, 0].bitcast(I32).rearrange("p j d -> p (j d)")
            r_dst = zg[0:RH, 1].bitcast(I32).rearrange("p j d -> p (j d)")
            r_srcf = zg[0:RH, 2].rearrange("p j d -> p (j d)")
            r_dstf = zg[0:RH, 3].rearrange("p j d -> p (j d)")
            r_hi = msg[0:RH, 0].bitcast(I32).rearrange("p j d -> p (j d)")
            r_lo = msg[0:RH, 1].bitcast(I32).rearrange("p j d -> p (j d)")
            RW = RB * SE
            r_e3 = hT[0:RH].rearrange("p b c s -> p (b c s)")
            r_e3b = summed[0:RH, 0:2].rearrange("p u j d -> p (u j d)")
            assert ZW + 5 * RW <= NT * D - U * J * D and RW == J * D and 2 * KC * SE == 2 * RW
            spare = xf_sb[0:RH].rearrange("p t d -> p (t d)")[:, ZW:]
            r_xyz = spare[:, 0:3 * RW]
            r_dig = [spare[:, (3 + k) * RW:(3 + k) * RW + RW // 2].bitcast(BF16).rearrange(
                "p (a j q) -> p a j q", a=RB, j=J) for k in range(2)]
            r_d2 = r_e3[:, 0:RW]
            r_t = r_e3[:, RW:2 * RW]
            r_c = r_e3b[:, 0:RW]
            r_m = r_e3b[:, RW:2 * RW]

            a_ld = [sem(f"a_ld{b}") for b in range(U)]
            dg_ld = [sem(f"dg_ld{b}") for b in range(U)]
            hi_rdy = sem("hi_rdy")
            lo_rdy = sem("lo_rdy")
            at_done = sem("at_done")
            aT_rdy = sem("aT_rdy")
            dg_done = sem("dg_done")
            col_rdy = sem("col_rdy")
            dst_rdy = sem("dst_rdy")
            pre_done = sem("pre_done")
            cap_rdy = sem("cap_rdy")
            exp_done = sem("exp_done")
            ln_done = sem("ln_done")
            h_rdy = sem("h_rdy")
            w_done = sem("w_done")
            z_ld = [sem(f"z_ld{b}") for b in range(U)]
            msg_rdy = sem("msg_rdy")
            same_rdy = sem("same_rdy")
            tabf_rdy = sem("tabf_rdy")
            tab_rdy = sem("tab_rdy")
            sum_done = sem("sum_done")
            sum_rdy = sem("sum_rdy")
            added = [sem(f"added{j}") for j in range(J)]

            def sup(n):
                return Step(n // U, n % U, U, NS)

            def steps(eng, body, first):
                run_steps(eng, body, first, NS + 2, U, NS)

            with nc.Block() as block:
                @block.sync
                def _(sp):
                    sp.wait_ge(consts, 1)
                    sp.dma_start(x_sb[:, 0:NT - 1, :],
                                 x[0:(NT - 1) * P, :].rearrange("(t p) d -> p t d", p=P)).then_inc(w_in, 16)
                    sp.dma_start(x_sb[0:NLAST, NT - 1, :], x[(NT - 1) * P:N, :]).then_inc(w_in, 16)
                    sp.wait_ge(prow_rdy, 1)
                    for a in range(RB):
                        rows = RH if a < RB - 1 else FULL
                        e0, e1 = a * RH * SE, (a * RH + rows) * SE
                        for dest, arr, w in ((r_int, src, 1), (r_dst, dst, 1),
                                             (r_xyz, edge3.rearrange("e c -> (e c)"), 3)):
                            sp.dma_start(dest[0:rows, a * SE * w:(a + 1) * SE * w],
                                         arr[e0 * w:e1 * w].rearrange("(r s) -> r s", s=SE * w)).then_inc(e_in, 16)
                            if rows < RH:
                                sp.dma_start(dest[rows:rows + 1, a * SE * w:(a * SE + LASTE) * w],
                                             arr[e1 * w:E * w].rearrange("(r s) -> r s", r=1)).then_inc(e_in, 16)
                    for dest, arr in ((lin1_sb[:], lin1_w.rearrange("(c p) n -> p c n", p=P)),
                                      (w2_sb[:], mlp_w2.rearrange("(c p) n -> p c n", p=P)),
                                      (w1_in[0:G, :], mlp_w1), (w1_in[64:64 + G, :], mlp_w1),
                                      (b1_col[:, 0:1], mlp_b1[0:P].rearrange("(p c) -> p c", c=1)),
                                      (b1_col[:, 1:2], mlp_b1[P:2 * P].rearrange("(p c) -> p c", c=1)),
                                      (b2_row[:], mlp_b2.rearrange("(r n) -> r n", r=1)),
                                      (lin2_sb[:], lin2_w.rearrange("(c p) n -> p c n", p=P)),
                                      (lin2b_row[:], lin2_b.rearrange("(r n) -> r n", r=1)),
                                      (rw_in[:], router_w),
                                      (rb_row[:], router_b.rearrange("(r n) -> r n", r=1))):
                        sp.dma_start(dest, arr).then_inc(w_in, 16)
                    sp.wait_ge(zero_rdy, 1)
                    zeros = xf_sb[:].rearrange("p t d -> p (t d)")[:, 0:ZW]
                    for tab in agg_dram + [xs_dram]:
                        flat = tab.rearrange("(p k) d -> p (k d)", p=P)
                        for k in range(flat.shape[1] // ZW):
                            sp.dma_start(flat[:, k * ZW:(k + 1) * ZW], zeros).then_inc(filled, 16)
                    sp.wait_ge(dig_rdy, 2)
                    for k in range(2):
                        for a in range(RB):
                            sp.dma_start(dig_dram[k, a * RH * SE:(a + 1) * RH * SE].rearrange("(r s) -> r s", s=SE),
                                         r_dig[k][:, a].rearrange("p j q -> p (j q)")).then_inc(dig_out, 16)
                    sp.wait_ge(dig_out, 16 * 2 * RB)

                    def load(t):
                        wait(sp, hi_rdy, t.n - U + 1)
                        wait(sp, lo_rdy, t.n - U + 1)
                        wait(sp, dg_done, t.n - U + 1)
                        sp.dma_start(digits[:, t.r, :], dig_dram[:, ds(t.n * SE, SE)]).then_inc(dg_ld[t.r], 16)
                        if isinstance(t.q, int) and t.n == NS - 1:
                            k = LASTE // J
                            sp.dma_start(a_in[0:k, t.r, :],
                                         edge50[t.n * SE:E, :].rearrange("(p j) g -> p (j g)", j=J)
                                         ).then_inc(a_ld[t.r], 16)
                            sp.dma_start(a_in[k:P, t.r, :],
                                         edge50[0:(P - k) * J, :].rearrange("(p j) g -> p (j g)", j=J)
                                         ).then_inc(a_ld[t.r], 16)
                        else:
                            sp.dma_start(a_in[:, t.r, :],
                                         edge50[ds(t.n * SE, SE), :].rearrange("(p j) g -> p (j g)", j=J)
                                         ).then_inc(a_ld[t.r], 16)

                    run_steps(sp, load, 0, NS, U, NS)
                    sp.wait_ge(filled, 16 * (J * TR * D // P // ZW + ET * D // ZW))
                    for j in range(J):
                        sp.wait_ge(added[j], 16 * NS)

                @block.gpsimd
                def _(pool):
                    nc.gpsimd.memset(x_sb[:, NT - 1, :], 0.0).then_inc(consts, 1)
                    nc.gpsimd.memset(ident[:], 1.0).then_inc(pchain, 1)
                    nc.gpsimd.memset(upper[:], 1.0).then_inc(pchain, 1)
                    nc.gpsimd.memset(ones_bf[:], 1.0).then_inc(pchain, 1)
                    pool.wait_ge(pchain, 3)
                    nc.gpsimd.affine_select(out=ident[:], in_=ident[:], compare_op=ALU.is_equal, fill=0.0, base=0,
                                            pattern=[[-1, P]], channel_multiplier=1).then_inc(consts, 1)
                    nc.gpsimd.affine_select(out=upper[:], in_=upper[:], compare_op=ALU.is_ge, fill=0.0, base=0,
                                            pattern=[[1, P]], channel_multiplier=-1).then_inc(consts, 1)
                    nc.gpsimd.affine_select(out=upper_bf[:], in_=ones_bf[:], compare_op=ALU.is_gt, fill=0.0, base=0,
                                            pattern=[[1, P]], channel_multiplier=-1).then_inc(consts, 1)
                    nc.gpsimd.iota(dummy[:], pattern=[[0, 1]], base=DUMMY, channel_multiplier=1,
                                   allow_small_or_imprecise_dtypes=True).then_inc(consts, 1)
                    nc.gpsimd.memset(ones_row[:], 1.0).then_inc(consts, 1)
                    nc.gpsimd.memset(neg_ln2[:], -LN2).then_inc(consts, 1)
                    nc.gpsimd.memset(digit_w[:], 1.0).then_inc(pchain, 1)
                    pool.wait_ge(pchain, 4)
                    nc.gpsimd.memset(digit_w[0:1, :], float(P)).then_inc(consts, 1)

                    def gather(t):
                        wait_apart(pool, dst_rdy, t.n + 1, pool_passed)
                        wait_apart(pool, msg_rdy, J * (t.n - U) + J, pool_passed)
                        for j in range(J):
                            nc.gpsimd.indirect_dma_start(
                                out=zg[:, t.r, j, :], out_offset=None, in_=z_dram,
                                in_offset=bass.IndirectOffsetOnAxis(ap=dstc[:, t.r, j:j + 1], axis=0)
                            ).then_inc(z_ld[t.r], 16)

                    def scatter(t):
                        wait_apart(pool, tab_rdy, t.n + 1, pool_passed)
                        wait_apart(pool, sum_rdy, t.n + 1, pool_passed)
                        for j in range(J):
                            wait_apart(pool, added[j], 16 * t.n, pool_passed)
                            nc.gpsimd.indirect_dma_start(
                                out=agg_dram[j],
                                out_offset=bass.IndirectOffsetOnAxis(ap=tabc[:, t.r, j:j + 1], axis=0),
                                in_=summed[:, t.r, j, :], in_offset=None, compute_op=ALU.add,
                                bounds_check=TR - 1).then_inc(added[j], 16)

                    pool.wait_ge(z_out[0], 16 * (NT // 2 + 1))
                    pool.wait_ge(z_out[1], 16 * (NT // 2))
                    pool.wait_ge(filled, 16 * (J * TR * D // P // ZW + ET * D // ZW))

                    def body(s):
                        if (s + 2).there():
                            gather(s + 2)
                        if (s + -2).there():
                            scatter(s + -2)

                    steps(pool, body, -2)

                @block.scalar
                def _(act):
                    act.wait_ge(pv_ask, 1)
                    nc.scalar.activation(r_d2, r_d2, ACT.Sqrt).then_inc(pv_rdy, 1)
                    act.wait_ge(pv_ask, 2)
                    nc.scalar.activation(r_t, r_t, ACT.Sin).then_inc(pv_rdy, 1)
                    act.wait_ge(sq_ask, 1)
                    nc.scalar.activation(rstd[:], tmp_n[:], ACT.Sqrt).then_inc(sq_rdy, 1)

                    def norm_tile(t):
                        n, b = t.n, t.slot
                        act.wait_ge(xnt_done, n + 1)
                        wait(act, mmz_done, n - 1)
                        nc.scalar.copy(xT[:, b, :], PS[:, b, 0:D]).then_inc(xT_rdy, 1)
                        act.wait_ge(zb_rdy, n + 1)
                        act.dma_start(z_dram[ds(n * P, P), :], rowbuf[:, b, :]).then_inc(z_out[b], 16)

                    run_steps(act, norm_tile, 0, NT, 2, NT)

                    def columns(t):
                        wait(act, msg_rdy, J * (t.n - U) + J)
                        nc.scalar.copy(sel[:, t.r, :], cols[:, ds(t.n, 1), 0:3 * J].rearrange("p a k -> p (a k)")
                                       ).then_inc(col_rdy, 1)
                        nc.scalar.copy(dstc[:, t.r, :], cols[:, ds(t.n, 1), 3 * J:4 * J].rearrange("p a k -> p (a k)")
                                       ).then_inc(dst_rdy, 1)

                    def high(t):
                        act.wait_ge(a_ld[t.r], 16 * (t.q + 1))
                        if isinstance(t.q, int) and t.n == NS - 1:
                            act.wait_ge(a_ld[t.r], 16 * (t.q + 2))
                        wait(act, at_done, t.n - 1)
                        nc.scalar.copy(a_hl[:, t.slot, :, 0:G],
                                       a_in[:, t.r, :].rearrange("p (j g) -> p j g", j=J)).then_inc(hi_rdy, 1)

                    def softplus(t):
                        for c in range(KC):
                            act.wait_ge(cap_rdy, KC * t.n + c + 1)
                            nc.scalar.activation(capped[:, c, :], capped[:, c, :], ACT.Exp).then_inc(exp_done, 1)
                        for c in range(KC):
                            act.wait_ge(exp_done, KC * t.n + c + 1)
                            nc.scalar.activation(capped[:, c, :], capped[:, c, :], ACT.Ln, bias=1.0).then_inc(ln_done, 1)

                    def features(t):
                        act.wait_ge(at_done, t.n + 1)
                        wait(act, pre_done, KC * (t.n - 1))
                        nc.scalar.copy(aT[:, t.slot, :], PS[:, 0, :]).then_inc(aT_rdy, 1)

                    def sums(t):
                        act.wait_ge(sum_done, t.n + 1)
                        for j in range(J):
                            wait(act, added[j], 16 * (t.n - U + 1))
                        nc.scalar.copy(summed[:, t.r].rearrange("p (a j) d -> p a (j d)", a=2),
                                       PS[:, 6:8, :]).then_inc(sum_rdy, 1)

                    act.wait_ge(prep_done, 1)
                    nc.scalar.preload_act_table_set("natural_log_exp_and_others")

                    def body(s):
                        if (s + 3).there():
                            columns(s + 3)
                            high(s + 3)
                        if (s + 1).there():
                            softplus(s + 1)
                        if (s + 2).there():
                            features(s + 2)
                        if (s + -1).there():
                            sums(s + -1)

                    steps(act, body, -3)

                @block.vector
                def _(dve):
                    links = [0]

                    def link(ins):
                        links[0] += 1
                        ins.then_inc(chain, 1)
                        dve.wait_ge(chain, links[0])

                    nc.vector.memset(r_int, PADROW).then_inc(chain, 1)
                    nc.vector.memset(r_dst, 0).then_inc(chain, 1)
                    nc.vector.memset(r_xyz, 2 * CUTOFF).then_inc(chain, 1)
                    links[0] += 3
                    dve.wait_ge(chain, 3)
                    nc.vector.memset(xf_sb[:].rearrange("p t d -> p (t d)")[:, 0:ZW], 0.0).then_inc(zero_rdy, 1)
                    nc.vector.memset(a_hl[:].bitcast(F32), 0.0).then_inc(prow_rdy, 1)
                    nc.vector.memset(w1_hh[:].bitcast(F32), 0.0).then_inc(chain, 1)
                    nc.vector.memset(b2_hl[:].bitcast(F32), 0.0).then_inc(chain, 1)
                    nc.vector.memset(ones_r[:].bitcast(F32), 1.0).then_inc(chain, 1)
                    links[0] += 3

                    dve.wait_ge(e_in, 16 * 3 * (RB + 1))
                    xyz = r_xyz.rearrange("p (s c) -> p s c", c=3)
                    nc.vector.tensor_tensor(r_t, xyz[:, :, 0], xyz[:, :, 0], ALU.mult).then_inc(chain, 1)
                    nc.vector.tensor_tensor(r_d2, xyz[:, :, 1], xyz[:, :, 1], ALU.mult).then_inc(chain, 1)
                    nc.vector.tensor_tensor(r_m, xyz[:, :, 2], xyz[:, :, 2], ALU.mult).then_inc(chain, 1)
                    links[0] += 3
                    dve.wait_ge(chain, links[0])
                    link(nc.vector.tensor_tensor(r_t, r_t, r_d2, ALU.add))
                    nc.vector.tensor_tensor(r_d2, r_t, r_m, ALU.add).then_inc(pv_ask, 1)
                    nc.vector.tensor_copy(r_srcf, r_int).then_inc(chain, 1)
                    nc.vector.tensor_copy(r_dstf, r_dst).then_inc(chain, 1)
                    nc.vector.tensor_scalar(r_hi, r_int, 7, None, ALU.arith_shift_right).then_inc(chain, 1)
                    nc.vector.tensor_scalar(r_lo, r_int, P - 1, None, ALU.bitwise_and).then_inc(chain, 1)
                    links[0] += 4
                    dve.wait_ge(chain, links[0])
                    for k, d in enumerate((r_hi, r_lo)):
                        nc.vector.tensor_copy(r_dig[k], d.rearrange("p (a q j) -> p a j q", a=RB, j=J)).then_inc(dig_rdy, 1)
                    dve.wait_ge(pv_rdy, 1)
                    nc.vector.tensor_scalar(r_m, r_d2, CUTOFF, 0.5, ALU.is_le, ALU.mult).then_inc(chain, 1)
                    nc.vector.tensor_scalar(r_t, r_d2, CUTOFF, -math.pi / CUTOFF, ALU.min, ALU.mult).then_inc(chain, 1)
                    links[0] += 2
                    dve.wait_ge(chain, links[0])
                    nc.vector.tensor_scalar(r_t, r_t, math.pi / 2, None, ALU.add).then_inc(pv_ask, 1)

                    dve.wait_ge(w_in, 16 * 13)
                    with dve.Fori(0, NT) as n:
                        nc.vector.bn_stats(node_row(stats, n), node_row(x_sb, n)).then_inc(st_rdy, 1)
                    dve.wait_ge(st_rdy, NT)
                    norm_bulk(dve, link, 1)

                    dve.wait_ge(pv_rdy, 2)
                    nc.vector.scalar_tensor_tensor(out=r_c, in0=r_t, scalar=1.0, in1=r_m, op0=ALU.add,
                                                   op1=ALU.mult).then_inc(prow_rdy, 1)
                    for k in range(3 * RB * J):
                        what, a, j = (0, 1, 3)[k // (RB * J)], k // J % RB, k % J
                        dve.wait_ge(pt_done, k + 1)
                        nc.vector.tensor_copy(cols[:, a * RH:(a + 1) * RH, what * J + j], PS[:, 4 + k % 2, 0:RH]
                                              ).then_inc(pt_free, 1)
                    dve.wait_ge(pt_free, 3 * RB * J)
                    dve.wait_ge(consts, 8)
                    nc.vector.tensor_scalar(cols[:, :, 2 * J:3 * J], cols[:, :, 0:J], -1.0, dummy[:, 0:1],
                                            ALU.mult, ALU.add).then_inc(prep_done, 1)

                    nc.vector.tensor_copy(ident_r[:], ident[:]).then_inc(chain, 1)
                    nc.vector.tensor_copy(w1_hh[0:G, :], w1_in[0:G, :]).then_inc(chain, 1)
                    nc.vector.tensor_copy(w1_hh[64:64 + G, :], w1_in[64:64 + G, :]).then_inc(chain, 1)
                    links[0] += 3
                    dve.wait_ge(chain, links[0])
                    link(nc.vector.tensor_tensor(w1_lo[:], w1_in[0:G, :], w1_hh[0:G, :].bitcast(F32), ALU.subtract))
                    dve.wait_ge(wprep_mm, 1)
                    for c in range(KC):
                        nc.vector.tensor_copy(rwT[:, c, :], PS[:, 6, c * NX:(c + 1) * NX]).then_inc(chain, 1)
                        links[0] += 1
                    link(nc.vector.tensor_tensor(b2_row[:], b2_row[:], PS[0:1, 7, 0:D], ALU.add))
                    link(nc.vector.tensor_copy(b2_hl[0:1, :], b2_row[:]))
                    link(nc.vector.tensor_tensor(b2_row[:], b2_row[:], b2_hl[0:1, :].bitcast(F32), ALU.subtract))
                    nc.vector.tensor_copy(b2_hl[32:33, :], b2_row[:]).then_inc(wprep, 1)

                    def norm_row(t):
                        wait(dve, xnt_done, t.n - 1)
                        wait(dve, res_rdy, t.n - 1)
                        nc.vector.tensor_scalar(xn[:, t.slot, :], node_row(x_sb, t.n), mean[:, ds(t.n, 1)],
                                                rstd[:, ds(t.n, 1)], ALU.subtract, ALU.mult).then_inc(xn_rdy, 1)

                    def norm_residual(t):
                        dve.wait_ge(xn_rdy, t.n + 1)
                        nc.vector.tensor_tensor(node_row(x_sb, t.n), node_row(x_sb, t.n), xn[:, t.slot, :], ALU.add
                                                ).then_inc(res_rdy, 1)

                    def z_rows(t):
                        dve.wait_ge(mmz_done, t.n + 1)
                        wait(dve, z_out[t.slot], 16 * t.turn)
                        nc.vector.tensor_copy(rowbuf[:, t.slot, :], PS[:, 2 + t.slot, 0:D]).then_inc(zb_rdy, 1)

                    def norm_step(s):
                        if (s + 1).there():
                            norm_row(s + 1)
                        if s.there():
                            norm_residual(s)
                            z_rows(s)

                    run_steps(dve, norm_step, -1, NT, 2, NT)

                    def low(t):
                        dve.wait_ge(hi_rdy, t.n + 1)
                        nc.vector.tensor_tensor(a_hl[:, t.slot, :, 64:64 + G],
                                                a_in[:, t.r, :].rearrange("p (j g) -> p j g", j=J),
                                                a_hl[:, t.slot, :, 0:G].bitcast(F32), ALU.subtract).then_inc(lo_rdy, 1)

                    def cap(t):
                        wait(dve, h_rdy, KC * t.n)
                        for c in range(KC):
                            dve.wait_ge(pre_done, KC * t.n + c + 1)
                            nc.vector.tensor_scalar(capped[:, c, :], PS[:, 1 + c, :], b1_col[:, c:c + 1], CAP,
                                                    ALU.add, ALU.min).then_inc(cap_rdy, 1)

                    def hidden(t):
                        wait(dve, w_done, 2 * (t.n - 1))
                        for c in range(KC):
                            dve.wait_ge(ln_done, KC * t.n + c + 1)
                            nc.vector.scalar_tensor_tensor(out=hT[:, t.slot, c, :], in0=PS[:, 1 + c, :],
                                                           scalar=b1_col[:, c:c + 1], in1=capped[:, c, :],
                                                           op0=ALU.add, op1=ALU.max).then_inc(h_rdy, 1)

                    def equal(t):
                        dve.wait_ge(dg_done, t.n + 1)
                        dve.wait_ge(col_rdy, t.n + 1)
                        wait(dve, sum_done, t.n - U + 1)
                        wait(dve, tabf_rdy, t.n - 1)
                        for j in range(J):
                            nc.vector.scalar_tensor_tensor(out=same[:, t.r, j, :], in0=PS[:, 5, j * P:(j + 1) * P],
                                                           scalar=sel[:, t.r, j:j + 1], in1=upper[:],
                                                           op0=ALU.is_equal, op1=ALU.mult,
                                                           accum_out=later[:, t.slot, j:j + 1]).then_inc(same_rdy, 1)

                    def targets_f(t):
                        dve.wait_ge(same_rdy, J * t.n + J)
                        wait(dve, tab_rdy, t.n - 1)
                        nc.vector.scalar_tensor_tensor(out=tab_f[:, t.slot, :], in0=later[:, t.slot, :], scalar=1.5,
                                                       in1=sel[:, t.r, 2 * J:3 * J], op0=ALU.is_gt, op1=ALU.mult
                                                       ).then_inc(tabf_rdy, 1)

                    def targets(t):
                        dve.wait_ge(tabf_rdy, t.n + 1)
                        for j in range(J):
                            wait(dve, added[j], 16 * (t.n - U + 1))
                        nc.vector.tensor_tensor(tabc[:, t.r, :], tab_f[:, t.slot, :], sel[:, t.r, 0:J], ALU.add
                                                ).then_inc(tab_rdy, 1)

                    def message(t, j):
                        if j % 2 == 0:
                            dve.wait_ge(w_done, 2 * t.n + j // 2 + 1)
                        if j == 0:
                            dve.wait_ge(z_ld[t.r], 16 * J * (t.q + 1))
                            wait(dve, sum_done, t.n - 1)
                        nc.vector.scalar_tensor_tensor(out=msg[:, t.slot, j, :],
                                                       in0=PS[:, 3 + j // 2, j % 2 * D:(j % 2 + 1) * D],
                                                       scalar=sel[:, t.r, J + j:J + j + 1], in1=zg[:, t.r, j, :],
                                                       op0=ALU.mult, op1=ALU.mult).then_inc(msg_rdy, 1)

                    def body(s):
                        if (s + 1).there():
                            cap(s + 1)
                        if s.there():
                            message(s, 0)
                            message(s, 1)
                        if (s + 1).there():
                            hidden(s + 1)
                        if (s + 3).there():
                            low(s + 3)
                        if (s + 1).there():
                            equal(s + 1)
                        if s.there():
                            message(s, 2)
                            message(s, 3)
                        if (s + 1).there():
                            targets_f(s + 1)
                            targets(s + 1)

                    steps(dve, body, -3)

                @block.tensor
                def _(pe):
                    pe.wait_ge(w_in, 16 * 13)
                    pe.wait_ge(consts, 8)
                    for c in range(KC):
                        nc.tensor.transpose(PS[:, 6, c * NX:(c + 1) * NX], rw_in[:, c * P:(c + 1) * P], ident[0:NX, 0:NX])
                    for c in range(KC):
                        last = nc.tensor.matmul(PS[0:1, 7, 0:D], neg_ln2[:], w2_sb[:, c, :], start=(c == 0),
                                                stop=(c == KC - 1))
                    last.then_inc(wprep_mm, 1)
                    pe.wait_ge(prow_rdy, 2)
                    for k in range(3 * RB * J):
                        rows, a, j = (r_srcf, r_c, r_dstf)[k // (RB * J)], k // J % RB, k % J
                        wait(pe, pt_free, k - 1)
                        nc.tensor.transpose(PS[:, 4 + k % 2, 0:RH],
                                            rows.rearrange("p (a q j) -> p a j q", a=RB, j=J)[:, a, j, :],
                                            ident[0:RH, 0:RH]).then_inc(pt_done, 1)

                    def flip(t):
                        pe.wait_ge(xn_rdy, t.n + 1)
                        wait(pe, xT_rdy, t.n - 1)
                        for c in range(KC):
                            last = nc.tensor.transpose(PS[:, t.slot, c * P:(c + 1) * P],
                                                       xn[:, t.slot, c * P:(c + 1) * P], ident[:])
                        last.then_inc(xnt_done, 1)

                    def product(t):
                        pe.wait_ge(xT_rdy, t.n + 1)
                        wait(pe, zb_rdy, t.n - 1)
                        for c in range(KC):
                            last = nc.tensor.matmul(PS[:, 2 + t.slot, 0:D], xT[:, t.slot, c * P:(c + 1) * P],
                                                    lin1_sb[:, c, :], start=(c == 0), stop=(c == KC - 1))
                        last.then_inc(mmz_done, 1)

                    def norm_step(s):
                        if (s + 1).there():
                            flip(s + 1)
                        if s.there():
                            product(s)

                    run_steps(pe, norm_step, -1, NT, 2, NT)
                    pe.wait_ge(zb_rdy, NT)
                    pe.wait_ge(pt_free, 3 * RB * J)

                    def spread(t):
                        pe.wait_ge(dg_ld[t.r], 16 * (t.q + 1))
                        wait(pe, same_rdy, J * t.n)
                        nc.tensor.matmul(PS[:, 5, :], digit_w[:], digits[:, t.r, :], start=True, stop=True
                                         ).then_inc(dg_done, 1)

                    def turn_features(t):
                        pe.wait_ge(lo_rdy, t.n + 1)
                        wait(pe, aT_rdy, t.n)
                        for j in range(J):
                            last = nc.tensor.transpose(PS[:, 0, j * P:(j + 1) * P].bitcast(F32R),
                                                       a_hl[:, t.slot, j, :], ident_r[:])
                        last.then_inc(at_done, 1)

                    def first_layer(t):
                        pe.wait_ge(aT_rdy, t.n + 1)
                        wait(pe, h_rdy, KC * t.n)
                        for c in range(KC):
                            nc.tensor.matmul(PS[:, 1 + c, :], w1_hh[:, c * P:(c + 1) * P], aT[:, t.slot, :],
                                             start=True, stop=False)
                            nc.tensor.matmul(PS[:, 1 + c, :], w1_lo[:, c * P:(c + 1) * P], aT[0:G, t.slot, :],
                                             start=False, stop=True).then_inc(pre_done, 1)

                    def second_layer(t):
                        pe.wait_ge(h_rdy, KC * t.n + KC)
                        for j in range(J):
                            if j % 2 == 0:
                                wait(pe, msg_rdy, J * (t.n - 1) + j + 2)
                            o = PS[:, 3 + j // 2, j % 2 * D:(j % 2 + 1) * D]
                            nc.tensor.matmul(o, ones_r[:], b2_hl[:], start=True, stop=False)
                            for c in range(KC):
                                last = nc.tensor.matmul(o, hT[:, t.slot, c, j * P:(j + 1) * P], w2_sb[:, c, :],
                                                        start=False, stop=(c == KC - 1))
                            if j % 2:
                                last.then_inc(w_done, 1)

                    def combine(t):
                        pe.wait_ge(same_rdy, J * t.n + J)
                        wait(pe, sum_rdy, t.n)
                        for j in range(J):
                            pe.wait_ge(msg_rdy, J * t.n + j + 1)
                            last = nc.tensor.matmul(PS[:, 6 + j // 2, j % 2 * D:(j % 2 + 1) * D], same[:, t.r, j, :],
                                                    msg[:, t.slot, j, :], start=True, stop=True)
                        last.then_inc(sum_done, 1)

                    pe.wait_ge(wprep, 1)

                    def body(s):
                        if (s + 1).there():
                            first_layer(s + 1)
                        if (s + 1).there():
                            spread(s + 1)
                        if s.there():
                            second_layer(s)
                        if (s + 2).there():
                            turn_features(s + 2)
                        if (s + -1).there():
                            combine(s + -1)

                    steps(pe, body, -2)

        ag = sb("ag", [P, 2, J, D])
        agsum = sb("agsum", [P, 2, D])
        capn = sb("capn", [P, 2, D])
        soft = sb("soft", [P, 2, D])
        lg = sb("lg", [P, NT, NX])
        oh = sb("oh", [P, NT, NX])
        oh_bf = sb("oh_bf", [P, NT, NX], BF16)
        best = sb("best", [P, NT])
        rank_w = sb("rank_w", [P, NX])
        valid = sb("valid", [P, 1])
        tot = sb("tot", [P, NX, NT])
        off = sb("off", [P, NX, NT])
        onesv = sb("onesv", [P, NX * NT])
        cnt = sb("cnt", [P, NX])
        pad_i = sb("pad_i", [P, NX], I32)
        padded = sb("padded", [P, NX])
        pend = sb("pend", [P, NX])
        shift = sb("shift", [P, NX])
        place = sb("place", [P, NT])
        tile_no = sb("tile_no", [1, ET])
        behind = sb("behind", [1, ET, NX])
        expert_f = sb("expert_f", [1, ET])
        expert = sb("expert", [1, ET], I32)
        place_c = sb("place_c", [P, 2, 1], I32)
        row_c = sb("row_c", [P, 2, D])
        xe = sb("xe", [P, 2, D])
        w1e = sb("w1e", [P, 2, KC, H])
        b1e = sb("b1e", [H, 2])
        w2e = sb("w2e", [H + 1, 2, D])
        he = sb("he", [H + 1, 2, P])
        yg = sb("yg", [P, 2, D])
        yo = sb("yo", [P, 2, D])

        ag_ld = [sem(f"ag_ld{b}") for b in range(2)]
        ag_sum = sem("ag_sum")
        agt_done = sem("agt_done")
        agT_rdy = sem("agT_rdy")
        lin2_done = sem("lin2_done")
        capn_rdy = sem("capn_rdy")
        expn_done = sem("expn_done")
        lnn_done = sem("lnn_done")
        soft_rdy = sem("soft_rdy")
        x2_rdy = sem("x2_rdy")
        st2_rdy = sem("st2_rdy")
        consts2 = sem("consts2")
        xn2_rdy = sem("xn2_rdy")
        xn2t_done = sem("xn2t_done")
        xf_rdy = sem("xf_rdy")
        xT2_rdy = sem("xT2_rdy")
        lg_done = sem("lg_done")
        lg_rdy = sem("lg_rdy")
        oh_rdy = sem("oh_rdy")
        count_done = sem("count_done")
        placed = sem("placed")
        pc_rdy = sem("pc_rdy")
        row_rdy = sem("row_rdy")
        sorted_in = [sem(f"sorted_in{b}") for b in range(2)]
        ex_rdy = sem("ex_rdy")
        xe_ld = [sem(f"xe_ld{b}") for b in range(2)]
        we_ld = [sem(f"we_ld{b}") for b in range(2)]
        xet_done = sem("xet_done")
        xeT_rdy = sem("xeT_rdy")
        l1_done = sem("l1_done")
        he_rdy = sem("he_rdy")
        l2_done = sem("l2_done")
        ye_rdy = sem("ye_rdy")
        ys_out = [sem(f"ys_out{b}") for b in range(2)]
        pg_rdy = sem("pg_rdy")
        yg_ld = [sem(f"yg_ld{b}") for b in range(2)]
        yo_rdy = sem("yo_rdy")
        o_out = [sem(f"o_out{b}") for b in range(2)]
        he_ones = sem("he_ones")

        with nc.Block() as block:
            @block.sync
            def _(sp):
                def load_sums(t):
                    wait(sp, ag_sum, t.n - 1)
                    for j in range(J):
                        sp.dma_start(ag[:, t.slot, j, :], agg_dram[j][ds(t.n * P, P), :]).then_inc(ag_ld[t.slot], 16)

                run_steps(sp, load_sums, 0, NT, 2, NT)

                sp.wait_ge(ex_rdy, 1)
                sp.wait_ge(sorted_in[0], 16 * (NT // 2 + 1))
                sp.wait_ge(sorted_in[1], 16 * (NT // 2))

                def load_expert(t):
                    b = t.slot
                    wait(sp, xet_done, t.n - 1)
                    sp.dma_start(xe[:, b, :], xs_dram[ds(t.n * P, P), :]).then_inc(xe_ld[b], 16)
                    e = sp.value_load(expert[0:1, ds(t.n, 1)], min_val=0, max_val=NX - 1)
                    wait(sp, l2_done, t.n - 1)
                    sp.dma_start(w1e[:, b], ffn_w1[ds(e, 1)].rearrange("a (c p) h -> p (a c) h", p=P)).then_inc(we_ld[b], 16)
                    sp.dma_start(b1e[:, b:b + 1], ffn_b1[ds(e, 1)].rearrange("a h -> h a")).then_inc(we_ld[b], 16)
                    sp.dma_start(w2e[0:H, b, :], ffn_w2[ds(e, 1)].rearrange("a h d -> (a h) d")).then_inc(we_ld[b], 16)
                    sp.dma_start(w2e[H:H + 1, b, :], ffn_b2[ds(e, 1)]).then_inc(we_ld[b], 16)

                run_steps(sp, load_expert, 0, ET, 2, ET)

                def store(t):
                    sp.wait_ge(yo_rdy, t.n + 1)
                    if isinstance(t.q, int) and t.n == NT - 1:
                        sp.dma_start(out[t.n * P:N, :], yo[0:NLAST, t.slot, :]).then_inc(o_out[t.slot], 16)
                    else:
                        sp.dma_start(out[ds(t.n * P, P), :], yo[:, t.slot, :]).then_inc(o_out[t.slot], 16)

                run_steps(sp, store, 0, NT, 2, NT)
                sp.wait_ge(o_out[0], 16 * (NT // 2 + 1))
                sp.wait_ge(o_out[1], 16 * (NT // 2))

            @block.gpsimd
            def _(pool):
                nc.gpsimd.iota(rank_w[:], pattern=[[-1, NX]], base=NX, channel_multiplier=0,
                               allow_small_or_imprecise_dtypes=True).then_inc(consts2, 1)
                nc.gpsimd.iota(tile_no[:], pattern=[[1, ET]], base=0, channel_multiplier=0,
                               allow_small_or_imprecise_dtypes=True).then_inc(consts2, 1)
                nc.gpsimd.memset(onesv[:], 1.0).then_inc(consts2, 1)
                nc.gpsimd.affine_select(out=valid[:], in_=neg_ln2[:], compare_op=ALU.is_gt, fill=0.0, base=NLAST,
                                        pattern=[[0, 1]], channel_multiplier=-1).then_inc(consts2, 1)

                def sort_rows(t):
                    wait_apart(pool, pc_rdy, t.n + 1, pool_passed)
                    wait_apart(pool, row_rdy, t.n + 1, pool_passed)
                    rows = NLAST if isinstance(t.q, int) and t.n == NT - 1 else P
                    nc.gpsimd.indirect_dma_start(
                        out=xs_dram, out_offset=bass.IndirectOffsetOnAxis(ap=place_c[0:rows, t.slot, :], axis=0),
                        in_=row_c[0:rows, t.slot, :], in_offset=None).then_inc(sorted_in[t.slot], 16)

                run_steps(pool, sort_rows, 0, NT, 2, NT)
                pool.wait_ge(ys_out[0], 16 * (ET // 2))
                pool.wait_ge(ys_out[1], 16 * (ET // 2))

                def fetch(t):
                    wait_apart(pool, pg_rdy, t.n + 1, pool_passed)
                    wait_apart(pool, yo_rdy, t.n - 1, pool_passed)
                    nc.gpsimd.indirect_dma_start(
                        out=yg[:, t.slot, :], out_offset=None, in_=ys_dram,
                        in_offset=bass.IndirectOffsetOnAxis(ap=place_c[:, t.slot, :], axis=0)
                    ).then_inc(yg_ld[t.slot], 16)

                run_steps(pool, fetch, 0, NT, 2, NT)

            @block.scalar
            def _(act):
                nc.scalar.preload_act_table_set("natural_log_exp_and_others")

                def turned(t):
                    act.wait_ge(agt_done, t.n + 1)
                    wait(act, lin2_done, t.n - 1)
                    nc.scalar.copy(xT[:, t.slot, :], PS[:, t.slot, 0:D]).then_inc(agT_rdy, 1)

                def softplus(t):
                    act.wait_ge(capn_rdy, t.n + 1)
                    nc.scalar.activation(capn[:, t.slot, :], capn[:, t.slot, :], ACT.Exp).then_inc(expn_done, 1)
                    act.wait_ge(expn_done, t.n + 1)
                    nc.scalar.activation(capn[:, t.slot, :], capn[:, t.slot, :], ACT.Ln, bias=1.0).then_inc(lnn_done, 1)

                def node_step(s):
                    if (s + 1).there():
                        turned(s + 1)
                    if s.there():
                        softplus(s)

                run_steps(act, node_step, -1, NT, 2, NT)

                act.wait_ge(sq_ask, 2)
                nc.scalar.activation(rstd[:], tmp_n[:], ACT.Sqrt).then_inc(sq_rdy, 1)

                def norm_tile(t):
                    act.wait_ge(xn2_rdy, t.n + 1)
                    nc.scalar.copy(node_row(xf_sb, t.n), xn[:, t.slot, :]).then_inc(xf_rdy, 1)
                    act.wait_ge(xn2t_done, t.n + 1)
                    wait(act, lg_done, t.n - 1)
                    nc.scalar.copy(xT[:, t.slot, :], PS[:, 4 + t.slot, 0:D]).then_inc(xT2_rdy, 1)

                run_steps(act, norm_tile, 0, NT, 2, NT)
                act.wait_ge(xf_rdy, NT)

                def stage_row(t):
                    wait(act, sorted_in[t.slot], 16 * t.turn)
                    nc.scalar.copy(row_c[:, t.slot, :], node_row(xf_sb, t.n)).then_inc(row_rdy, 1)

                run_steps(act, stage_row, 0, NT, 2, NT)

                def rows_turned(t):
                    act.wait_ge(xet_done, t.n + 1)
                    wait(act, l1_done, t.n - 1)
                    nc.scalar.copy(xT[:, t.slot, :], PS[:, t.slot, 0:D]).then_inc(xeT_rdy, 1)

                def hidden(t):
                    act.wait_ge(l1_done, t.n + 1)
                    wait(act, l2_done, t.n - 1)
                    nc.scalar.activation(he[0:H, t.slot, :], PS[0:H, 2 + t.slot, 0:P], ACT.Relu,
                                         bias=b1e[:, t.slot:t.slot + 1]).then_inc(he_rdy, 1)

                def results(t):
                    act.wait_ge(ye_rdy, t.n + 1)
                    act.dma_start(ys_dram[ds(t.n * P, P), :], rowbuf[:, t.slot, :]).then_inc(ys_out[t.slot], 16)

                act.wait_ge(he_ones, 1)

                def expert_step(s):
                    if (s + 1).there():
                        rows_turned(s + 1)
                    if s.there():
                        hidden(s)
                    if (s + -1).there():
                        results(s + -1)

                run_steps(act, expert_step, -1, ET + 1, 2, ET)

            @block.vector
            def _(dve):
                links = [0]

                def link(ins):
                    links[0] += 1
                    ins.then_inc(chain2, 1)
                    dve.wait_ge(chain2, links[0])

                nc.vector.memset(he[:], 1.0).then_inc(he_ones, 1)

                def sum_tables(t):
                    dve.wait_ge(ag_ld[t.slot], 16 * J * (t.turn + 1))
                    wait(dve, agt_done, t.n - 1)
                    nc.vector.tensor_reduce(agsum[:, t.slot, :], ag[:, t.slot].rearrange("p j d -> p d j"), AX.X,
                                            ALU.add).then_inc(ag_sum, 1)

                def cap(t):
                    dve.wait_ge(lin2_done, t.n + 1)
                    wait(dve, soft_rdy, t.n - 1)
                    nc.vector.tensor_scalar(capn[:, t.slot, :], PS[:, 2 + t.slot, 0:D], CAP, None, ALU.min
                                            ).then_inc(capn_rdy, 1)

                def soften(t):
                    dve.wait_ge(lnn_done, t.n + 1)
                    wait(dve, x2_rdy, t.n - 1)
                    nc.vector.tensor_tensor(soft[:, t.slot, :], PS[:, 2 + t.slot, 0:D], capn[:, t.slot, :], ALU.max
                                            ).then_inc(soft_rdy, 1)

                def residual(t):
                    dve.wait_ge(soft_rdy, t.n + 1)
                    nc.vector.scalar_tensor_tensor(out=node_row(x_sb, t.n), in0=soft[:, t.slot, :], scalar=-LN2,
                                                   in1=node_row(x_sb, t.n), op0=ALU.add, op1=ALU.add).then_inc(x2_rdy, 1)

                def statistics(t):
                    dve.wait_ge(x2_rdy, t.n + 1)
                    nc.vector.bn_stats(node_row(stats, t.n), node_row(x_sb, t.n)).then_inc(st2_rdy, 1)

                def node_step(s):
                    if (s + -1).there():
                        soften(s + -1)
                    if (s + 1).there():
                        sum_tables(s + 1)
                    if (s + -1).there():
                        residual(s + -1)
                    if s.there():
                        cap(s)
                    if (s + -1).there():
                        statistics(s + -1)

                run_steps(dve, node_step, -1, NT + 1, 2, NT)
                dve.wait_ge(st2_rdy, NT)
                norm_bulk(dve, link, 2)

                def norm_row(t):
                    wait(dve, xn2t_done, t.n - 1)
                    wait(dve, xf_rdy, t.n - 1)
                    nc.vector.tensor_scalar(xn[:, t.slot, :], node_row(x_sb, t.n), mean[:, ds(t.n, 1)],
                                            rstd[:, ds(t.n, 1)], ALU.subtract, ALU.mult).then_inc(xn2_rdy, 1)

                def logits(t):
                    dve.wait_ge(lg_done, t.n + 1)
                    nc.vector.tensor_copy(node_row(lg, t.n), PS[:, 6 + t.slot, 0:NX]).then_inc(lg_rdy, 1)

                def norm_step(s):
                    if (s + 1).there():
                        norm_row(s + 1)
                    if s.there():
                        logits(s)

                run_steps(dve, norm_step, -1, NT, 2, NT)
                dve.wait_ge(lg_rdy, NT)
                dve.wait_ge(consts2, 4)

                def over_experts(a):
                    return a.unsqueeze(2).to_broadcast([P, NT, NX])

                def over_tiles(a):
                    return a.unsqueeze(1).to_broadcast([P, NT, NX])

                link(nc.vector.tensor_reduce(best[:], lg[:], AX.X, ALU.max))
                link(nc.vector.tensor_tensor(oh[:], lg[:], over_experts(best[:]), ALU.is_ge))
                link(nc.vector.tensor_tensor(oh[:], oh[:], over_tiles(rank_w[:]), ALU.mult))
                link(nc.vector.tensor_reduce(best[:], oh[:], AX.X, ALU.max))
                link(nc.vector.tensor_tensor(oh[:], over_tiles(rank_w[:]), over_experts(best[:]), ALU.is_equal))
                link(nc.vector.tensor_scalar(valid[:], valid[:], 0.0, None, ALU.is_lt))
                link(nc.vector.tensor_scalar(oh[:, NT - 1, :], oh[:, NT - 1, :], valid[:, 0:1], None, ALU.mult))
                nc.vector.tensor_copy(oh_bf[:], oh[:]).then_inc(oh_rdy, 1)

                dve.wait_ge(count_done, 1)
                TQ = 512 // NX
                for k in range(4):
                    t0, t1 = k * TQ, min(NT, (k + 1) * TQ)
                    if t0 < NT:
                        nc.vector.tensor_copy(tot[:, :, t0:t1], PS[:, 4 + k, 0:(t1 - t0) * NX].rearrange(
                            "p (t e) -> p e t", e=NX)).then_inc(chain2, 1)
                        links[0] += 1
                dve.wait_ge(chain2, links[0])
                flat_tot, flat_off = tot[:].rearrange("p e t -> p (e t)"), off[:].rearrange("p e t -> p (e t)")
                link(nc.vector.tensor_tensor_scan(flat_off, onesv[:], flat_tot, 0.0, ALU.mult, ALU.add))
                link(nc.vector.tensor_reduce(cnt[:], tot[:], AX.X, ALU.add))
                link(nc.vector.tensor_scalar(pad_i[:], cnt[:], float(P - 1), None, ALU.add))
                link(nc.vector.tensor_scalar(pad_i[:], pad_i[:], 7, 7, ALU.arith_shift_right, ALU.logical_shift_left))
                link(nc.vector.tensor_copy(padded[:], pad_i[:]))
                link(nc.vector.tensor_tensor_scan(pend[:], onesv[:, 0:NX], padded[:], 0.0, ALU.mult, ALU.add))
                link(nc.vector.tensor_tensor(shift[:], pend[:], padded[:], ALU.subtract))
                link(nc.vector.tensor_tensor(shift[:], shift[:], off[:, :, NT - 1], ALU.subtract))
                link(nc.vector.tensor_tensor(shift[:], shift[:], cnt[:], ALU.add))
                link(nc.vector.tensor_tensor(flat_off, flat_off, flat_tot, ALU.subtract))
                link(nc.vector.tensor_tensor(off[:], off[:], shift[:].unsqueeze(2).to_broadcast([P, NX, NT]), ALU.add))
                for k in range(4):
                    t0, t1 = k * TQ, min(NT, (k + 1) * TQ)
                    if t0 < NT:
                        nc.vector.tensor_tensor(lg[:, t0:t1, :], off[:, :, t0:t1].rearrange("p e t -> p t e"),
                                                PS[:, k, 0:(t1 - t0) * NX].rearrange("p (t e) -> p t e", e=NX), ALU.add
                                                ).then_inc(chain2, 1)
                        links[0] += 1
                dve.wait_ge(chain2, links[0])
                link(nc.vector.tensor_tensor(lg[:], lg[:], oh[:], ALU.mult))
                nc.vector.tensor_reduce(place[:], lg[:], AX.X, ALU.add).then_inc(placed, 1)
                link(nc.vector.tensor_scalar(pend[:], pend[:], 1.0 / P, None, ALU.mult))
                link(nc.vector.tensor_tensor(behind[:], tile_no[:].unsqueeze(2).to_broadcast([1, ET, NX]),
                                             pend[0:1, :].unsqueeze(1).to_broadcast([1, ET, NX]), ALU.is_ge))
                link(nc.vector.tensor_reduce(expert_f[:], behind[:], AX.X, ALU.add))
                nc.vector.tensor_scalar(expert[:], expert_f[:], float(NX - 1), None, ALU.min).then_inc(ex_rdy, 1)
                dve.wait_ge(placed, 1)

                def stage_place(t):
                    wait(dve, sorted_in[t.slot], 16 * t.turn)
                    nc.vector.tensor_copy(place_c[:, t.slot, :], place[:, ds(t.n, 1)]).then_inc(pc_rdy, 1)

                run_steps(dve, stage_place, 0, NT, 2, NT)

                def results(t):
                    dve.wait_ge(l2_done, t.n + 1)
                    wait(dve, ys_out[t.slot], 16 * t.turn)
                    nc.vector.tensor_scalar(rowbuf[:, t.slot, :], PS[:, 4 + t.slot, 0:D], 0.0, None, ALU.max
                                            ).then_inc(ye_rdy, 1)

                run_steps(dve, results, 0, ET, 2, ET)
                dve.wait_ge(sorted_in[0], 16 * (NT // 2 + 1))
                dve.wait_ge(sorted_in[1], 16 * (NT // 2))

                def stage_fetch(t):
                    wait(dve, yg_ld[t.slot], 16 * t.turn)
                    nc.vector.tensor_copy(place_c[:, t.slot, :], place[:, ds(t.n, 1)]).then_inc(pg_rdy, 1)

                def finish(t):
                    dve.wait_ge(yg_ld[t.slot], 16 * (t.turn + 1))
                    wait(dve, o_out[t.slot], 16 * t.turn)
                    nc.vector.tensor_tensor(yo[:, t.slot, :], node_row(x_sb, t.n), yg[:, t.slot, :], ALU.add
                                            ).then_inc(yo_rdy, 1)

                def out_step(s):
                    if (s + 1).there():
                        stage_fetch(s + 1)
                    if s.there():
                        finish(s)

                run_steps(dve, out_step, -1, NT, 2, NT)

            @block.tensor
            def _(pe):
                def turn_rows(source, ready, done, copied, bank):
                    def flip(t):
                        pe.wait_ge(ready, t.n + 1)
                        wait(pe, copied, t.n - 1)
                        for c in range(KC):
                            last = nc.tensor.transpose(PS[:, bank + t.slot, c * P:(c + 1) * P],
                                                       source[:, t.slot, c * P:(c + 1) * P], ident[:])
                        last.then_inc(done, 1)
                    return flip

                flip_sums = turn_rows(agsum, ag_sum, agt_done, agT_rdy, 0)

                def lin2(t):
                    pe.wait_ge(agT_rdy, t.n + 1)
                    wait(pe, soft_rdy, t.n - 1)
                    nc.tensor.matmul(PS[:, 2 + t.slot, 0:D], ones_row[:], lin2b_row[:], start=True, stop=False)
                    for c in range(KC):
                        last = nc.tensor.matmul(PS[:, 2 + t.slot, 0:D], xT[:, t.slot, c * P:(c + 1) * P],
                                                lin2_sb[:, c, :], start=False, stop=(c == KC - 1))
                    last.then_inc(lin2_done, 1)

                def node_step(s):
                    if (s + 1).there():
                        flip_sums(s + 1)
                    if s.there():
                        lin2(s)

                run_steps(pe, node_step, -1, NT, 2, NT)

                flip_rows = turn_rows(xn, xn2_rdy, xn2t_done, xT2_rdy, 4)

                def router(t):
                    pe.wait_ge(xT2_rdy, t.n + 1)
                    wait(pe, lg_rdy, t.n - 1)
                    nc.tensor.matmul(PS[:, 6 + t.slot, 0:NX], ones_row[:], rb_row[:], start=True, stop=False)
                    for c in range(KC):
                        last = nc.tensor.matmul(PS[:, 6 + t.slot, 0:NX], xT[:, t.slot, c * P:(c + 1) * P],
                                                rwT[:, c, :], start=False, stop=(c == KC - 1))
                    last.then_inc(lg_done, 1)

                def norm_step(s):
                    if (s + 1).there():
                        flip_rows(s + 1)
                    if s.there():
                        router(s)

                run_steps(pe, norm_step, -1, NT, 2, NT)

                pe.wait_ge(oh_rdy, 1)
                TQ = 512 // NX
                for half, weights in ((0, upper_bf), (4, ones_bf)):
                    for k in range(4):
                        t0, t1 = k * TQ, min(NT, (k + 1) * TQ)
                        if t0 < NT:
                            last = nc.tensor.matmul(PS[:, half + k, 0:(t1 - t0) * NX], weights[:],
                                                    oh_bf[:, t0:t1, :].rearrange("p t e -> p (t e)"), start=True, stop=True)
                last.then_inc(count_done, 1)

                def flip_expert(t):
                    pe.wait_ge(xe_ld[t.slot], 16 * (t.turn + 1))
                    wait(pe, xeT_rdy, t.n - 1)
                    for c in range(KC):
                        last = nc.tensor.transpose(PS[:, t.slot, c * P:(c + 1) * P], xe[:, t.slot, c * P:(c + 1) * P],
                                                   ident[:])
                    last.then_inc(xet_done, 1)

                def layer1(t):
                    pe.wait_ge(we_ld[t.slot], 16 * 4 * (t.turn + 1))
                    pe.wait_ge(xeT_rdy, t.n + 1)
                    wait(pe, he_rdy, t.n - 1)
                    for c in range(KC):
                        last = nc.tensor.matmul(PS[0:H, 2 + t.slot, 0:P], w1e[:, t.slot, c, :],
                                                xT[:, t.slot, c * P:(c + 1) * P], start=(c == 0), stop=(c == KC - 1))
                    last.then_inc(l1_done, 1)

                def layer2(t):
                    pe.wait_ge(he_rdy, t.n + 1)
                    wait(pe, ye_rdy, t.n - 1)
                    nc.tensor.matmul(PS[:, 4 + t.slot, 0:D], he[:, t.slot, :], w2e[:, t.slot, :], start=True, stop=True
                                     ).then_inc(l2_done, 1)

                def expert_step(s):
                    if (s + 1).there():
                        flip_expert(s + 1)
                    if s.there():
                        layer1(s)
                    if (s + -1).there():
                        layer2(s + -1)

                run_steps(pe, expert_step, -1, ET + 1, 2, ET)


_INS = ["x", "src", "dst", "edge_attr_3", "edge_attr_50", "L0_gnn_mlp_w1", "L0_gnn_mlp_b1", "L0_gnn_mlp_w2",
        "L0_gnn_mlp_b2", "L0_gnn_lin1_w", "L0_gnn_lin2_w", "L0_gnn_lin2_b", "L0_ffn_router_w", "L0_ffn_router_b",
        "L0_ffn_W1", "L0_ffn_b1", "L0_ffn_W2", "L0_ffn_b2"]


def kernel(**inputs):
    import numpy as _np
    import concourse.bacc as _bacc
    from concourse import mybir as _mybir
    from concourse.bass_utils import run_bass_kernel_spmd as _run

    nc = _bacc.Bacc("TRN2", target_bir_lowering=False, num_devices=1)
    arrays, args = {}, []
    for name in _INS:
        a = _np.ascontiguousarray(inputs[name])
        arrays[f"in_{name}"] = a
        args.append(nc.dram_tensor(f"in_{name}", a.shape, _mybir.dt.from_np(a.dtype), kind="ExternalInput").ap())
    shape = inputs["x"].shape
    result = nc.dram_tensor("out_0", shape, _mybir.dt.float32, kind="ExternalOutput").ap()
    gnn_moe(nc, *args, result)
    r = _run(nc, [arrays], core_ids=[0])
    return r.results[0]["out_0"]
```

```python
import math
from contextlib import ExitStack

import concourse.bass as bass
import concourse.mybir as mybir

P = 128


class Step:
    def __init__(self, q, r, u, count):
        self.q, self.r, self.u, self.count = q, r, u, count

    def __add__(self, d):
        return Step(self.q + (self.r + d) // self.u, (self.r + d) % self.u, self.u, self.count)

    @property
    def n(self):
        return self.q * self.u + self.r

    @property
    def slot(self):
        return self.r % 2

    @property
    def turn(self):
        return self.q * (self.u // 2) + self.r // 2

    def there(self):
        return not isinstance(self.q, int) or 0 <= self.n < self.count


def run_steps(eng, body, first, end, u, count):
    start = max(1, -(-(end - count) // u))
    turns = (count - max(1, -first)) // u
    for n in range(first, start * u):
        body(Step(n // u, n % u, u, count))
    with eng.Fori(start, turns) as q:
        for r in range(u):
            body(Step(q, r, u, count))
    for n in range(turns * u, end):
        body(Step(n // u, n % u, u, count))


def wait_apart(eng, semaphore, value, passed):
    if not isinstance(value, int) or value > 0:
        eng.wait_ge(semaphore, value)
        eng.sem_inc(passed, 1)


def wait(eng, semaphore, value):
    if not isinstance(value, int) or value > 0:
        eng.wait_ge(semaphore, value)


def gnn_moe(nc, x, src, dst, edge3, edge50, mlp_w1, mlp_b1, mlp_w2, mlp_b2, lin1_w, lin2_w, lin2_b,
            router_w, router_b, ffn_w1, ffn_b1, ffn_w2, ffn_b2, out):
    F32, F32R, BF16, I32 = mybir.dt.float32, mybir.dt.float32r, mybir.dt.bfloat16, mybir.dt.int32
    ALU, ACT, AX = mybir.AluOpType, mybir.ActivationFunctionType, mybir.AxisListType
    ds = bass.ds

    N, D = x.shape
    E, G = edge50.shape
    NX, _, H = ffn_w1.shape
    KC = D // P
    NT = -(-N // P)
    TG = NT // 7
    NLAST = N - (NT - 1) * P
    J = 4
    SE = J * P
    NS = -(-E // SE)
    U = 4
    UE = 8
    LASTE = E - (NS - 1) * SE
    RB = 2
    RH = NS // RB
    FULL = (NS - 1) % RH
    DUMMY = N
    PADROW = N + P
    TR = -(-(PADROW + 1) // P) * P
    ET = NX + (N - NX) // P
    XW = D + 4
    WW = KC * H + D + 1
    XG = NT // TG
    PADDEST = NT * P
    CAP = 40.0
    LN2 = math.log(2.0)
    EPS = 1e-5
    CUTOFF = 2.0
    assert NS == RB * RH and NS % U == 0 and LASTE % J == 0 and NT % 2 == 1 and ET % 2 == 0 and H < P
    assert NT == XG * TG and 2 * H == P

    z_dram = nc.dram_tensor("z_rows", [NT * P, D], F32).ap()
    dig_dram = nc.dram_tensor("src_digits", [2, NS * SE], BF16).ap()
    agg_dram = [nc.dram_tensor(f"agg_table{j}", [TR, D], F32).ap() for j in range(J)]
    xs_dram = nc.dram_tensor("sorted_rows", [ET * P, XW], F32).ap()
    wtab = nc.dram_tensor("expert_weights", [NX, P, WW], F32).ap()
    ZW = 2560
    XZ = ET * XW // 10
    assert (TR * D // P) % ZW == 0 and (ET * XW) % 10 == 0 and XZ <= ZW

    ctx = ExitStack()
    with ctx:
        def sb(name, shape, dt=F32):
            return ctx.enter_context(nc.sbuf_tensor(name, shape, dt))

        def sem(name):
            return ctx.enter_context(nc.semaphore(name))

        x_sb = sb("x_sb", [P, NT, D])
        ident = sb("ident", [P, P])
        ident_r = sb("ident_r", [P, P], F32R)
        upper = sb("upper", [P, P])
        upper_bf = sb("upper_bf", [P, P], BF16)
        ones_bf = sb("ones_bf", [P, P], BF16)
        ones_row = sb("ones_row", [1, P])
        ones_r = sb("ones_r", [33, P], F32R)
        neg_ln2 = sb("neg_ln2", [P, 1])
        half_c = sb("half_c", [P, 1])
        dummy = sb("dummy_rows", [P, 1])
        digit_w = sb("digit_w", [2, P], BF16)
        w1_in = sb("w1_in", [P, D])
        w1_hh = sb("w1_hh", [P, D], F32R)
        w1_lo = sb("w1_lo", [G, D], F32R)
        w1_res = sb("w1_res", [G, D])
        b1_col = sb("b1_col", [P, KC])
        w2_sb = sb("w2_sb", [P, KC, D])
        b2_row = sb("b2_row", [1, D])
        b2_hl = sb("b2_hl", [33, D], F32R)
        lin1_sb = sb("lin1_sb", [P, KC, D])
        lin2_sb = sb("lin2_sb", [P, KC, D])
        lin2b_row = sb("lin2b_row", [1, D])
        lin2b_hl = sb("lin2b_hl", [33, D], F32R)
        rw_in = sb("rw_in", [NX, D])
        rwT = sb("rwT", [P, KC, NX])
        rb_all = sb("rb_all", [P, NX])
        stats = sb("stats", [P, NT, 6])
        mean = sb("mean", [P, NT])
        rstd = sb("rstd", [P, NT])
        tmp_n = sb("tmp_n", [P, NT])
        cols = sb("cols", [P, NS, 4 * J])

        PS = ctx.enter_context(nc.psum_tensor("PS", [P, 8, 512], F32))

        w_in = sem("w_in")
        x_in = [sem(f"x_in{g}") for g in range(XG)]
        staged = sem("staged")
        e_in = sem("e_in")
        zero_rdy = sem("zero_rdy")
        filled = sem("filled")
        consts = sem("consts")
        pool_passed = sem("pool_passed")
        pchain = sem("pchain")
        chain = sem("chain")
        chain2 = sem("chain2")
        st_rdy = sem("st_rdy")
        res_rdy = sem("res_rdy")
        xn_rdy = sem("xn_rdy")
        xnt_done = sem("xnt_done")
        xT_rdy = sem("xT_rdy")
        mmz_done = sem("mmz_done")
        zb_rdy = sem("zb_rdy")
        z_out = [sem(f"z_out{b}") for b in range(4)]
        sq_ask = sem("sq_ask")
        sq_rdy = sem("sq_rdy")
        pv_ask = sem("pv_ask")
        pv_rdy = sem("pv_rdy")
        padded_rdy = sem("padded_rdy")
        prow_rdy = sem("prow_rdy")
        pt_done = sem("pt_done")
        pt_free = sem("pt_free")
        dig_rdy = sem("dig_rdy")
        dig_out = sem("dig_out")
        wprep = sem("wprep")
        wprep_mm = sem("wprep_mm")
        prep_done = sem("prep_done")

        def node_row(a, n):
            return a[:, ds(n, 1), :].rearrange("p a d -> p (a d)")

        def norm_bulk(vec, link, count):
            me, mo = stats[:, :, 1], stats[:, :, 4]
            link(nc.vector.tensor_tensor(mean[:], me, mo, ALU.add))
            link(nc.vector.tensor_tensor(tmp_n[:], me, mo, ALU.subtract))
            link(nc.vector.tensor_scalar(mean[:], mean[:], 0.5, None, ALU.mult))
            link(nc.vector.scalar_tensor_tensor(out=tmp_n[:], in0=tmp_n[:], scalar=0.25, in1=tmp_n[:],
                                                op0=ALU.mult, op1=ALU.mult))
            link(nc.vector.tensor_tensor(rstd[:], stats[:, :, 2], stats[:, :, 5], ALU.add))
            link(nc.vector.scalar_tensor_tensor(out=tmp_n[:], in0=rstd[:], scalar=1.0 / D, in1=tmp_n[:],
                                                op0=ALU.mult, op1=ALU.add))
            nc.vector.tensor_scalar(tmp_n[:], tmp_n[:], EPS, None, ALU.add).then_inc(sq_ask, 1)
            vec.wait_ge(sq_rdy, count)
            link(nc.vector.reciprocal(rstd[:], rstd[:]))

        part1 = ExitStack()
        with part1:
            def sb1(name, shape, dt=F32):
                return part1.enter_context(nc.sbuf_tensor(name, shape, dt))

            xn = sb1("xn", [P, U, D])
            xT = sb1("xT", [P, 2, D])
            rowbuf = sb1("rowbuf", [P, U, D])
            RW = RB * SE
            work = sb1("work", [P, ZW + 5 * RW + U * J * D])
            a_in = sb1("a_in", [P, U, J * G])
            a_hl = sb1("a_hl", [P, 2, J, P], F32R)
            aT = sb1("aT", [P, 2, SE], F32R)
            digits = sb1("digits", [2, U, SE], BF16)
            dstc = sb1("dstc", [P, U, J], I32)
            sel = sb1("sel", [P, U, 3 * J])
            capped = sb1("capped", [P, KC, SE])
            hT = sb1("hT", [P, 2, KC, SE])
            zg = sb1("zg", [P, U, J, D])
            msg = sb1("msg", [P, 2, J, D])
            same = sb1("same", [P, U, J, P])
            later = sb1("later", [P, 2, J])
            tab_f = sb1("tab_f", [P, 2, J])
            tabc = sb1("tabc", [P, U, J], I32)
            summed = work[:, ZW + 5 * RW:].rearrange("p (u j d) -> p u j d", u=U, j=J)

            r_int = zg[0:RH, 0].bitcast(I32).rearrange("p j d -> p (j d)")
            r_dst = zg[0:RH, 1].bitcast(I32).rearrange("p j d -> p (j d)")
            r_srcf = zg[0:RH, 2].rearrange("p j d -> p (j d)")
            r_dstf = zg[0:RH, 3].rearrange("p j d -> p (j d)")
            r_hi = msg[0:RH, 0].bitcast(I32).rearrange("p j d -> p (j d)")
            r_lo = msg[0:RH, 1].bitcast(I32).rearrange("p j d -> p (j d)")
            r_e3 = hT[0:RH].rearrange("p b c s -> p (b c s)")
            r_e3b = summed[0:RH, 0:2].rearrange("p u j d -> p (u j d)")
            assert RW == J * D and 2 * KC * SE == 2 * RW
            spare = work[0:RH, ZW:ZW + 5 * RW]
            r_xyz = spare[:, 0:3 * RW]
            r_dig = [spare[:, (3 + k) * RW:(3 + k) * RW + RW // 2].bitcast(BF16).rearrange(
                "p (a j q) -> p a j q", a=RB, j=J) for k in range(2)]
            r_d2 = r_e3[:, 0:RW]
            r_t = r_e3[:, RW:2 * RW]
            r_c = r_e3b[:, 0:RW]
            r_m = r_e3b[:, RW:2 * RW]

            a_ld = [sem(f"a_ld{b}") for b in range(U)]
            dg_ld = [sem(f"dg_ld{b}") for b in range(U)]
            hi_rdy = sem("hi_rdy")
            lo_rdy = sem("lo_rdy")
            at_done = sem("at_done")
            aT_rdy = sem("aT_rdy")
            dg_done = sem("dg_done")
            col_rdy = sem("col_rdy")
            dst_rdy = sem("dst_rdy")
            pre_done = sem("pre_done")
            cap_rdy = sem("cap_rdy")
            exp_done = sem("exp_done")
            ln_done = sem("ln_done")
            h_rdy = sem("h_rdy")
            w_done = sem("w_done")
            z_ld = [sem(f"z_ld{b}") for b in range(U)]
            msg_rdy = sem("msg_rdy")
            same_rdy = sem("same_rdy")
            tabf_rdy = sem("tabf_rdy")
            tab_rdy = sem("tab_rdy")
            sum_done = sem("sum_done")
            sum_rdy = sem("sum_rdy")
            added = [sem(f"added{j}") for j in range(J)]

            def sup(n):
                return Step(n // U, n % U, U, NS)

            def steps(eng, body, first):
                run_steps(eng, body, first, NS + 2, U, NS)

            with nc.Block() as block:
                @block.sync
                def _(sp):
                    sp.wait_ge(padded_rdy, 3)
                    for a in range(RB):
                        rows = RH if a < RB - 1 else FULL
                        e0, e1 = a * RH * SE, (a * RH + rows) * SE
                        for dest, arr, w in ((r_xyz, edge3.rearrange("e c -> (e c)"), 3), (r_int, src, 1),
                                             (r_dst, dst, 1)):
                            sp.dma_start(dest[0:rows, a * SE * w:(a + 1) * SE * w],
                                         arr[e0 * w:e1 * w].rearrange("(r s) -> r s", s=SE * w)).then_inc(e_in, 16)
                            if rows < RH:
                                sp.dma_start(dest[rows:rows + 1, a * SE * w:(a * SE + LASTE) * w],
                                             arr[e1 * w:E * w].rearrange("(r s) -> r s", r=1)).then_inc(e_in, 16)
                    sp.wait_ge(consts, 1)
                    for g in range(XG):
                        t0, t1 = g * TG, min((g + 1) * TG, NT - 1)
                        sp.dma_start(x_sb[:, t0:t1, :],
                                     x[t0 * P:t1 * P, :].rearrange("(t p) d -> p t d", p=P)).then_inc(x_in[g], 16)
                    sp.dma_start(x_sb[0:NLAST, NT - 1, :], x[(NT - 1) * P:N, :]).then_inc(x_in[XG - 1], 16)
                    for dest, arr in ((lin1_sb[:], lin1_w.rearrange("(c p) n -> p c n", p=P)),
                                      (w2_sb[:], mlp_w2.rearrange("(c p) n -> p c n", p=P)),
                                      (w1_in[0:G, :], mlp_w1), (w1_in[64:64 + G, :], mlp_w1),
                                      (b1_col[:, 0:1], mlp_b1[0:P].rearrange("(p c) -> p c", c=1)),
                                      (b1_col[:, 1:2], mlp_b1[P:2 * P].rearrange("(p c) -> p c", c=1)),
                                      (b2_row[:], mlp_b2.rearrange("(r n) -> r n", r=1)),
                                      (lin2_sb[:], lin2_w.rearrange("(c p) n -> p c n", p=P)),
                                      (lin2b_row[:], lin2_b.rearrange("(r n) -> r n", r=1)),
                                      (rw_in[:], router_w),
                                      (rb_all[:], router_b.rearrange("(r n) -> r n", r=1).to_broadcast([P, NX]))):
                        sp.dma_start(dest, arr).then_inc(w_in, 16)
                    sp.wait_ge(zero_rdy, 1)
                    zeros = work[:, 0:ZW]
                    fills = 0
                    for tab in agg_dram:
                        flat = tab.rearrange("(p k) d -> p (k d)", p=P)
                        for k in range(flat.shape[1] // ZW):
                            fills += 1
                            if fills > 9:
                                sp.wait_ge(xn_rdy, 4 * (fills - 9))
                            sp.dma_start(flat[:, k * ZW:(k + 1) * ZW], zeros).then_inc(filled, 16)
                    sp.wait_ge(dig_rdy, 2)
                    for k in range(2):
                        for a in range(RB):
                            sp.dma_start(dig_dram[k, a * RH * SE:(a + 1) * RH * SE].rearrange("(r s) -> r s", s=SE),
                                         r_dig[k][:, a].rearrange("p j q -> p (j q)")).then_inc(dig_out, 16)
                    sp.wait_ge(dig_out, 16 * 2 * RB)

                    def load(t):
                        wait(sp, hi_rdy, t.n - U + 1)
                        wait(sp, lo_rdy, t.n - U + 1)
                        wait(sp, dg_done, t.n - U + 1)
                        sp.dma_start(digits[:, t.r, :], dig_dram[:, ds(t.n * SE, SE)]).then_inc(dg_ld[t.r], 16)
                        if isinstance(t.q, int) and t.n == NS - 1:
                            k = LASTE // J
                            sp.dma_start(a_in[0:k, t.r, :],
                                         edge50[t.n * SE:E, :].rearrange("(p j) g -> p (j g)", j=J)
                                         ).then_inc(a_ld[t.r], 16)
                            sp.dma_start(a_in[k:P, t.r, :],
                                         edge50[0:(P - k) * J, :].rearrange("(p j) g -> p (j g)", j=J)
                                         ).then_inc(a_ld[t.r], 16)
                        else:
                            sp.dma_start(a_in[:, t.r, :],
                                         edge50[ds(t.n * SE, SE), :].rearrange("(p j) g -> p (j g)", j=J)
                                         ).then_inc(a_ld[t.r], 16)

                    run_steps(sp, load, 0, NS, U, NS)
                    for j in range(J):
                        sp.wait_ge(added[j], 16 * NS)

                @block.gpsimd
                def _(pool):
                    nc.gpsimd.memset(r_xyz, 2 * CUTOFF).then_inc(padded_rdy, 1)
                    nc.gpsimd.memset(x_sb[:, NT - 1, :], 0.0).then_inc(consts, 1)
                    nc.gpsimd.memset(ident[:], 1.0).then_inc(pchain, 1)
                    nc.gpsimd.memset(upper[:], 1.0).then_inc(pchain, 1)
                    nc.gpsimd.memset(ones_bf[:], 1.0).then_inc(pchain, 1)
                    pool.wait_ge(pchain, 3)
                    nc.gpsimd.affine_select(out=ident[:], in_=ident[:], compare_op=ALU.is_equal, fill=0.0, base=0,
                                            pattern=[[-1, P]], channel_multiplier=1).then_inc(consts, 1)
                    nc.gpsimd.affine_select(out=upper[:], in_=upper[:], compare_op=ALU.is_ge, fill=0.0, base=0,
                                            pattern=[[1, P]], channel_multiplier=-1).then_inc(consts, 1)
                    nc.gpsimd.affine_select(out=upper_bf[:], in_=ones_bf[:], compare_op=ALU.is_gt, fill=0.0, base=0,
                                            pattern=[[1, P]], channel_multiplier=-1).then_inc(consts, 1)
                    nc.gpsimd.iota(dummy[:], pattern=[[0, 1]], base=DUMMY, channel_multiplier=1,
                                   allow_small_or_imprecise_dtypes=True).then_inc(consts, 1)
                    nc.gpsimd.memset(ones_row[:], 1.0).then_inc(consts, 1)
                    nc.gpsimd.memset(neg_ln2[:], -LN2).then_inc(consts, 1)
                    nc.gpsimd.memset(half_c[:], 0.5).then_inc(consts, 1)
                    nc.gpsimd.memset(digit_w[:], 1.0).then_inc(pchain, 1)
                    pool.wait_ge(pchain, 4)
                    nc.gpsimd.memset(digit_w[0:1, :], float(P)).then_inc(consts, 1)

                    def gather(t):
                        wait_apart(pool, dst_rdy, t.n + 1, pool_passed)
                        wait_apart(pool, msg_rdy, J * (t.n - U) + J, pool_passed)
                        for j in range(J):
                            nc.gpsimd.indirect_dma_start(
                                out=zg[:, t.r, j, :], out_offset=None, in_=z_dram,
                                in_offset=bass.IndirectOffsetOnAxis(ap=dstc[:, t.r, j:j + 1], axis=0)
                            ).then_inc(z_ld[t.r], 16)

                    def scatter(t):
                        wait_apart(pool, tab_rdy, t.n + 1, pool_passed)
                        wait_apart(pool, sum_rdy, t.n + 1, pool_passed)
                        for j in range(J):
                            wait_apart(pool, added[j], 16 * t.n, pool_passed)
                            nc.gpsimd.indirect_dma_start(
                                out=agg_dram[j],
                                out_offset=bass.IndirectOffsetOnAxis(ap=tabc[:, t.r, j:j + 1], axis=0),
                                in_=summed[:, t.r, j, :], in_offset=None, compute_op=ALU.add,
                                bounds_check=TR - 1).then_inc(added[j], 16)

                    def residual(t):
                        pool.wait_ge(xn_rdy, t.n + 1)
                        nc.gpsimd.tensor_tensor(node_row(x_sb, t.n), node_row(x_sb, t.n), xn[:, t.r, :], ALU.add
                                                ).then_inc(res_rdy, 1)

                    run_steps(pool, residual, 0, NT, U, NT)

                    for b in range(U):
                        pool.wait_ge(z_out[b], 16 * len(range(b, NT, U)))

                    def body(s):
                        if (s + 2).there():
                            gather(s + 2)
                        if (s + -2).there():
                            if isinstance(s.q, int) and s.n == 2:
                                pool.wait_ge(filled, 16 * (J * TR * D // P // ZW))
                            scatter(s + -2)

                    steps(pool, body, -2)

                @block.scalar
                def _(act):
                    act.wait_ge(pv_ask, 1)
                    nc.scalar.activation(r_d2, r_d2, ACT.Sqrt).then_inc(pv_rdy, 1)
                    act.wait_ge(pv_ask, 2)
                    nc.scalar.activation(r_t, r_t, ACT.Sin).then_inc(pv_rdy, 1)
                    act.wait_ge(sq_ask, 1)
                    nc.scalar.activation(rstd[:], tmp_n[:], ACT.Sqrt).then_inc(sq_rdy, 1)

                    def norm_tile(t):
                        act.wait_ge(xnt_done, t.n + 1)
                        wait(act, mmz_done, t.n - 1)
                        nc.scalar.copy(xT[:, t.slot, :], PS[:, t.slot, 0:D]).then_inc(xT_rdy, 1)

                    def store_z(t):
                        act.wait_ge(zb_rdy, t.n + 1)
                        act.dma_start(z_dram[ds(t.n * P, P), :], rowbuf[:, t.r, :]).then_inc(z_out[t.r], 16)

                    def norm_step(s):
                        if (s + 1).there():
                            norm_tile(s + 1)
                        if (s + -1).there():
                            store_z(s + -1)

                    run_steps(act, norm_step, -1, NT + 1, U, NT)

                    def columns(t):
                        wait(act, msg_rdy, J * (t.n - U) + J)
                        nc.scalar.copy(sel[:, t.r, :], cols[:, ds(t.n, 1), 0:3 * J].rearrange("p a k -> p (a k)")
                                       ).then_inc(col_rdy, 1)
                        nc.scalar.copy(dstc[:, t.r, :], cols[:, ds(t.n, 1), 3 * J:4 * J].rearrange("p a k -> p (a k)")
                                       ).then_inc(dst_rdy, 1)

                    def high(t):
                        act.wait_ge(a_ld[t.r], 16 * (t.q + 1))
                        if isinstance(t.q, int) and t.n == NS - 1:
                            act.wait_ge(a_ld[t.r], 16 * (t.q + 2))
                        wait(act, at_done, t.n - 1)
                        nc.scalar.copy(a_hl[:, t.slot, :, 0:G],
                                       a_in[:, t.r, :].rearrange("p (j g) -> p j g", j=J)).then_inc(hi_rdy, 1)

                    def softplus(t):
                        for c in range(KC):
                            act.wait_ge(cap_rdy, KC * t.n + c + 1)
                            nc.scalar.activation(capped[:, c, :], capped[:, c, :], ACT.Exp).then_inc(exp_done, 1)
                        for c in range(KC):
                            act.wait_ge(exp_done, KC * t.n + c + 1)
                            nc.scalar.activation(capped[:, c, :], capped[:, c, :], ACT.Ln, bias=1.0).then_inc(ln_done, 1)

                    def features(t):
                        act.wait_ge(at_done, t.n + 1)
                        wait(act, pre_done, KC * (t.n - 1))
                        nc.scalar.copy(aT[:, t.slot, :], PS[:, 0, :]).then_inc(aT_rdy, 1)

                    def sums(t):
                        act.wait_ge(sum_done, t.n + 1)
                        for j in range(J):
                            wait(act, added[j], 16 * (t.n - U + 1))
                        nc.scalar.copy(summed[:, t.r].rearrange("p (a j) d -> p a (j d)", a=2),
                                       PS[:, 6:8, :]).then_inc(sum_rdy, 1)

                    act.wait_ge(prep_done, 1)
                    nc.scalar.preload_act_table_set("natural_log_exp_and_others")

                    def body(s):
                        if (s + 3).there():
                            columns(s + 3)
                            high(s + 3)
                        if (s + 1).there():
                            softplus(s + 1)
                        if (s + 2).there():
                            features(s + 2)
                        if (s + -1).there():
                            sums(s + -1)

                    steps(act, body, -3)

                @block.vector
                def _(dve):
                    links = [0]

                    def link(ins):
                        links[0] += 1
                        ins.then_inc(chain, 1)
                        dve.wait_ge(chain, links[0])

                    nc.vector.memset(r_int, PADROW).then_inc(padded_rdy, 1)
                    nc.vector.memset(r_dst, 0).then_inc(padded_rdy, 1)
                    nc.vector.memset(work[:, 0:ZW], 0.0).then_inc(zero_rdy, 1)
                    nc.vector.memset(a_hl[:].bitcast(F32), 0.0).then_inc(prow_rdy, 1)
                    nc.vector.memset(w1_hh[:].bitcast(F32), 0.0).then_inc(chain, 1)
                    nc.vector.memset(b2_hl[:].bitcast(F32), 0.0).then_inc(chain, 1)
                    nc.vector.memset(lin2b_hl[:].bitcast(F32), 0.0).then_inc(chain, 1)
                    nc.vector.memset(ones_r[:].bitcast(F32), 1.0).then_inc(chain, 1)
                    links[0] += 4

                    dve.wait_ge(e_in, 16 * 3 * (RB + 1))
                    xyz = r_xyz.rearrange("p (s c) -> p s c", c=3)
                    nc.vector.tensor_tensor(r_t, xyz[:, :, 0], xyz[:, :, 0], ALU.mult).then_inc(chain, 1)
                    nc.vector.tensor_tensor(r_d2, xyz[:, :, 1], xyz[:, :, 1], ALU.mult).then_inc(chain, 1)
                    nc.vector.tensor_tensor(r_m, xyz[:, :, 2], xyz[:, :, 2], ALU.mult).then_inc(chain, 1)
                    links[0] += 3
                    dve.wait_ge(chain, links[0])
                    link(nc.vector.tensor_tensor(r_t, r_t, r_d2, ALU.add))
                    nc.vector.tensor_tensor(r_d2, r_t, r_m, ALU.add).then_inc(pv_ask, 1)
                    nc.vector.tensor_copy(r_srcf, r_int).then_inc(chain, 1)
                    nc.vector.tensor_copy(r_dstf, r_dst).then_inc(chain, 1)
                    nc.vector.tensor_scalar(r_hi, r_int, 7, None, ALU.arith_shift_right).then_inc(chain, 1)
                    nc.vector.tensor_scalar(r_lo, r_int, P - 1, None, ALU.bitwise_and).then_inc(chain, 1)
                    links[0] += 4
                    dve.wait_ge(chain, links[0])
                    for k, d in enumerate((r_hi, r_lo)):
                        nc.vector.tensor_copy(r_dig[k], d.rearrange("p (a q j) -> p a j q", a=RB, j=J)).then_inc(dig_rdy, 1)
                    dve.wait_ge(pv_rdy, 1)
                    nc.vector.tensor_scalar(r_m, r_d2, CUTOFF, 0.5, ALU.is_le, ALU.mult).then_inc(chain, 1)
                    nc.vector.tensor_scalar(r_t, r_d2, CUTOFF, -math.pi / CUTOFF, ALU.min, ALU.mult).then_inc(chain, 1)
                    links[0] += 2
                    dve.wait_ge(chain, links[0])
                    nc.vector.tensor_scalar(r_t, r_t, math.pi / 2, None, ALU.add).then_inc(pv_ask, 1)

                    for g in range(XG):
                        dve.wait_ge(x_in[g], 16 if g < XG - 1 else 32)
                        for n in range(g * TG, (g + 1) * TG):
                            nc.vector.bn_stats(stats[:, n, :], x_sb[:, n, :]).then_inc(st_rdy, 1)
                    dve.wait_ge(st_rdy, NT)
                    norm_bulk(dve, link, 1)

                    dve.wait_ge(pv_rdy, 2)
                    nc.vector.scalar_tensor_tensor(out=r_c, in0=r_t, scalar=1.0, in1=r_m, op0=ALU.add,
                                                   op1=ALU.mult).then_inc(prow_rdy, 1)
                    for k in range(3 * RB * J):
                        what, a, j = (0, 1, 3)[k // (RB * J)], k // J % RB, k % J
                        dve.wait_ge(pt_done, k + 1)
                        nc.vector.tensor_copy(cols[:, a * RH:(a + 1) * RH, what * J + j], PS[:, 4 + k % 2, 0:RH]
                                              ).then_inc(pt_free, 1)
                    dve.wait_ge(pt_free, 3 * RB * J)
                    dve.wait_ge(consts, 9)
                    nc.vector.tensor_scalar(cols[:, :, 2 * J:3 * J], cols[:, :, 0:J], -1.0, dummy[:, 0:1],
                                            ALU.mult, ALU.add).then_inc(prep_done, 1)

                    dve.wait_ge(w_in, 16 * 11)
                    nc.vector.tensor_copy(ident_r[:], ident[:]).then_inc(chain, 1)
                    nc.vector.tensor_copy(w1_hh[0:G, :], w1_in[0:G, :]).then_inc(chain, 1)
                    nc.vector.tensor_copy(w1_hh[64:64 + G, :], w1_in[64:64 + G, :]).then_inc(chain, 1)
                    links[0] += 3
                    dve.wait_ge(chain, links[0])
                    link(nc.vector.tensor_tensor(w1_lo[:], w1_in[0:G, :], w1_hh[0:G, :].bitcast(F32), ALU.subtract))
                    dve.wait_ge(wprep_mm, 1)
                    for c in range(KC):
                        nc.vector.tensor_copy(rwT[:, c, :], PS[:, 6, c * NX:(c + 1) * NX]).then_inc(chain, 1)
                        links[0] += 1
                    link(nc.vector.tensor_tensor(b2_row[:], b2_row[:], PS[0:1, 7, 0:D], ALU.add))
                    for row, hl in ((b2_row, b2_hl), (lin2b_row, lin2b_hl)):
                        link(nc.vector.tensor_copy(hl[0:1, :], row[:]))
                        link(nc.vector.tensor_tensor(row[:], row[:], hl[0:1, :].bitcast(F32), ALU.subtract))
                        nc.vector.tensor_copy(hl[32:33, :], row[:]).then_inc(wprep, 1)

                    def norm_row(t):
                        wait(dve, xnt_done, t.n - U + 1)
                        wait(dve, res_rdy, t.n - U + 1)
                        nc.vector.tensor_scalar(xn[:, t.r, :], node_row(x_sb, t.n), mean[:, ds(t.n, 1)],
                                                rstd[:, ds(t.n, 1)], ALU.subtract, ALU.mult).then_inc(xn_rdy, 1)

                    def z_rows(t):
                        dve.wait_ge(mmz_done, t.n + 1)
                        wait(dve, z_out[t.r], 16 * t.q)
                        nc.vector.tensor_copy(rowbuf[:, t.r, :], PS[:, 2 + t.slot, 0:D]).then_inc(zb_rdy, 1)

                    def norm_step(s):
                        if (s + 3).there():
                            norm_row(s + 3)
                        if s.there():
                            z_rows(s)

                    run_steps(dve, norm_step, -3, NT, U, NT)

                    def low(t):
                        dve.wait_ge(hi_rdy, t.n + 1)
                        nc.vector.tensor_tensor(a_hl[:, t.slot, :, 64:64 + G],
                                                a_in[:, t.r, :].rearrange("p (j g) -> p j g", j=J),
                                                a_hl[:, t.slot, :, 0:G].bitcast(F32), ALU.subtract).then_inc(lo_rdy, 1)

                    def cap(t):
                        wait(dve, h_rdy, KC * t.n)
                        for c in range(KC):
                            dve.wait_ge(pre_done, KC * t.n + c + 1)
                            nc.vector.tensor_scalar(capped[:, c, :], PS[:, 1 + c, :], b1_col[:, c:c + 1], CAP,
                                                    ALU.add, ALU.min).then_inc(cap_rdy, 1)

                    def hidden(t):
                        wait(dve, w_done, 2 * (t.n - 1))
                        for c in range(KC):
                            dve.wait_ge(ln_done, KC * t.n + c + 1)
                            nc.vector.scalar_tensor_tensor(out=hT[:, t.slot, c, :], in0=PS[:, 1 + c, :],
                                                           scalar=b1_col[:, c:c + 1], in1=capped[:, c, :],
                                                           op0=ALU.add, op1=ALU.max).then_inc(h_rdy, 1)

                    def equal(t):
                        dve.wait_ge(dg_done, t.n + 1)
                        dve.wait_ge(col_rdy, t.n + 1)
                        wait(dve, sum_done, t.n - U + 1)
                        wait(dve, tabf_rdy, t.n - 1)
                        for j in range(J):
                            nc.vector.scalar_tensor_tensor(out=same[:, t.r, j, :], in0=PS[:, 5, j * P:(j + 1) * P],
                                                           scalar=sel[:, t.r, j:j + 1], in1=upper[:],
                                                           op0=ALU.is_equal, op1=ALU.mult,
                                                           accum_out=later[:, t.slot, j:j + 1]).then_inc(same_rdy, 1)

                    def targets_f(t):
                        dve.wait_ge(same_rdy, J * t.n + J)
                        wait(dve, tab_rdy, t.n - 1)
                        nc.vector.scalar_tensor_tensor(out=tab_f[:, t.slot, :], in0=later[:, t.slot, :], scalar=1.5,
                                                       in1=sel[:, t.r, 2 * J:3 * J], op0=ALU.is_gt, op1=ALU.mult
                                                       ).then_inc(tabf_rdy, 1)

                    def targets(t):
                        dve.wait_ge(tabf_rdy, t.n + 1)
                        for j in range(J):
                            wait(dve, added[j], 16 * (t.n - U + 1))
                        nc.vector.tensor_tensor(tabc[:, t.r, :], tab_f[:, t.slot, :], sel[:, t.r, 0:J], ALU.add
                                                ).then_inc(tab_rdy, 1)

                    def message(t, j):
                        if j % 2 == 0:
                            dve.wait_ge(w_done, 2 * t.n + j // 2 + 1)
                        if j == 0:
                            dve.wait_ge(z_ld[t.r], 16 * J * (t.q + 1))
                            wait(dve, sum_done, t.n - 1)
                        nc.vector.scalar_tensor_tensor(out=msg[:, t.slot, j, :],
                                                       in0=PS[:, 3 + j // 2, j % 2 * D:(j % 2 + 1) * D],
                                                       scalar=sel[:, t.r, J + j:J + j + 1], in1=zg[:, t.r, j, :],
                                                       op0=ALU.mult, op1=ALU.mult).then_inc(msg_rdy, 1)

                    def body(s):
                        if (s + 1).there():
                            cap(s + 1)
                        if s.there():
                            message(s, 0)
                            message(s, 1)
                        if (s + 1).there():
                            hidden(s + 1)
                        if (s + 3).there():
                            low(s + 3)
                        if (s + 1).there():
                            equal(s + 1)
                        if s.there():
                            message(s, 2)
                            message(s, 3)
                        if (s + 1).there():
                            targets_f(s + 1)
                            targets(s + 1)

                    steps(dve, body, -3)

                @block.tensor
                def _(pe):
                    pe.wait_ge(w_in, 16 * 11)
                    pe.wait_ge(consts, 9)
                    for c in range(KC):
                        nc.tensor.transpose(PS[:, 6, c * NX:(c + 1) * NX], rw_in[:, c * P:(c + 1) * P], ident[0:NX, 0:NX])
                    for c in range(KC):
                        last = nc.tensor.matmul(PS[0:1, 7, 0:D], neg_ln2[:], w2_sb[:, c, :], start=(c == 0),
                                                stop=(c == KC - 1))
                    last.then_inc(wprep_mm, 1)
                    pe.wait_ge(prow_rdy, 2)
                    for k in range(3 * RB * J):
                        rows, a, j = (r_srcf, r_c, r_dstf)[k // (RB * J)], k // J % RB, k % J
                        wait(pe, pt_free, k - 1)
                        nc.tensor.transpose(PS[:, 4 + k % 2, 0:RH],
                                            rows.rearrange("p (a q j) -> p a j q", a=RB, j=J)[:, a, j, :],
                                            ident[0:RH, 0:RH]).then_inc(pt_done, 1)

                    def flip(t):
                        pe.wait_ge(xn_rdy, t.n + 1)
                        wait(pe, xT_rdy, t.n - 1)
                        for c in range(KC):
                            last = nc.tensor.transpose(PS[:, t.slot, c * P:(c + 1) * P],
                                                       xn[:, t.r, c * P:(c + 1) * P], ident[:])
                        last.then_inc(xnt_done, 1)

                    def product(t):
                        pe.wait_ge(xT_rdy, t.n + 1)
                        wait(pe, zb_rdy, t.n - 1)
                        for c in range(KC):
                            last = nc.tensor.matmul(PS[:, 2 + t.slot, 0:D], xT[:, t.slot, c * P:(c + 1) * P],
                                                    lin1_sb[:, c, :], start=(c == 0), stop=(c == KC - 1))
                        last.then_inc(mmz_done, 1)

                    def norm_step(s):
                        if (s + 2).there():
                            flip(s + 2)
                        if s.there():
                            product(s)

                    run_steps(pe, norm_step, -2, NT, U, NT)
                    pe.wait_ge(zb_rdy, NT)
                    pe.wait_ge(pt_free, 3 * RB * J)

                    def spread(t):
                        pe.wait_ge(dg_ld[t.r], 16 * (t.q + 1))
                        wait(pe, same_rdy, J * t.n)
                        nc.tensor.matmul(PS[:, 5, :], digit_w[:], digits[:, t.r, :], start=True, stop=True
                                         ).then_inc(dg_done, 1)

                    def turn_features(t):
                        pe.wait_ge(lo_rdy, t.n + 1)
                        wait(pe, aT_rdy, t.n)
                        for j in range(J):
                            last = nc.tensor.transpose(PS[:, 0, j * P:(j + 1) * P].bitcast(F32R),
                                                       a_hl[:, t.slot, j, :], ident_r[:])
                        last.then_inc(at_done, 1)

                    def first_layer(t):
                        pe.wait_ge(aT_rdy, t.n + 1)
                        wait(pe, h_rdy, KC * t.n)
                        for c in range(KC):
                            nc.tensor.matmul(PS[:, 1 + c, :], w1_hh[:, c * P:(c + 1) * P], aT[:, t.slot, :],
                                             start=True, stop=False)
                            nc.tensor.matmul(PS[:, 1 + c, :], w1_lo[:, c * P:(c + 1) * P], aT[0:G, t.slot, :],
                                             start=False, stop=True).then_inc(pre_done, 1)

                    def second_layer(t):
                        pe.wait_ge(h_rdy, KC * t.n + KC)
                        for j in range(J):
                            if j % 2 == 0:
                                wait(pe, msg_rdy, J * (t.n - 1) + j + 2)
                            o = PS[:, 3 + j // 2, j % 2 * D:(j % 2 + 1) * D]
                            nc.tensor.matmul(o, ones_r[:], b2_hl[:], start=True, stop=False)
                            for c in range(KC):
                                last = nc.tensor.matmul(o, hT[:, t.slot, c, j * P:(j + 1) * P], w2_sb[:, c, :],
                                                        start=False, stop=(c == KC - 1))
                            if j % 2:
                                last.then_inc(w_done, 1)

                    def combine(t):
                        pe.wait_ge(same_rdy, J * t.n + J)
                        wait(pe, sum_rdy, t.n)
                        for j in range(J):
                            pe.wait_ge(msg_rdy, J * t.n + j + 1)
                            last = nc.tensor.matmul(PS[:, 6 + j // 2, j % 2 * D:(j % 2 + 1) * D], same[:, t.r, j, :],
                                                    msg[:, t.slot, j, :], start=True, stop=True)
                        last.then_inc(sum_done, 1)

                    pe.wait_ge(wprep, 2)

                    def body(s):
                        if (s + 1).there():
                            first_layer(s + 1)
                        if (s + 1).there():
                            spread(s + 1)
                        if s.there():
                            second_layer(s)
                        if (s + 2).there():
                            turn_features(s + 2)
                        if (s + -1).there():
                            combine(s + -1)

                    steps(pe, body, -2)

        ag = sb("ag", [P, U, J, D])
        agsum = sb("agsum", [P, U, D])
        expn = sb("expn", [P, U, D])
        soft = sb("soft", [P, U, D])
        aggT = sb("aggT", [P, U, D])
        centred = sb("centred", [P, U, D])
        centT = sb("centT", [P, 2, D])
        neg_mean = sb("neg_mean", [P, U])
        lg = sb("lg", [P, NT, NX])
        oh = sb("oh", [P, NT, NX])
        oh_bf = sb("oh_bf", [P, NT, NX], BF16)
        best = sb("best", [P, NT])
        rank_w = sb("rank_w", [P, NX])
        valid = sb("valid", [P, 1])
        tot = sb("tot", [P, NX, NT])
        off = sb("off", [P, NX, NT])
        onesv = sb("onesv", [P, NX * NT])
        cnt = sb("cnt", [P, NX])
        pad_i = sb("pad_i", [P, NX], I32)
        padded = sb("padded", [P, NX])
        pend = sb("pend", [P, NX])
        shift = sb("shift", [P, NX])
        place = sb("place", [P, NT])
        info = sb("info", [P, NT, XW - D])
        back = sb("back", [P, NT])
        tile_no = sb("tile_no", [1, ET])
        behind = sb("behind", [1, ET, NX])
        expert_f = sb("expert_f", [1, ET])
        expert = sb("expert", [1, ET], I32)
        place_c = sb("place_c", [P, U, 1], I32)
        row_c = sb("row_c", [P, U, XW])
        zeros2 = sb("zeros2", [P, XZ])
        xe = sb("xe", [P, UE, XW])
        xen = sb("xen", [P, U, D])
        dest_c = sb("dest_c", [P, UE, 1], I32)
        we = sb("we", [P, UE, WW])
        he = sb("he", [H + 1, U, P])
        yo = ag[:].rearrange("p u j d -> p (u j) d")[:, 0:UE]

        ag_ld = [sem(f"ag_ld{b}") for b in range(U)]
        ag_sum = sem("ag_sum")
        agt_done = sem("agt_done")
        agT_rdy = sem("agT_rdy")
        lin2_done = sem("lin2_done")
        abs_done = sem("abs_done")
        expn_done = sem("expn_done")
        lnn_done = sem("lnn_done")
        soft_rdy = sem("soft_rdy")
        x2_rdy = sem("x2_rdy")
        st2_rdy = sem("st2_rdy")
        consts2 = sem("consts2")
        mean_rdy = sem("mean_rdy")
        cent_rdy = sem("cent_rdy")
        centt_done = sem("centt_done")
        centT_rdy = sem("centT_rdy")
        lg_done = sem("lg_done")
        lg_rdy = sem("lg_rdy")
        oh_rdy = sem("oh_rdy")
        count_done = sem("count_done")
        placed = sem("placed")
        pc_rdy = sem("pc_rdy")
        row_rdy = sem("row_rdy")
        info_rdy = sem("info_rdy")
        sorted_in = [sem(f"sorted_in{b}") for b in range(U)]
        ex_rdy = sem("ex_rdy")
        zero2_rdy = sem("zero2_rdy")
        xe_ld = [sem(f"xe_ld{b}") for b in range(UE)]
        we_ld = [sem(f"we_ld{b}") for b in range(UE)]
        xen_rdy = sem("xen_rdy")
        xet_done = sem("xet_done")
        xeT_rdy = sem("xeT_rdy")
        dest_rdy = sem("dest_rdy")
        l1_done = sem("l1_done")
        he_rdy = sem("he_rdy")
        l2_done = sem("l2_done")
        yo_rdy = sem("yo_rdy")
        y_out = [sem(f"y_out{b}") for b in range(UE)]
        he_ones = sem("he_ones")

        with nc.Block() as block:
            @block.sync
            def _(sp):
                def load_sums(t):
                    wait(sp, ag_sum, t.n - U + 1)
                    for j in range(J):
                        sp.dma_start(ag[:, t.r, j, :], agg_dram[j][ds(t.n * P, P), :]).then_inc(ag_ld[t.r], 16)

                run_steps(sp, load_sums, 0, NT, U, NT)

                def stage_experts():
                    sp.wait_ge(zero2_rdy, 1)
                    flat = xs_dram.rearrange("(p k) d -> p (k d)", p=P)
                    for k in range(flat.shape[1] // XZ):
                        sp.dma_start(flat[:, k * XZ:(k + 1) * XZ], zeros2[:]).then_inc(staged, 16)
                    for c in range(KC):
                        sp.dma_start(wtab[:, :, c * H:(c + 1) * H], ffn_w1[:, c * P:(c + 1) * P, :]
                                     ).then_inc(staged, 16)
                    for k in range(2):
                        sp.dma_start(wtab[:, k * H:(k + 1) * H, KC * H:KC * H + D], ffn_w2).then_inc(staged, 16)
                        sp.dma_start(wtab[:, k * H:(k + 1) * H, WW - 1], ffn_b1,
                                     allow_slow_non_contiguous=True).then_inc(staged, 16)
                    sp.wait_ge(staged, 16 * (ET * XW // XZ + 6))
                    sp.dma_start(wtab[:, H, KC * H:KC * H + D], ffn_b2).then_inc(staged, 16)

                stage_experts()
                sp.wait_ge(staged, 16 * (ET * XW // XZ + 7))
                sp.wait_ge(ex_rdy, 1)

                def load_expert(t):
                    e = sp.value_load(expert[0:1, ds(t.n, 1)], min_val=0, max_val=NX - 1)
                    wait(sp, l2_done, t.n - UE + 1)
                    sp.dma_start(we[:, t.r, :], wtab[ds(e, 1)].rearrange("a p w -> p (a w)")).then_inc(we_ld[t.r], 16)

                run_steps(sp, load_expert, 0, ET, UE, ET)

                for b in range(UE):
                    sp.wait_ge(y_out[b], 16 * len(range(b, ET, UE)))

            @block.gpsimd
            def _(pool):
                nc.gpsimd.memset(zeros2[:], 0.0).then_inc(zero2_rdy, 1)
                nc.gpsimd.iota(rank_w[:], pattern=[[-1, NX]], base=NX, channel_multiplier=0,
                               allow_small_or_imprecise_dtypes=True).then_inc(consts2, 1)
                nc.gpsimd.iota(tile_no[:], pattern=[[1, ET]], base=0, channel_multiplier=0,
                               allow_small_or_imprecise_dtypes=True).then_inc(consts2, 1)
                nc.gpsimd.iota(back[:], pattern=[[P, NT]], base=-PADDEST, channel_multiplier=1,
                               allow_small_or_imprecise_dtypes=True).then_inc(consts2, 1)
                nc.gpsimd.memset(onesv[:], 1.0).then_inc(consts2, 1)
                nc.gpsimd.affine_select(out=valid[:], in_=neg_ln2[:], compare_op=ALU.is_gt, fill=0.0, base=NLAST,
                                        pattern=[[0, 1]], channel_multiplier=-1).then_inc(consts2, 1)

                def residual(t):
                    pool.wait_ge(soft_rdy, t.n + 1)
                    nc.gpsimd.tensor_tensor(node_row(x_sb, t.n), node_row(x_sb, t.n), soft[:, t.r, :], ALU.add
                                            ).then_inc(x2_rdy, 1)

                run_steps(pool, residual, 0, NT, U, NT)

                def sort_rows(t):
                    wait_apart(pool, pc_rdy, t.n + 1, pool_passed)
                    wait_apart(pool, info_rdy, t.n + 1, pool_passed)
                    wait_apart(pool, row_rdy, t.n + 1, pool_passed)
                    rows = NLAST if isinstance(t.q, int) and t.n == NT - 1 else P
                    nc.gpsimd.indirect_dma_start(
                        out=xs_dram, out_offset=bass.IndirectOffsetOnAxis(ap=place_c[0:rows, t.r, :], axis=0),
                        in_=row_c[0:rows, t.r, :], in_offset=None).then_inc(sorted_in[t.r], 16)

                pool.wait_ge(staged, 16 * (ET * XW // XZ + 7))
                run_steps(pool, sort_rows, 0, NT, U, NT)

                def deliver(t):
                    wait_apart(pool, dest_rdy, t.n + 1, pool_passed)
                    wait_apart(pool, yo_rdy, t.n + 1, pool_passed)
                    nc.gpsimd.indirect_dma_start(
                        out=out, out_offset=bass.IndirectOffsetOnAxis(ap=dest_c[:, t.r, :], axis=0),
                        in_=yo[:, t.r, :], in_offset=None, bounds_check=N - 1, oob_is_err=False
                    ).then_inc(y_out[t.r], 16)

                run_steps(pool, deliver, 0, ET, UE, ET)

            @block.scalar
            def _(act):
                nc.scalar.preload_act_table_set("natural_log_exp_and_others")

                def turned(t):
                    act.wait_ge(agt_done, t.n + 1)
                    wait(act, lin2_done, t.n - U + 1)
                    nc.scalar.copy(aggT[:, t.r, :], PS[:, t.slot, 0:D]).then_inc(agT_rdy, 1)

                def softplus(t):
                    act.wait_ge(lin2_done, t.n + 1)
                    wait(act, soft_rdy, t.n - U + 1)
                    nc.scalar.activation(expn[:, t.r, :], PS[:, 2 + t.r, 0:D], ACT.Abs).then_inc(abs_done, 1)
                    act.wait_ge(abs_done, t.n + 1)
                    nc.scalar.activation(expn[:, t.r, :], expn[:, t.r, :], ACT.Exp, scale=-1.0).then_inc(expn_done, 1)
                    act.wait_ge(expn_done, t.n + 1)
                    nc.scalar.activation(expn[:, t.r, :], expn[:, t.r, :], ACT.Ln, bias=half_c[:],
                                         scale=0.5).then_inc(lnn_done, 1)

                def centre(t):
                    act.wait_ge(mean_rdy, t.n + 1)
                    act.wait_ge(x2_rdy, t.n + 1)
                    wait(act, centt_done, t.n - U + 1)
                    nc.scalar.activation(centred[:, t.r, :], node_row(x_sb, t.n), ACT.Identity,
                                         bias=neg_mean[:, t.r:t.r + 1]).then_inc(cent_rdy, 1)

                def centre_turned(t):
                    act.wait_ge(centt_done, t.n + 1)
                    wait(act, lg_done, t.n - 1)
                    nc.scalar.copy(centT[:, t.slot, :], PS[:, 6, 0:D]).then_inc(centT_rdy, 1)

                def node_step(s):
                    if (s + 1).there():
                        turned(s + 1)
                    if s.there():
                        softplus(s)
                    if (s + -5).there():
                        centre_turned(s + -5)
                    if (s + -4).there():
                        centre(s + -4)

                run_steps(act, node_step, -1, NT + 5, U, NT)

                act.wait_ge(sq_ask, 2)
                nc.scalar.activation(rstd[:], tmp_n[:], ACT.Sqrt).then_inc(sq_rdy, 1)

                def stage_row(t):
                    wait(act, sorted_in[t.r], 16 * t.q)
                    nc.scalar.copy(row_c[:, t.r, 0:D], node_row(x_sb, t.n)).then_inc(row_rdy, 1)

                run_steps(act, stage_row, 0, NT, U, NT)

                def rows_turned(t):
                    act.wait_ge(xet_done, t.n + 1)
                    wait(act, l1_done, t.n - U + 1)
                    nc.scalar.copy(aggT[:, t.r % U, :], PS[:, t.slot, 0:D]).then_inc(xeT_rdy, 1)

                def hidden(t):
                    act.wait_ge(l1_done, t.n + 1)
                    wait(act, l2_done, t.n - U + 1)
                    nc.scalar.activation(he[0:H, t.r % U, :], PS[0:H, 2 + t.slot, 0:P], ACT.Relu,
                                         bias=we[0:H, t.r, WW - 1:WW]).then_inc(he_rdy, 1)

                def load_rows(t):
                    wait(act, yo_rdy, t.n - UE + 1)
                    act.dma_start(xe[:, t.r, :], xs_dram[ds(t.n * P, P), :]).then_inc(xe_ld[t.r], 16)

                act.wait_ge(he_ones, 1)
                for b in range(U):
                    act.wait_ge(sorted_in[b], 16 * len(range(b, NT, U)))

                def expert_step(s):
                    if (s + 5).there():
                        load_rows(s + 5)
                    if (s + 1).there():
                        rows_turned(s + 1)
                    if s.there():
                        hidden(s)

                run_steps(act, expert_step, -5, ET, UE, ET)

            @block.vector
            def _(dve):
                links = [0]

                def link(ins):
                    links[0] += 1
                    ins.then_inc(chain2, 1)
                    dve.wait_ge(chain2, links[0])

                nc.vector.memset(he[:], 1.0).then_inc(he_ones, 1)

                def sum_tables(t):
                    dve.wait_ge(ag_ld[t.r], 16 * J * (t.q + 1))
                    wait(dve, agt_done, t.n - U + 1)
                    nc.vector.tensor_reduce(agsum[:, t.r, :], ag[:, t.r].rearrange("p j d -> p d j"), AX.X,
                                            ALU.add).then_inc(ag_sum, 1)

                def soften(t):
                    dve.wait_ge(lnn_done, t.n + 1)
                    wait(dve, x2_rdy, t.n - U + 1)
                    nc.vector.scalar_tensor_tensor(out=soft[:, t.r, :], in0=PS[:, 2 + t.r, 0:D], scalar=0.0,
                                                   in1=expn[:, t.r, :], op0=ALU.max, op1=ALU.add).then_inc(soft_rdy, 1)

                def statistics(t):
                    dve.wait_ge(x2_rdy, t.n + 1)
                    nc.vector.bn_stats(node_row(stats, t.n), node_row(x_sb, t.n)).then_inc(st2_rdy, 1)

                def mean_of(t):
                    dve.wait_ge(st2_rdy, t.n + 1)
                    wait(dve, cent_rdy, t.n - U + 1)
                    even = stats[:, ds(t.n, 1), 1:2].rearrange("p a d -> p (a d)")
                    odd = stats[:, ds(t.n, 1), 4:5].rearrange("p a d -> p (a d)")
                    nc.vector.tensor_scalar(neg_mean[:, t.r:t.r + 1], even, odd, -0.5, ALU.add, ALU.mult
                                            ).then_inc(mean_rdy, 1)

                def logits(t):
                    dve.wait_ge(lg_done, t.n + 1)
                    nc.vector.tensor_copy(node_row(lg, t.n), PS[:, 7, 0:NX]).then_inc(lg_rdy, 1)

                def node_step(s):
                    if (s + -7).there():
                        logits(s + -7)
                    if (s + -1).there():
                        soften(s + -1)
                    if (s + -3).there():
                        statistics(s + -3)
                    if (s + 2).there():
                        sum_tables(s + 2)
                    if (s + -3).there():
                        mean_of(s + -3)

                run_steps(dve, node_step, -2, NT + 7, U, NT)
                norm_bulk(dve, link, 2)

                dve.wait_ge(lg_rdy, NT)
                dve.wait_ge(consts2, 5)

                def over_experts(a):
                    return a.unsqueeze(2).to_broadcast([P, NT, NX])

                def over_tiles(a):
                    return a.unsqueeze(1).to_broadcast([P, NT, NX])

                link(nc.vector.tensor_tensor(lg[:], lg[:], over_experts(rstd[:]), ALU.mult))
                link(nc.vector.tensor_tensor(lg[:], lg[:], over_tiles(rb_all[:]), ALU.add))
                link(nc.vector.tensor_reduce(best[:], lg[:], AX.X, ALU.max))
                link(nc.vector.tensor_tensor(oh[:], lg[:], over_experts(best[:]), ALU.is_ge))
                link(nc.vector.tensor_tensor(oh[:], oh[:], over_tiles(rank_w[:]), ALU.mult))
                link(nc.vector.tensor_reduce(best[:], oh[:], AX.X, ALU.max))
                link(nc.vector.tensor_tensor(oh[:], over_tiles(rank_w[:]), over_experts(best[:]), ALU.is_equal))
                link(nc.vector.tensor_scalar(valid[:], valid[:], 0.0, None, ALU.is_lt))
                link(nc.vector.tensor_scalar(oh[:, NT - 1, :], oh[:, NT - 1, :], valid[:, 0:1], None, ALU.mult))
                nc.vector.tensor_copy(oh_bf[:], oh[:]).then_inc(oh_rdy, 1)

                dve.wait_ge(count_done, 1)
                TQ = 512 // NX
                for k in range(4):
                    t0, t1 = k * TQ, min(NT, (k + 1) * TQ)
                    if t0 < NT:
                        nc.vector.tensor_copy(tot[:, :, t0:t1], PS[:, 4 + k, 0:(t1 - t0) * NX].rearrange(
                            "p (t e) -> p e t", e=NX)).then_inc(chain2, 1)
                        links[0] += 1
                dve.wait_ge(chain2, links[0])
                flat_tot, flat_off = tot[:].rearrange("p e t -> p (e t)"), off[:].rearrange("p e t -> p (e t)")
                link(nc.vector.tensor_tensor_scan(flat_off, onesv[:], flat_tot, 0.0, ALU.mult, ALU.add))
                link(nc.vector.tensor_reduce(cnt[:], tot[:], AX.X, ALU.add))
                link(nc.vector.tensor_scalar(pad_i[:], cnt[:], float(P - 1), None, ALU.add))
                link(nc.vector.tensor_scalar(pad_i[:], pad_i[:], 7, 7, ALU.arith_shift_right, ALU.logical_shift_left))
                link(nc.vector.tensor_copy(padded[:], pad_i[:]))
                link(nc.vector.tensor_tensor_scan(pend[:], onesv[:, 0:NX], padded[:], 0.0, ALU.mult, ALU.add))
                link(nc.vector.tensor_tensor(shift[:], pend[:], padded[:], ALU.subtract))
                link(nc.vector.tensor_tensor(shift[:], shift[:], off[:, :, NT - 1], ALU.subtract))
                link(nc.vector.tensor_tensor(shift[:], shift[:], cnt[:], ALU.add))
                link(nc.vector.tensor_tensor(flat_off, flat_off, flat_tot, ALU.subtract))
                link(nc.vector.tensor_tensor(off[:], off[:], shift[:].unsqueeze(2).to_broadcast([P, NX, NT]), ALU.add))
                for k in range(4):
                    t0, t1 = k * TQ, min(NT, (k + 1) * TQ)
                    if t0 < NT:
                        nc.vector.tensor_tensor(lg[:, t0:t1, :], off[:, :, t0:t1].rearrange("p e t -> p t e"),
                                                PS[:, k, 0:(t1 - t0) * NX].rearrange("p (t e) -> p t e", e=NX), ALU.add
                                                ).then_inc(chain2, 1)
                        links[0] += 1
                dve.wait_ge(chain2, links[0])
                link(nc.vector.tensor_tensor(lg[:], lg[:], oh[:], ALU.mult))
                nc.vector.tensor_reduce(place[:], lg[:], AX.X, ALU.add).then_inc(placed, 1)
                link(nc.vector.tensor_scalar(pend[:], pend[:], 1.0 / P, None, ALU.mult))
                link(nc.vector.tensor_tensor(behind[:], tile_no[:].unsqueeze(2).to_broadcast([1, ET, NX]),
                                             pend[0:1, :].unsqueeze(1).to_broadcast([1, ET, NX]), ALU.is_ge))
                link(nc.vector.tensor_reduce(expert_f[:], behind[:], AX.X, ALU.add))
                nc.vector.tensor_scalar(expert[:], expert_f[:], float(NX - 1), None, ALU.min).then_inc(ex_rdy, 1)
                for k, a in enumerate((mean, rstd, back, back)):
                    nc.vector.tensor_copy(info[:, :, k], a[:]).then_inc(placed, 1)
                dve.wait_ge(placed, 5)

                def stage_place(t):
                    wait(dve, sorted_in[t.r], 16 * t.q)
                    nc.vector.tensor_copy(place_c[:, t.r, :], place[:, ds(t.n, 1)]).then_inc(pc_rdy, 1)
                    nc.vector.tensor_copy(row_c[:, t.r, D:XW], node_row(info, t.n)).then_inc(info_rdy, 1)

                run_steps(dve, stage_place, 0, NT, U, NT)

                def norm_sorted(t):
                    dve.wait_ge(xe_ld[t.r], 16 * (t.q + 1))
                    wait(dve, xet_done, t.n - U + 1)
                    nc.vector.tensor_scalar(xen[:, t.r % U, :], xe[:, t.r, 0:D], xe[:, t.r, D:D + 1],
                                            xe[:, t.r, D + 1:D + 2], ALU.subtract, ALU.mult).then_inc(xen_rdy, 1)
                    wait(dve, y_out[t.r], 16 * t.q)
                    nc.vector.tensor_scalar(dest_c[:, t.r, :], xe[:, t.r, D + 2:D + 3], float(PADDEST), None,
                                            ALU.add).then_inc(dest_rdy, 1)

                def results(t):
                    dve.wait_ge(l2_done, t.n + 1)
                    wait(dve, y_out[t.r], 16 * t.q)
                    nc.vector.scalar_tensor_tensor(out=yo[:, t.r, :], in0=PS[:, 4 + t.r % U, 0:D], scalar=0.0,
                                                   in1=xe[:, t.r, 0:D], op0=ALU.max, op1=ALU.add).then_inc(yo_rdy, 1)

                def expert_step(s):
                    if (s + 3).there():
                        norm_sorted(s + 3)
                    if (s + -2).there():
                        results(s + -2)

                run_steps(dve, expert_step, -3, ET + 2, UE, ET)

            @block.tensor
            def _(pe):
                def turn_rows(source, ready, done, copied, banks):
                    def flip(t):
                        bank = t.r % banks
                        pe.wait_ge(ready, t.n + 1)
                        wait(pe, copied, t.n - banks + 1)
                        for c in range(KC):
                            last = nc.tensor.transpose(PS[:, bank, c * P:(c + 1) * P],
                                                       source[:, t.r % U, c * P:(c + 1) * P], ident[:])
                        last.then_inc(done, 1)
                    return flip

                flip_sums = turn_rows(agsum, ag_sum, agt_done, agT_rdy, 2)

                def lin2(t):
                    pe.wait_ge(agT_rdy, t.n + 1)
                    wait(pe, soft_rdy, t.n - U + 1)
                    nc.tensor.matmul(PS[:, 2 + t.r, 0:D], ones_r[:], lin2b_hl[:], start=True, stop=False)
                    for c in range(KC):
                        last = nc.tensor.matmul(PS[:, 2 + t.r, 0:D], aggT[:, t.r, c * P:(c + 1) * P],
                                                lin2_sb[:, c, :], start=False, stop=(c == KC - 1))
                    last.then_inc(lin2_done, 1)

                def flip_centred(t):
                    pe.wait_ge(cent_rdy, t.n + 1)
                    wait(pe, centT_rdy, t.n)
                    for c in range(KC):
                        last = nc.tensor.transpose(PS[:, 6, c * P:(c + 1) * P],
                                                   centred[:, t.r, c * P:(c + 1) * P], ident[:])
                    last.then_inc(centt_done, 1)

                def router(t):
                    pe.wait_ge(centT_rdy, t.n + 1)
                    wait(pe, lg_rdy, t.n)
                    for c in range(KC):
                        last = nc.tensor.matmul(PS[:, 7, 0:NX], centT[:, t.slot, c * P:(c + 1) * P],
                                                rwT[:, c, :], start=(c == 0), stop=(c == KC - 1))
                    last.then_inc(lg_done, 1)

                def node_step(s):
                    if (s + 1).there():
                        flip_sums(s + 1)
                    if s.there():
                        lin2(s)
                    if (s + -5).there():
                        flip_centred(s + -5)
                    if (s + -6).there():
                        router(s + -6)

                run_steps(pe, node_step, -1, NT + 6, U, NT)

                pe.wait_ge(oh_rdy, 1)
                TQ = 512 // NX
                for half, weights in ((0, upper_bf), (4, ones_bf)):
                    for k in range(4):
                        t0, t1 = k * TQ, min(NT, (k + 1) * TQ)
                        if t0 < NT:
                            last = nc.tensor.matmul(PS[:, half + k, 0:(t1 - t0) * NX], weights[:],
                                                    oh_bf[:, t0:t1, :].rearrange("p t e -> p (t e)"), start=True, stop=True)
                last.then_inc(count_done, 1)
                pe.wait_ge(placed, 1)

                flip_expert = turn_rows(xen, xen_rdy, xet_done, xeT_rdy, 2)

                def layer1(t):
                    pe.wait_ge(we_ld[t.r], 16 * (t.q + 1))
                    pe.wait_ge(xeT_rdy, t.n + 1)
                    wait(pe, he_rdy, t.n - 1)
                    for c in range(KC):
                        last = nc.tensor.matmul(PS[0:H, 2 + t.slot, 0:P], we[:, t.r, c * H:(c + 1) * H],
                                                aggT[:, t.r % U, c * P:(c + 1) * P], start=(c == 0), stop=(c == KC - 1))
                    last.then_inc(l1_done, 1)

                def layer2(t):
                    pe.wait_ge(he_rdy, t.n + 1)
                    wait(pe, yo_rdy, t.n - U + 1)
                    nc.tensor.matmul(PS[:, 4 + t.r % U, 0:D], he[:, t.r % U, :], we[0:H + 1, t.r, KC * H:KC * H + D],
                                     start=True, stop=True).then_inc(l2_done, 1)

                def expert_step(s):
                    if (s + 1).there():
                        flip_expert(s + 1)
                    if s.there():
                        layer1(s)
                    if (s + -1).there():
                        layer2(s + -1)

                run_steps(pe, expert_step, -1, ET + 1, UE, ET)


_INS = ["x", "src", "dst", "edge_attr_3", "edge_attr_50", "L0_gnn_mlp_w1", "L0_gnn_mlp_b1", "L0_gnn_mlp_w2",
        "L0_gnn_mlp_b2", "L0_gnn_lin1_w", "L0_gnn_lin2_w", "L0_gnn_lin2_b", "L0_ffn_router_w", "L0_ffn_router_b",
        "L0_ffn_W1", "L0_ffn_b1", "L0_ffn_W2", "L0_ffn_b2"]


def kernel(**inputs):
    import numpy as _np
    import concourse.bacc as _bacc
    from concourse import mybir as _mybir
    from concourse.bass_utils import run_bass_kernel_spmd as _run

    nc = _bacc.Bacc("TRN2", target_bir_lowering=False, num_devices=1)
    arrays, args = {}, []
    for name in _INS:
        a = _np.ascontiguousarray(inputs[name])
        arrays[f"in_{name}"] = a
        args.append(nc.dram_tensor(f"in_{name}", a.shape, _mybir.dt.from_np(a.dtype), kind="ExternalInput").ap())
    shape = inputs["x"].shape
    result = nc.dram_tensor("out_0", shape, _mybir.dt.float32, kind="ExternalOutput").ap()
    gnn_moe(nc, *args, result)
    r = _run(nc, [arrays], core_ids=[0])
    return r.results[0]["out_0"]
```

```python
import math
from contextlib import ExitStack

import concourse.bass as bass
import concourse.mybir as mybir

P = 128


class Step:
    def __init__(self, q, r, u, count):
        self.q, self.r, self.u, self.count = q, r, u, count

    def __add__(self, d):
        return Step(self.q + (self.r + d) // self.u, (self.r + d) % self.u, self.u, self.count)

    @property
    def n(self):
        return self.q * self.u + self.r

    @property
    def slot(self):
        return self.r % 2

    @property
    def turn(self):
        return self.q * (self.u // 2) + self.r // 2

    def there(self):
        return not isinstance(self.q, int) or 0 <= self.n < self.count


def run_steps(eng, body, first, end, u, count):
    start = max(1, -(-(end - count) // u), -(-first // u))
    turns = (count - max(1, -first)) // u
    for n in range(first, start * u):
        body(Step(n // u, n % u, u, count))
    with eng.Fori(start, turns) as q:
        for r in range(u):
            body(Step(q, r, u, count))
    for n in range(turns * u, end):
        body(Step(n // u, n % u, u, count))


def wait_apart(eng, semaphore, value, passed):
    if not isinstance(value, int) or value > 0:
        eng.wait_ge(semaphore, value)
        eng.sem_inc(passed, 1)


def wait(eng, semaphore, value):
    if not isinstance(value, int) or value > 0:
        eng.wait_ge(semaphore, value)


def gnn_moe(nc, x, src, dst, edge3, edge50, mlp_w1, mlp_b1, mlp_w2, mlp_b2, lin1_w, lin2_w, lin2_b,
            router_w, router_b, ffn_w1, ffn_b1, ffn_w2, ffn_b2, out):
    F32, F32R, BF16, I32 = mybir.dt.float32, mybir.dt.float32r, mybir.dt.bfloat16, mybir.dt.int32
    ALU, ACT, AX = mybir.AluOpType, mybir.ActivationFunctionType, mybir.AxisListType
    ds = bass.ds

    N, D = x.shape
    E, G = edge50.shape
    NX, _, H = ffn_w1.shape
    KC = D // P
    NT = -(-N // P)
    TG = NT // 7
    NLAST = N - (NT - 1) * P
    J = 4
    WJ = 2
    DW = (J + WJ) * P
    SE = J * P
    NS = -(-E // SE)
    U = 4
    UE = 8
    LASTE = E - (NS - 1) * SE
    RB = 2
    RH = NS // RB
    FULL = (NS - 1) % RH
    DUMMY = N
    PADROW = N + P
    TR = -(-(PADROW + 1) // P) * P
    ET = NX + (N - NX) // P
    XW = D + 4
    WW = KC * H + D + 1
    XG = NT // TG
    PADDEST = NT * P
    LN2 = math.log(2.0)
    EPS = 1e-5
    CUTOFF = 2.0
    assert NS == RB * RH and NS % U == 0 and LASTE % J == 0 and NT % 2 == 1 and ET % 2 == 0 and H < P
    assert NT == XG * TG and 2 * H == P

    z_dram = nc.dram_tensor("z_rows", [NT * P, D], F32).ap()
    dig_dram = nc.dram_tensor("src_digits", [2, NS * DW], BF16).ap()
    base_dram = nc.dram_tensor("window_rows", [NS], I32).ap()
    agg_dram = [nc.dram_tensor(f"agg_table{j}", [TR, D], F32).ap() for j in range(J)]
    xs_dram = nc.dram_tensor("sorted_rows", [ET * P, XW], F32).ap()
    wtab = nc.dram_tensor("expert_weights", [NX, P, WW], F32).ap()
    ZW = 2560
    XZ = ET * XW // 10
    assert (TR * D // P) % ZW == 0 and (ET * XW) % 10 == 0 and XZ <= ZW

    ctx = ExitStack()
    with ctx:
        def sb(name, shape, dt=F32):
            return ctx.enter_context(nc.sbuf_tensor(name, shape, dt))

        def sem(name):
            return ctx.enter_context(nc.semaphore(name))

        x_sb = sb("x_sb", [P, NT, D])
        ident = sb("ident", [P, P])
        ident_r = sb("ident_r", [P, P], F32R)
        upper = sb("upper", [P, P])
        minus_from = sb("minus_from", [P, P], BF16)
        ones_bf = sb("ones_bf", [P, P], BF16)
        ones_row = sb("ones_row", [1, P])
        ones_r = sb("ones_r", [33, P], F32R)
        neg_ln2 = sb("neg_ln2", [P, 1])
        half_c = sb("half_c", [P, 1])
        dummy = sb("dummy_rows", [P, 1])
        part_no = sb("part_no", [P, 1])
        digit_w = sb("digit_w", [2, P], BF16)
        w1_in = sb("w1_in", [P, D])
        w1_hh = sb("w1_hh", [P, D], F32R)
        w1_lo = sb("w1_lo", [G + 1, D], F32R)
        w2_sb = sb("w2_sb", [P, KC, D])
        b2_row = sb("b2_row", [1, D])
        b2_hl = sb("b2_hl", [33, D], F32R)
        lin1_sb = sb("lin1_sb", [P, KC, D])
        lin2_sb = sb("lin2_sb", [P, KC, D])
        lin2b_row = sb("lin2b_row", [1, D])
        lin2b_hl = sb("lin2b_hl", [33, D], F32R)
        rw_in = sb("rw_in", [NX, D])
        rwT = sb("rwT", [P, KC, NX])
        rb_all = sb("rb_all", [P, NX])
        stats = sb("stats", [P, NT, 6])
        mean = sb("mean", [P, NT])
        rstd = sb("rstd", [P, NT])
        tmp_n = sb("tmp_n", [P, NT])
        cols = sb("cols", [P, NS, 4 * J])

        PS = ctx.enter_context(nc.psum_tensor("PS", [P, 8, 512], F32))

        w_in = sem("w_in")
        x_in = [sem(f"x_in{g}") for g in range(XG)]
        staged = sem("staged")
        e_in = sem("e_in")
        zero_rdy = sem("zero_rdy")
        filled = sem("filled")
        consts = sem("consts")
        pool_passed = sem("pool_passed")
        pchain = sem("pchain")
        chain = sem("chain")
        chain2 = sem("chain2")
        st_rdy = sem("st_rdy")
        res_rdy = sem("res_rdy")
        xn_rdy = sem("xn_rdy")
        xnt_done = sem("xnt_done")
        xT_rdy = sem("xT_rdy")
        mmz_done = sem("mmz_done")
        zb_rdy = sem("zb_rdy")
        z_out = [sem(f"z_out{b}") for b in range(4)]
        sq_ask = sem("sq_ask")
        sq_rdy = sem("sq_rdy")
        pv_ask = sem("pv_ask")
        pv_rdy = sem("pv_rdy")
        padded_rdy = sem("padded_rdy")
        prow_rdy = sem("prow_rdy")
        pt_done = sem("pt_done")
        pt_free = sem("pt_free")
        dig_rdy = sem("dig_rdy")
        dig_out = sem("dig_out")
        wprep = sem("wprep")
        wprep_mm = sem("wprep_mm")
        prep_done = sem("prep_done")

        def node_row(a, n):
            return a[:, ds(n, 1), :].rearrange("p a d -> p (a d)")

        def norm_bulk(vec, link, count):
            me, mo = stats[:, :, 1], stats[:, :, 4]
            link(nc.vector.tensor_tensor(mean[:], me, mo, ALU.add))
            link(nc.vector.tensor_tensor(tmp_n[:], me, mo, ALU.subtract))
            link(nc.vector.tensor_scalar(mean[:], mean[:], 0.5, None, ALU.mult))
            link(nc.vector.scalar_tensor_tensor(out=tmp_n[:], in0=tmp_n[:], scalar=0.25, in1=tmp_n[:],
                                                op0=ALU.mult, op1=ALU.mult))
            link(nc.vector.tensor_tensor(rstd[:], stats[:, :, 2], stats[:, :, 5], ALU.add))
            link(nc.vector.scalar_tensor_tensor(out=tmp_n[:], in0=rstd[:], scalar=1.0 / D, in1=tmp_n[:],
                                                op0=ALU.mult, op1=ALU.add))
            nc.vector.tensor_scalar(tmp_n[:], tmp_n[:], EPS, None, ALU.add).then_inc(sq_ask, 1)
            vec.wait_ge(sq_rdy, count)
            link(nc.vector.reciprocal(rstd[:], rstd[:]))

        part1 = ExitStack()
        with part1:
            def sb1(name, shape, dt=F32):
                return part1.enter_context(nc.sbuf_tensor(name, shape, dt))

            rowbuf = sb1("rowbuf", [P, U, D])
            RW = RB * SE
            work = sb1("work", [P, ZW + 5 * RW + U * J * D])
            a_in = sb1("a_in", [P, U, J * G])
            a_hl = sb1("a_hl", [P, 2, J, P], F32R)
            aT = sb1("aT", [P, 2, SE], F32R)
            digits = sb1("digits", [2, U, DW], BF16)
            zw_hi = sb1("zw_hi", [P, 2, D], F32R)
            zw_lo = sb1("zw_lo", [P, 2, D], F32R)
            onehot = sb1("onehot", [P, 2, WJ * P], F32R)
            base = sb1("base", [RH, RB])
            base_i = sb1("base_i", [RH, RB], I32)
            base_row = sb1("base_row", [1, NS], I32)
            reach = sb1("reach", [RH, 1])
            reach_all = sb1("reach_all", [1, 1])
            outside = sb1("outside", [1, 1], I32)
            dstc = sb1("dstc", [P, U, J], I32)
            sel = sb1("sel", [P, U, 3 * J])
            hT = sb1("hT", [P, 2, KC, SE])
            zg = sb1("zg", [P, U, J, D])
            msg_hi = sb1("msg_hi", [P, 2, J, D], F32R)
            msg_lo = sb1("msg_lo", [P, 2, J, D], F32R)
            same = sb1("same", [P, U, J, P], F32R)
            later = sb1("later", [P, 2, J])
            tab_f = sb1("tab_f", [P, 2, J])
            tabc = sb1("tabc", [P, U, J], I32)
            summed = work[:, ZW + 5 * RW:].rearrange("p (u j d) -> p u j d", u=U, j=J)

            r_int = zg[0:RH, 0].bitcast(I32).rearrange("p j d -> p (j d)")
            r_dst = zg[0:RH, 1].bitcast(I32).rearrange("p j d -> p (j d)")
            r_srcf = zg[0:RH, 2].rearrange("p j d -> p (j d)")
            r_dstf = zg[0:RH, 3].rearrange("p j d -> p (j d)")
            r_hi = cols[0:RH].rearrange("p n k -> p (n k)")[:, 0:RW].bitcast(I32)
            r_lo = rowbuf[0:RH].rearrange("p u d -> p (u d)").bitcast(I32)
            r_e3 = hT[0:RH].rearrange("p b c s -> p (b c s)")
            r_e3b = summed[0:RH, 0:2].rearrange("p u j d -> p (u j d)")
            assert RW == J * D and 2 * KC * SE == 2 * RW
            spare = work[0:RH, ZW:ZW + 5 * RW]
            r_xyz = spare[:, 0:3 * RW]
            assert 3 * RW == 2 * J * D + U * D and U * D + 2 * D <= 3 * RW and RW == KC * SE and U * D == RW
            xn = work[:, ZW:ZW + U * D].rearrange("p (u d) -> p u d", u=U)
            xT = work[:, ZW + U * D:ZW + U * D + 2 * D].rearrange("p (b d) -> p b d", b=2)
            msg = work[:, ZW:ZW + 2 * J * D].rearrange("p (b j d) -> p b j d", b=2, j=J)
            zwin = work[:, ZW + 2 * J * D:ZW + 3 * RW].rearrange("p (u d) -> p u d", u=U)
            soft1 = work[:, ZW + 3 * RW:ZW + 4 * RW].rearrange("p (c s) -> p c s", c=KC)
            r_dig = [spare[:, (3 + k) * RW:(3 + k) * RW + RB * DW // 2].bitcast(BF16).rearrange(
                "p (a j q) -> p a j q", a=RB, j=J + WJ) for k in range(2)]
            r_d2 = r_e3[:, 0:RW]
            r_t = r_e3[:, RW:2 * RW]
            r_c = r_e3b[:, 0:RW]
            r_m = r_e3b[:, RW:2 * RW]

            a_ld = [sem(f"a_ld{b}") for b in range(U)]
            dg_ld = [sem(f"dg_ld{b}") for b in range(U)]
            hi_rdy = sem("hi_rdy")
            lo_rdy = sem("lo_rdy")
            at_done = sem("at_done")
            aT_rdy = sem("aT_rdy")
            dg_done = sem("dg_done")
            col_rdy = sem("col_rdy")
            dst_rdy = sem("dst_rdy")
            pre_done = sem("pre_done")
            absv_done = sem("absv_done")
            exp_done = sem("exp_done")
            ln_done = sem("ln_done")
            h_rdy = sem("h_rdy")
            w_done = sem("w_done")
            z_ld = [sem(f"z_ld{b}") for b in range(U)]
            msg_rdy = sem("msg_rdy")
            same_rdy = sem("same_rdy")
            tabf_rdy = sem("tabf_rdy")
            tab_rdy = sem("tab_rdy")
            sum_done = sem("sum_done")
            sum_rdy = sem("sum_rdy")
            added = [sem(f"added{j}") for j in range(J)]
            base_rdy = sem("base_rdy")
            base_in = sem("base_in")
            reach_rdy = sem("reach_rdy")
            reach_done = sem("reach_done")
            outside_rdy = sem("outside_rdy")
            zw_ld = [sem(f"zw_ld{b}") for b in range(U)]
            rel_done = sem("rel_done")
            onehot_rdy = sem("onehot_rdy")
            expand_done = sem("expand_done")
            zx_rdy = sem("zx_rdy")
            zwhi_rdy = sem("zwhi_rdy")
            zwlo_rdy = sem("zwlo_rdy")
            mhi_rdy = sem("mhi_rdy")
            mlo_rdy = sem("mlo_rdy")

            def sup(n):
                return Step(n // U, n % U, U, NS)

            def steps(eng, body, first):
                run_steps(eng, body, first, NS + 2, U, NS)

            with nc.Block() as block:
                @block.sync
                def _(sp):
                    sp.wait_ge(padded_rdy, 3)
                    for a in range(RB):
                        rows = RH if a < RB - 1 else FULL
                        e0, e1 = a * RH * SE, (a * RH + rows) * SE
                        for dest, arr, w in ((r_xyz, edge3.rearrange("e c -> (e c)"), 3), (r_int, src, 1),
                                             (r_dst, dst, 1)):
                            sp.dma_start(dest[0:rows, a * SE * w:(a + 1) * SE * w],
                                         arr[e0 * w:e1 * w].rearrange("(r s) -> r s", s=SE * w)).then_inc(e_in, 16)
                            if rows < RH:
                                sp.dma_start(dest[rows:rows + 1, a * SE * w:(a * SE + LASTE) * w],
                                             arr[e1 * w:E * w].rearrange("(r s) -> r s", r=1)).then_inc(e_in, 16)
                    sp.wait_ge(consts, 1)
                    for g in range(XG):
                        t0, t1 = g * TG, min((g + 1) * TG, NT - 1)
                        sp.dma_start(x_sb[:, t0:t1, :],
                                     x[t0 * P:t1 * P, :].rearrange("(t p) d -> p t d", p=P)).then_inc(x_in[g], 16)
                    sp.dma_start(x_sb[0:NLAST, NT - 1, :], x[(NT - 1) * P:N, :]).then_inc(x_in[XG - 1], 16)
                    sp.wait_ge(dig_rdy, 4)
                    for k in range(2):
                        for a in range(RB):
                            sp.dma_start(dig_dram[k, a * RH * DW:(a + 1) * RH * DW].rearrange("(r s) -> r s", s=DW),
                                         r_dig[k][:, a].rearrange("p j q -> p (j q)")).then_inc(dig_out, 16)
                    sp.wait_ge(base_rdy, 1)
                    for a in range(RB):
                        sp.dma_start(base_dram[a * RH:(a + 1) * RH].rearrange("(r o) -> r o", o=1),
                                     base_i[:, a:a + 1]).then_inc(dig_out, 16)
                    sp.wait_ge(dig_out, 16 * 3 * RB)
                    sp.dma_start(base_row[:], base_dram.rearrange("(o r) -> o r", o=1)).then_inc(base_in, 16)

                    sp.wait_ge(zero_rdy, 1)
                    sp.wait_ge(w_in, 16 * 10)
                    zeros = work[:, 0:ZW]
                    parts = TR * D // P // ZW

                    def fill(k):
                        flat = agg_dram[k // parts].rearrange("(p k) d -> p (k d)", p=P)
                        sp.dma_start(flat[:, k % parts * ZW:(k % parts + 1) * ZW], zeros).then_inc(filled, 16)

                    for k in range(J * parts - 6):
                        if k >= 5:
                            sp.wait_ge(xn_rdy, 4 * (k - 4))
                        fill(k)

                    def load(t):
                        wait(sp, hi_rdy, t.n - U + 1)
                        wait(sp, lo_rdy, t.n - U + 1)
                        wait(sp, dg_done, t.n - U + 1)
                        sp.dma_start(digits[:, t.r, :], dig_dram[:, ds(t.n * DW, DW)]).then_inc(dg_ld[t.r], 16)
                        if isinstance(t.q, int) and t.n == NS - 1:
                            k = LASTE // J
                            sp.dma_start(a_in[0:k, t.r, :],
                                         edge50[t.n * SE:E, :].rearrange("(p j) g -> p (j g)", j=J)
                                         ).then_inc(a_ld[t.r], 16)
                            sp.dma_start(a_in[k:P, t.r, :],
                                         edge50[0:(P - k) * J, :].rearrange("(p j) g -> p (j g)", j=J)
                                         ).then_inc(a_ld[t.r], 16)
                        else:
                            sp.dma_start(a_in[:, t.r, :],
                                         edge50[ds(t.n * SE, SE), :].rearrange("(p j) g -> p (j g)", j=J)
                                         ).then_inc(a_ld[t.r], 16)

                    def window(t):
                        wait(sp, zwlo_rdy, t.n - U + 1)
                        row = sp.value_load(base_row[0:1, ds(t.n, 1)], min_val=0, max_val=NT * P - P)
                        sp.dma_start(zwin[:, t.r, :], z_dram[ds(row, P), :]).then_inc(zw_ld[t.r], 16)

                    def edge_loads(windowed):
                        def load_all(t):
                            load(t)
                            if windowed:
                                window(t)

                        for n in range(U, 2 * U):
                            if n < U + 3:
                                sp.wait_ge(z_ld[n - U], 16 * (J - WJ if windowed else J))
                                fill(J * parts - 6 + 2 * (n - U))
                                fill(J * parts - 5 + 2 * (n - U))
                            load_all(Step(1, n - U, U, NS))
                        run_steps(sp, load_all, 2 * U, NS, U, NS)

                    for n in range(U):
                        load(Step(0, n, U, NS))
                    sp.wait_ge(base_in, 16)
                    sp.wait_ge(outside_rdy, 1)
                    for b in range(U):
                        sp.wait_ge(z_out[b], 16 * len(range(b, NT, U)))
                    general = sp.value_load(outside[0:1, 0:1], min_val=0, max_val=1)
                    with sp.If(general == 0):
                        for n in range(U):
                            window(Step(0, n, U, NS))
                        edge_loads(True)
                    with sp.Else():
                        edge_loads(False)
                    for j in range(J):
                        sp.wait_ge(added[j], 16 * NS)

                @block.gpsimd
                def _(pool):
                    nc.gpsimd.memset(r_xyz, 2 * CUTOFF).then_inc(padded_rdy, 1)
                    nc.gpsimd.memset(x_sb[:, NT - 1, :], 0.0).then_inc(consts, 1)
                    nc.gpsimd.memset(ident[:], 1.0).then_inc(pchain, 1)
                    nc.gpsimd.memset(upper[:], 1.0).then_inc(pchain, 1)
                    nc.gpsimd.memset(ones_bf[:], 1.0).then_inc(pchain, 1)
                    nc.gpsimd.memset(minus_from[:], -1.0).then_inc(pchain, 1)
                    pool.wait_ge(pchain, 4)
                    nc.gpsimd.affine_select(out=ident[:], in_=ident[:], compare_op=ALU.is_equal, fill=0.0, base=0,
                                            pattern=[[-1, P]], channel_multiplier=1).then_inc(consts, 1)
                    nc.gpsimd.affine_select(out=upper[:], in_=upper[:], compare_op=ALU.is_ge, fill=0.0, base=0,
                                            pattern=[[1, P]], channel_multiplier=-1).then_inc(consts, 1)
                    nc.gpsimd.affine_select(out=minus_from[:], in_=minus_from[:], compare_op=ALU.is_ge, fill=0.0,
                                            base=0, pattern=[[-1, P]], channel_multiplier=1).then_inc(consts, 1)
                    nc.gpsimd.iota(dummy[:], pattern=[[0, 1]], base=DUMMY, channel_multiplier=1,
                                   allow_small_or_imprecise_dtypes=True).then_inc(consts, 1)
                    nc.gpsimd.iota(part_no[:], pattern=[[0, 1]], base=0, channel_multiplier=1,
                                   allow_small_or_imprecise_dtypes=True).then_inc(consts, 1)
                    nc.gpsimd.memset(ones_row[:], 1.0).then_inc(consts, 1)
                    nc.gpsimd.memset(neg_ln2[:], -LN2).then_inc(consts, 1)
                    nc.gpsimd.memset(half_c[:], 0.5).then_inc(consts, 1)
                    nc.gpsimd.memset(digit_w[:], 1.0).then_inc(pchain, 1)
                    pool.wait_ge(pchain, 5)
                    nc.gpsimd.memset(digit_w[0:1, :], float(P)).then_inc(consts, 1)

                    def gather(t, tiles):
                        wait_apart(pool, dst_rdy, t.n + 1, pool_passed)
                        wait_apart(pool, msg_rdy, J * (t.n - U) + J, pool_passed)
                        for j in tiles:
                            nc.gpsimd.indirect_dma_start(
                                out=zg[:, t.r, j, :], out_offset=None, in_=z_dram,
                                in_offset=bass.IndirectOffsetOnAxis(ap=dstc[:, t.r, j:j + 1], axis=0)
                            ).then_inc(z_ld[t.r], 16)

                    def scatter(t):
                        wait_apart(pool, tab_rdy, t.n + 1, pool_passed)
                        wait_apart(pool, sum_rdy, t.n + 1, pool_passed)
                        for j in range(J):
                            wait_apart(pool, added[j], 16 * t.n, pool_passed)
                            nc.gpsimd.indirect_dma_start(
                                out=agg_dram[j],
                                out_offset=bass.IndirectOffsetOnAxis(ap=tabc[:, t.r, j:j + 1], axis=0),
                                in_=summed[:, t.r, j, :], in_offset=None, compute_op=ALU.add,
                                bounds_check=TR - 1).then_inc(added[j], 16)

                    for dest, arr in ((lin1_sb[:], lin1_w.rearrange("(c p) n -> p c n", p=P)),
                                      (w2_sb[:], mlp_w2.rearrange("(c p) n -> p c n", p=P)),
                                      (w1_in[0:G, :], mlp_w1), (w1_in[64:64 + G, :], mlp_w1),
                                      (w1_in[G:G + 1, :], mlp_b1.rearrange("(r n) -> r n", r=1)),
                                      (b2_row[:], mlp_b2.rearrange("(r n) -> r n", r=1)),
                                      (lin2_sb[:], lin2_w.rearrange("(c p) n -> p c n", p=P)),
                                      (lin2b_row[:], lin2_b.rearrange("(r n) -> r n", r=1)),
                                      (rw_in[:], router_w),
                                      (rb_all[:], router_b.rearrange("(r n) -> r n", r=1).to_broadcast([P, NX]))):
                        pool.dma_start(dest, arr).then_inc(w_in, 16)

                    def residual(t):
                        pool.wait_ge(xn_rdy, t.n + 1)
                        nc.gpsimd.tensor_tensor(node_row(x_sb, t.n), node_row(x_sb, t.n), xn[:, t.r, :], ALU.add
                                                ).then_inc(res_rdy, 1)

                    run_steps(pool, residual, 0, NT, U, NT)

                    for b in range(U):
                        pool.wait_ge(z_out[b], 16 * len(range(b, NT, U)))

                    def edge_dmas(tiles):
                        def body(s):
                            if (s + 2).there():
                                gather(s + 2, tiles)
                            if (s + -2).there():
                                if isinstance(s.q, int) and s.n == 2:
                                    pool.wait_ge(filled, 16 * J * (TR * D // P // ZW))
                                scatter(s + -2)

                        steps(pool, body, -2)

                    pool.wait_ge(outside_rdy, 1)
                    general = pool.value_load(outside[0:1, 0:1], min_val=0, max_val=1)
                    with pool.If(general == 0):
                        edge_dmas(range(WJ, J))
                    with pool.Else():
                        edge_dmas(range(J))

                @block.scalar
                def _(act):
                    act.wait_ge(pv_ask, 1)
                    nc.scalar.activation(r_d2, r_d2, ACT.Sqrt).then_inc(pv_rdy, 1)
                    act.wait_ge(pv_ask, 2)
                    nc.scalar.activation(r_t, r_t, ACT.Sin).then_inc(pv_rdy, 1)
                    for k in range(3 * RB):
                        what, a = (0, 1, 3)[k // RB], k % RB
                        act.wait_ge(pt_done, k + 1)
                        nc.scalar.copy(cols[:, a * RH:(a + 1) * RH, what * J:(what + 1) * J],
                                       PS[:, 4 + k % 2, 0:J * RH].rearrange("p (j r) -> p r j", j=J)
                                       ).then_inc(pt_free, 1)
                    act.wait_ge(sq_ask, 1)
                    nc.scalar.activation(rstd[:], tmp_n[:], ACT.Sqrt).then_inc(sq_rdy, 1)

                    def norm_tile(t):
                        act.wait_ge(xnt_done, t.n + 1)
                        wait(act, mmz_done, t.n - 1)
                        nc.scalar.copy(xT[:, t.slot, :], PS[:, t.slot, 0:D]).then_inc(xT_rdy, 1)

                    def store_z(t):
                        act.wait_ge(zb_rdy, t.n + 1)
                        act.dma_start(z_dram[ds(t.n * P, P), :], rowbuf[:, t.r, :]).then_inc(z_out[t.r], 16)

                    def norm_step(s):
                        if (s + 1).there():
                            norm_tile(s + 1)
                        if (s + -1).there():
                            store_z(s + -1)

                    run_steps(act, norm_step, -1, NT + 1, U, NT)

                    def columns(t):
                        wait(act, msg_rdy, J * (t.n - U) + J)
                        nc.scalar.copy(sel[:, t.r, :], cols[:, ds(t.n, 1), 0:3 * J].rearrange("p a k -> p (a k)")
                                       ).then_inc(col_rdy, 1)
                        nc.scalar.copy(dstc[:, t.r, :], cols[:, ds(t.n, 1), 3 * J:4 * J].rearrange("p a k -> p (a k)")
                                       ).then_inc(dst_rdy, 1)

                    def high(t):
                        act.wait_ge(a_ld[t.r], 16 * (t.q + 1))
                        if isinstance(t.q, int) and t.n == NS - 1:
                            act.wait_ge(a_ld[t.r], 16 * (t.q + 2))
                        wait(act, at_done, t.n - 1)
                        nc.scalar.copy(a_hl[:, t.slot, :, 0:G],
                                       a_in[:, t.r, :].rearrange("p (j g) -> p j g", j=J)).then_inc(hi_rdy, 1)

                    def softplus(t):
                        wait(act, h_rdy, KC * t.n)
                        for c in range(KC):
                            act.wait_ge(pre_done, KC * t.n + c + 1)
                            nc.scalar.activation(soft1[:, c, :], PS[:, 1 + c, :], ACT.Abs).then_inc(absv_done, 1)
                        for c in range(KC):
                            act.wait_ge(absv_done, KC * t.n + c + 1)
                            nc.scalar.activation(soft1[:, c, :], soft1[:, c, :], ACT.Exp, scale=-1.0
                                                 ).then_inc(exp_done, 1)
                        for c in range(KC):
                            act.wait_ge(exp_done, KC * t.n + c + 1)
                            nc.scalar.activation(soft1[:, c, :], soft1[:, c, :], ACT.Ln, bias=1.0).then_inc(ln_done, 1)

                    def features(t):
                        act.wait_ge(at_done, t.n + 1)
                        wait(act, pre_done, KC * (t.n - 1))
                        nc.scalar.copy(aT[:, t.slot, :], PS[:, 0, :]).then_inc(aT_rdy, 1)

                    def sums(t):
                        act.wait_ge(sum_done, t.n + 1)
                        for j in range(J):
                            wait(act, added[j], 16 * (t.n - U + 1))
                        nc.scalar.copy(summed[:, t.r].rearrange("p (a j) d -> p a (j d)", a=2),
                                       PS[:, 6:8, :]).then_inc(sum_rdy, 1)

                    act.wait_ge(prep_done, 1)
                    nc.scalar.preload_act_table_set("natural_log_exp_and_others")

                    def expanded(t):
                        act.wait_ge(expand_done, t.n + 1)
                        wait(act, msg_rdy, J * (t.n - U) + J)
                        nc.scalar.copy(zg[:, t.r, 0:WJ, :].rearrange("p j d -> p (j d)"), PS[:, 5, 0:WJ * D]
                                       ).then_inc(zx_rdy, 1)

                    def window_high(t):
                        act.wait_ge(zw_ld[t.r], 16 * (t.q + 1))
                        wait(act, expand_done, t.n - 1)
                        nc.scalar.copy(zw_hi[:, t.slot, :], zwin[:, t.r, :]).then_inc(zwhi_rdy, 1)

                    def message_high(t):
                        act.wait_ge(msg_rdy, J * t.n + J)
                        wait(act, sum_done, t.n - 1)
                        nc.scalar.copy(msg_hi[:, t.slot], msg[:, t.slot]).then_inc(mhi_rdy, 1)

                    def edge_work(windowed):
                        def body(s):
                            if (s + -1).there():
                                message_high(s + -1)
                            if (s + 3).there():
                                columns(s + 3)
                                high(s + 3)
                            if windowed and (s + 2).there():
                                window_high(s + 2)
                            if (s + 1).there():
                                softplus(s + 1)
                            if (s + 2).there():
                                features(s + 2)
                            if windowed and (s + 1).there():
                                expanded(s + 1)
                            if (s + -1).there():
                                sums(s + -1)

                        steps(act, body, -3)

                    act.wait_ge(dig_out, 16 * 3 * RB)
                    act.wait_ge(outside_rdy, 1)
                    general = act.value_load(outside[0:1, 0:1], min_val=0, max_val=1)
                    with act.If(general == 0):
                        edge_work(True)
                    with act.Else():
                        edge_work(False)

                @block.vector
                def _(dve):
                    links = [0]

                    def link(ins):
                        links[0] += 1
                        ins.then_inc(chain, 1)
                        dve.wait_ge(chain, links[0])

                    nc.vector.memset(r_int, PADROW).then_inc(padded_rdy, 1)
                    nc.vector.memset(r_dst, N - 1).then_inc(padded_rdy, 1)
                    nc.vector.memset(work[:, 0:ZW], 0.0).then_inc(zero_rdy, 1)
                    nc.vector.memset(a_hl[:].bitcast(F32), 0.0).then_inc(prow_rdy, 1)
                    nc.vector.memset(w1_hh[:].bitcast(F32), 0.0).then_inc(chain, 1)
                    nc.vector.memset(b2_hl[:].bitcast(F32), 0.0).then_inc(chain, 1)
                    nc.vector.memset(lin2b_hl[:].bitcast(F32), 0.0).then_inc(chain, 1)
                    nc.vector.memset(ones_r[:].bitcast(F32), 1.0).then_inc(chain, 1)
                    links[0] += 4
                    dve.wait_ge(prow_rdy, 1)
                    nc.vector.memset(a_hl[:, :, :, G:G + 1].bitcast(F32), 1.0).then_inc(chain, 1)
                    links[0] += 1

                    dve.wait_ge(e_in, 16 * 3 * (RB + 1))
                    xyz = r_xyz.rearrange("p (s c) -> p s c", c=3)
                    nc.vector.tensor_tensor(r_t, xyz[:, :, 0], xyz[:, :, 0], ALU.mult).then_inc(chain, 1)
                    nc.vector.tensor_tensor(r_d2, xyz[:, :, 1], xyz[:, :, 1], ALU.mult).then_inc(chain, 1)
                    nc.vector.tensor_tensor(r_m, xyz[:, :, 2], xyz[:, :, 2], ALU.mult).then_inc(chain, 1)
                    links[0] += 3
                    dve.wait_ge(chain, links[0])
                    link(nc.vector.tensor_tensor(r_t, r_t, r_d2, ALU.add))
                    nc.vector.tensor_tensor(r_d2, r_t, r_m, ALU.add).then_inc(pv_ask, 1)
                    nc.vector.tensor_copy(r_srcf, r_int).then_inc(chain, 1)
                    nc.vector.tensor_copy(r_dstf, r_dst).then_inc(chain, 1)
                    nc.vector.tensor_scalar(r_hi, r_int, 7, None, ALU.arith_shift_right).then_inc(chain, 1)
                    nc.vector.tensor_scalar(r_lo, r_int, P - 1, None, ALU.bitwise_and).then_inc(chain, 1)
                    links[0] += 4
                    dve.wait_ge(chain, links[0])
                    for k, d in enumerate((r_hi, r_lo)):
                        nc.vector.tensor_copy(r_dig[k][:, :, 0:J, :], d.rearrange("p (a q j) -> p a j q", a=RB, j=J)
                                              ).then_inc(dig_rdy, 1)
                    link(nc.vector.tensor_reduce(base[:], r_dstf.rearrange("p (a s) -> p a s", a=RB), AX.X, ALU.min))
                    link(nc.vector.tensor_scalar(base[:], base[:], float(NT * P - P), None, ALU.min))
                    nc.vector.tensor_copy(base_i[:], base[:]).then_inc(base_rdy, 1)
                    nc.vector.memset(r_dig[0][:, :, J:, :], 0.0).then_inc(dig_rdy, 1)
                    nc.vector.tensor_tensor(r_dig[1][:, :, J:, :],
                                            r_dstf.rearrange("p (a q j) -> p a j q", a=RB, j=J)[:, :, 0:WJ, :],
                                            base[:].unsqueeze(2).unsqueeze(3).to_broadcast([RH, RB, WJ, P]),
                                            ALU.subtract).then_inc(dig_rdy, 1)
                    dve.wait_ge(dig_rdy, 4)
                    nc.vector.tensor_reduce(reach[:], r_dig[1][:, :, J:, :], AX.XYZ, ALU.max).then_inc(reach_rdy, 1)
                    dve.wait_ge(pv_rdy, 1)
                    nc.vector.tensor_scalar(r_m, r_d2, CUTOFF, 0.5, ALU.is_le, ALU.mult).then_inc(chain, 1)
                    nc.vector.tensor_scalar(r_t, r_d2, CUTOFF, -math.pi / CUTOFF, ALU.min, ALU.mult).then_inc(chain, 1)
                    links[0] += 2
                    dve.wait_ge(chain, links[0])
                    nc.vector.tensor_scalar(r_t, r_t, math.pi / 2, None, ALU.add).then_inc(pv_ask, 1)

                    dve.wait_ge(pv_rdy, 2)
                    nc.vector.scalar_tensor_tensor(out=r_c, in0=r_t, scalar=1.0, in1=r_m, op0=ALU.add,
                                                   op1=ALU.mult).then_inc(prow_rdy, 1)

                    for g in range(XG):
                        dve.wait_ge(x_in[g], 16 if g < XG - 1 else 32)
                        for n in range(g * TG, (g + 1) * TG):
                            nc.vector.bn_stats(stats[:, n, :], x_sb[:, n, :]).then_inc(st_rdy, 1)
                    dve.wait_ge(st_rdy, NT)
                    norm_bulk(dve, link, 1)

                    dve.wait_ge(reach_done, 1)
                    link(nc.vector.tensor_reduce(reach_all[:], PS[0:1, 6, 256:256 + RH], AX.X, ALU.max))
                    nc.vector.tensor_scalar(outside[:], reach_all[:], P - 0.5, None, ALU.is_gt).then_inc(outside_rdy, 1)
                    dve.wait_ge(pt_free, 3 * RB)
                    dve.wait_ge(consts, 10)
                    nc.vector.tensor_scalar(cols[:, :, 2 * J:3 * J], cols[:, :, 0:J], -1.0, dummy[:, 0:1],
                                            ALU.mult, ALU.add).then_inc(prep_done, 1)

                    def norm_row(t):
                        wait(dve, xnt_done, t.n - U + 1)
                        wait(dve, res_rdy, t.n - U + 1)
                        nc.vector.tensor_scalar(xn[:, t.r, :], node_row(x_sb, t.n), mean[:, ds(t.n, 1)],
                                                rstd[:, ds(t.n, 1)], ALU.subtract, ALU.mult).then_inc(xn_rdy, 1)

                    def z_rows(t):
                        dve.wait_ge(mmz_done, t.n + 1)
                        wait(dve, z_out[t.r], 16 * t.q)
                        nc.vector.tensor_copy(rowbuf[:, t.r, :], PS[:, 2 + t.slot, 0:D]).then_inc(zb_rdy, 1)

                    def norm_step(s):
                        if (s + 3).there():
                            norm_row(s + 3)
                        if s.there():
                            z_rows(s)

                    run_steps(dve, norm_step, -3, NT, U, NT)

                    dve.wait_ge(w_in, 16 * 10)
                    nc.vector.tensor_copy(ident_r[:], ident[:]).then_inc(chain, 1)
                    nc.vector.tensor_copy(w1_hh[0:G + 1, :], w1_in[0:G + 1, :]).then_inc(chain, 1)
                    nc.vector.tensor_copy(w1_hh[64:64 + G, :], w1_in[64:64 + G, :]).then_inc(chain, 1)
                    links[0] += 3
                    dve.wait_ge(chain, links[0])
                    link(nc.vector.tensor_tensor(w1_lo[:], w1_in[0:G + 1, :], w1_hh[0:G + 1, :].bitcast(F32), ALU.subtract))
                    dve.wait_ge(wprep_mm, 1)
                    for c in range(KC):
                        nc.vector.tensor_copy(rwT[:, c, :], PS[:, 6, c * NX:(c + 1) * NX]).then_inc(chain, 1)
                        links[0] += 1
                    link(nc.vector.tensor_tensor(b2_row[:], b2_row[:], PS[0:1, 7, 0:D], ALU.add))
                    for row, hl in ((b2_row, b2_hl), (lin2b_row, lin2b_hl)):
                        link(nc.vector.tensor_copy(hl[0:1, :], row[:]))
                        link(nc.vector.tensor_tensor(row[:], row[:], hl[0:1, :].bitcast(F32), ALU.subtract))
                        nc.vector.tensor_copy(hl[32:33, :], row[:]).then_inc(wprep, 1)

                    def low(t):
                        dve.wait_ge(hi_rdy, t.n + 1)
                        nc.vector.tensor_tensor(a_hl[:, t.slot, :, 64:64 + G],
                                                a_in[:, t.r, :].rearrange("p (j g) -> p j g", j=J),
                                                a_hl[:, t.slot, :, 0:G].bitcast(F32), ALU.subtract).then_inc(lo_rdy, 1)

                    def hidden(t):
                        wait(dve, w_done, 2 * (t.n - 1))
                        for c in range(KC):
                            dve.wait_ge(ln_done, KC * t.n + c + 1)
                            nc.vector.scalar_tensor_tensor(out=hT[:, t.slot, c, :], in0=PS[:, 1 + c, :], scalar=0.0,
                                                           in1=soft1[:, c, :], op0=ALU.max, op1=ALU.add
                                                           ).then_inc(h_rdy, 1)

                    def window_low(t):
                        dve.wait_ge(zwhi_rdy, t.n + 1)
                        wait(dve, expand_done, t.n - 1)
                        nc.vector.tensor_tensor(zw_lo[:, t.slot, :], zwin[:, t.r, :],
                                                zw_hi[:, t.slot, :].bitcast(F32), ALU.subtract).then_inc(zwlo_rdy, 1)

                    def message_low(t):
                        dve.wait_ge(mhi_rdy, t.n + 1)
                        wait(dve, sum_done, t.n - 1)
                        nc.vector.tensor_tensor(msg_lo[:, t.slot], msg[:, t.slot],
                                                msg_hi[:, t.slot].bitcast(F32), ALU.subtract).then_inc(mlo_rdy, 1)

                    def equal(t):
                        dve.wait_ge(dg_done, t.n + 1)
                        dve.wait_ge(col_rdy, t.n + 1)
                        wait(dve, sum_done, t.n - U + 1)
                        wait(dve, tabf_rdy, t.n - 1)
                        for j in range(J):
                            nc.vector.scalar_tensor_tensor(out=same[:, t.r, j, :], in0=PS[:, 5, j * P:(j + 1) * P],
                                                           scalar=sel[:, t.r, j:j + 1], in1=upper[:],
                                                           op0=ALU.is_equal, op1=ALU.mult,
                                                           accum_out=later[:, t.slot, j:j + 1]).then_inc(same_rdy, 1)

                    def targets_f(t):
                        dve.wait_ge(same_rdy, J * t.n + J)
                        wait(dve, tab_rdy, t.n - 1)
                        nc.vector.scalar_tensor_tensor(out=tab_f[:, t.slot, :], in0=later[:, t.slot, :], scalar=1.5,
                                                       in1=sel[:, t.r, 2 * J:3 * J], op0=ALU.is_gt, op1=ALU.mult
                                                       ).then_inc(tabf_rdy, 1)

                    def targets(t):
                        dve.wait_ge(tabf_rdy, t.n + 1)
                        for j in range(J):
                            wait(dve, added[j], 16 * (t.n - U + 1))
                        nc.vector.tensor_tensor(tabc[:, t.r, :], tab_f[:, t.slot, :], sel[:, t.r, 0:J], ALU.add
                                                ).then_inc(tab_rdy, 1)

                    def hot(t):
                        dve.wait_ge(rel_done, t.n + 1)
                        wait(dve, expand_done, t.n - 1)
                        nc.vector.tensor_scalar(onehot[:, t.slot, :], PS[:, 0, 0:WJ * P], part_no[:, 0:1], None,
                                                ALU.is_equal).then_inc(onehot_rdy, 1)

                    def message(t, j, windowed):
                        if j % 2 == 0:
                            dve.wait_ge(w_done, 2 * t.n + j // 2 + 1)
                        if j == 0:
                            wait(dve, mlo_rdy, t.n - 1)
                            if windowed:
                                dve.wait_ge(zx_rdy, t.n + 1)
                            else:
                                dve.wait_ge(z_ld[t.r], 16 * J * (t.q + 1))
                        if j == WJ and windowed:
                            dve.wait_ge(z_ld[t.r], 16 * (J - WJ) * (t.q + 1))
                        nc.vector.scalar_tensor_tensor(out=msg[:, t.slot, j, :],
                                                       in0=PS[:, 3 + j // 2, j % 2 * D:(j % 2 + 1) * D],
                                                       scalar=sel[:, t.r, J + j:J + j + 1], in1=zg[:, t.r, j, :],
                                                       op0=ALU.mult, op1=ALU.mult).then_inc(msg_rdy, 1)

                    def edge_work(windowed):
                        def body(s):
                            if windowed and (s + 1).there():
                                hot(s + 1)
                            if (s + -1).there():
                                message_low(s + -1)
                            if (s + 3).there():
                                low(s + 3)
                            if windowed and (s + 2).there():
                                window_low(s + 2)
                            if (s + 1).there():
                                equal(s + 1)
                            if s.there():
                                message(s, 0, windowed)
                                message(s, 1, windowed)
                            if (s + 1).there():
                                hidden(s + 1)
                            if s.there():
                                message(s, 2, windowed)
                                message(s, 3, windowed)
                            if (s + 1).there():
                                targets_f(s + 1)
                                targets(s + 1)

                        steps(dve, body, -3)

                    dve.wait_ge(res_rdy, NT)
                    dve.wait_ge(outside_rdy, 1)
                    general = dve.value_load(outside[0:1, 0:1], min_val=0, max_val=1)
                    with dve.If(general == 0):
                        edge_work(True)
                    with dve.Else():
                        edge_work(False)

                @block.tensor
                def _(pe):
                    pe.wait_ge(consts, 10)
                    pe.wait_ge(prow_rdy, 2)
                    for k in range(3 * RB):
                        rows, a = (r_srcf, r_c, r_dstf)[k // RB], k % RB
                        wait(pe, pt_free, k - 1)
                        for j in range(J):
                            last = nc.tensor.transpose(PS[:, 4 + k % 2, j * RH:(j + 1) * RH],
                                                       rows.rearrange("p (a q j) -> p a j q", a=RB, j=J)[:, a, j, :],
                                                       ident[0:RH, 0:RH])
                        last.then_inc(pt_done, 1)

                    pe.wait_ge(w_in, 16 * 10)
                    for c in range(KC):
                        nc.tensor.transpose(PS[:, 6, c * NX:(c + 1) * NX], rw_in[:, c * P:(c + 1) * P], ident[0:NX, 0:NX])
                    for c in range(KC):
                        last = nc.tensor.matmul(PS[0:1, 7, 0:D], neg_ln2[:], w2_sb[:, c, :], start=(c == 0),
                                                stop=(c == KC - 1))
                    last.then_inc(wprep_mm, 1)
                    pe.wait_ge(reach_rdy, 1)
                    nc.tensor.transpose(PS[0:1, 6, 256:256 + RH], reach[:], ident[0:RH, 0:RH]).then_inc(reach_done, 1)

                    def flip(t):
                        pe.wait_ge(xn_rdy, t.n + 1)
                        wait(pe, xT_rdy, t.n - 1)
                        for c in range(KC):
                            last = nc.tensor.transpose(PS[:, t.slot, c * P:(c + 1) * P],
                                                       xn[:, t.r, c * P:(c + 1) * P], ident[:])
                        last.then_inc(xnt_done, 1)

                    def product(t):
                        pe.wait_ge(xT_rdy, t.n + 1)
                        wait(pe, zb_rdy, t.n - 1)
                        for c in range(KC):
                            last = nc.tensor.matmul(PS[:, 2 + t.slot, 0:D], xT[:, t.slot, c * P:(c + 1) * P],
                                                    lin1_sb[:, c, :], start=(c == 0), stop=(c == KC - 1))
                        last.then_inc(mmz_done, 1)

                    def norm_step(s):
                        if (s + 2).there():
                            flip(s + 2)
                        if s.there():
                            product(s)

                    run_steps(pe, norm_step, -2, NT, U, NT)
                    pe.wait_ge(zb_rdy, NT)
                    pe.wait_ge(pt_free, 3 * RB)

                    def spread(t, windowed):
                        pe.wait_ge(dg_ld[t.r], 16 * (t.q + 1))
                        if windowed:
                            pe.wait_ge(aT_rdy, t.n + 1)
                            nc.tensor.matmul(PS[:, 0, 0:WJ * P], digit_w[:], digits[:, t.r, SE:DW], start=True,
                                             stop=True).then_inc(rel_done, 1)
                            wait(pe, zx_rdy, t.n)
                        wait(pe, same_rdy, J * t.n)
                        nc.tensor.matmul(PS[:, 5, :], digit_w[:], digits[:, t.r, 0:SE], start=True, stop=True
                                         ).then_inc(dg_done, 1)

                    def expand(t):
                        pe.wait_ge(zwhi_rdy, t.n + 1)
                        pe.wait_ge(zwlo_rdy, t.n + 1)
                        pe.wait_ge(onehot_rdy, t.n + 1)
                        pe.wait_ge(same_rdy, J * t.n + J)
                        for j in range(WJ):
                            for part in (zw_hi, zw_lo):
                                last = nc.tensor.matmul(PS[:, 5, j * D:(j + 1) * D],
                                                        onehot[:, t.slot, j * P:(j + 1) * P], part[:, t.slot, :],
                                                        start=(part is zw_hi), stop=(part is zw_lo))
                        last.then_inc(expand_done, 1)

                    def turn_features(t, windowed):
                        pe.wait_ge(lo_rdy, t.n + 1)
                        wait(pe, aT_rdy, t.n)
                        if windowed:
                            wait(pe, onehot_rdy, t.n)
                        for j in range(J):
                            last = nc.tensor.transpose(PS[:, 0, j * P:(j + 1) * P].bitcast(F32R),
                                                       a_hl[:, t.slot, j, :], ident_r[:])
                        last.then_inc(at_done, 1)

                    def first_layer(t):
                        pe.wait_ge(aT_rdy, t.n + 1)
                        wait(pe, h_rdy, KC * t.n)
                        for c in range(KC):
                            nc.tensor.matmul(PS[:, 1 + c, :], w1_hh[:, c * P:(c + 1) * P], aT[:, t.slot, :],
                                             start=True, stop=False)
                            nc.tensor.matmul(PS[:, 1 + c, :], w1_lo[:, c * P:(c + 1) * P], aT[0:G + 1, t.slot, :],
                                             start=False, stop=True).then_inc(pre_done, 1)

                    def second_layer(t):
                        pe.wait_ge(h_rdy, KC * t.n + KC)
                        for j in range(J):
                            if j % 2 == 0:
                                wait(pe, msg_rdy, J * (t.n - 1) + j + 2)
                            o = PS[:, 3 + j // 2, j % 2 * D:(j % 2 + 1) * D]
                            nc.tensor.matmul(o, ones_r[:], b2_hl[:], start=True, stop=False)
                            for c in range(KC):
                                last = nc.tensor.matmul(o, hT[:, t.slot, c, j * P:(j + 1) * P], w2_sb[:, c, :],
                                                        start=False, stop=(c == KC - 1))
                            if j % 2:
                                last.then_inc(w_done, 1)

                    def combine(t):
                        pe.wait_ge(same_rdy, J * t.n + J)
                        wait(pe, sum_rdy, t.n)
                        pe.wait_ge(mhi_rdy, t.n + 1)
                        pe.wait_ge(mlo_rdy, t.n + 1)
                        for j in range(J):
                            for k, part in enumerate((msg_hi[:, t.slot, j, :], msg_lo[:, t.slot, j, :])):
                                last = nc.tensor.matmul(PS[:, 6 + j // 2, j % 2 * D:(j % 2 + 1) * D],
                                                        same[:, t.r, j, :], part, start=(k == 0), stop=(k == 1))
                        last.then_inc(sum_done, 1)

                    pe.wait_ge(wprep, 2)

                    def edge_work(windowed):
                        def body(s):
                            if (s + 1).there():
                                first_layer(s + 1)
                                spread(s + 1, windowed)
                            if s.there():
                                second_layer(s)
                            if (s + 2).there():
                                turn_features(s + 2, windowed)
                            if windowed and (s + 1).there():
                                expand(s + 1)
                            if (s + -1).there():
                                combine(s + -1)

                        steps(pe, body, -2)

                    pe.wait_ge(outside_rdy, 1)
                    general = pe.value_load(outside[0:1, 0:1], min_val=0, max_val=1)
                    with pe.If(general == 0):
                        edge_work(True)
                    with pe.Else():
                        edge_work(False)

        ag = sb("ag", [P, U, J, D])
        agsum = sb("agsum", [P, U, D])
        expn = sb("expn", [P, U, D])
        soft = sb("soft", [P, U, D])
        aggT = sb("aggT", [P, U, D])
        centred = sb("centred", [P, U, D])
        centT = sb("centT", [P, 2, D])
        neg_mean = sb("neg_mean", [P, U])
        lg = sb("lg", [P, NT, NX])
        oh = sb("oh", [P, NT, NX])
        oh_bf = sb("oh_bf", [P, NT, NX], BF16)
        best = sb("best", [P, NT])
        rank_w = sb("rank_w", [P, NX])
        valid = sb("valid", [P, 1])
        tot = sb("tot", [P, NX, NT])
        off = sb("off", [P, NX, NT])
        onesv = sb("onesv", [P, NX * NT])
        cnt = sb("cnt", [P, NX])
        pad_i = sb("pad_i", [P, NX], I32)
        padded = sb("padded", [P, NX])
        pend = sb("pend", [P, NX])
        shift = sb("shift", [P, NX])
        place = sb("place", [P, NT])
        info = sb("info", [P, NT, XW - D])
        back = sb("back", [P, NT])
        tile_no = sb("tile_no", [ET, 1])
        behind = sb("behind", [ET, NX])
        expert_f = sb("expert_f", [ET, 1])
        expert = sb("expert", [1, ET], I32)
        place_c = sb("place_c", [P, U, 1], I32)
        row_c = sb("row_c", [P, U, XW])
        zeros2 = sb("zeros2", [P, XZ])
        xe = sb("xe", [P, UE, XW])
        xen = sb("xen", [P, U, D])
        dest_c = sb("dest_c", [P, UE, 1], I32)
        we = sb("we", [P, UE, WW])
        he = sb("he", [H + 1, U, P])
        yo = ag[:].rearrange("p u j d -> p (u j) d")[:, 0:UE]

        ag_ld = [sem(f"ag_ld{b}") for b in range(U)]
        ag_sum = sem("ag_sum")
        agt_done = sem("agt_done")
        agT_rdy = sem("agT_rdy")
        lin2_done = sem("lin2_done")
        abs_done = sem("abs_done")
        expn_done = sem("expn_done")
        lnn_done = sem("lnn_done")
        soft_rdy = sem("soft_rdy")
        x2_rdy = sem("x2_rdy")
        st2_rdy = sem("st2_rdy")
        consts2 = sem("consts2")
        mean_rdy = sem("mean_rdy")
        cent_rdy = sem("cent_rdy")
        centt_done = sem("centt_done")
        centT_rdy = sem("centT_rdy")
        lg_done = sem("lg_done")
        lg_rdy = sem("lg_rdy")
        oh_rdy = sem("oh_rdy")
        count_done = sem("count_done")
        placed = sem("placed")
        info_made = sem("info_made")
        exp_col = sem("exp_col")
        exp_row = sem("exp_row")
        pc_rdy = sem("pc_rdy")
        row_rdy = sem("row_rdy")
        info_rdy = sem("info_rdy")
        sorted_in = [sem(f"sorted_in{b}") for b in range(U)]
        ex_rdy = sem("ex_rdy")
        zero2_rdy = sem("zero2_rdy")
        ex_ld = [sem(f"ex_ld{b}") for b in range(UE)]
        xen_rdy = sem("xen_rdy")
        xet_done = sem("xet_done")
        xeT_rdy = sem("xeT_rdy")
        dest_rdy = sem("dest_rdy")
        l1_done = sem("l1_done")
        he_rdy = sem("he_rdy")
        l2_done = sem("l2_done")
        yo_rdy = sem("yo_rdy")
        y_out = [sem(f"y_out{b}") for b in range(UE)]
        he_ones = sem("he_ones")

        with nc.Block() as block:
            @block.sync
            def _(sp):
                def load_sums(t):
                    wait(sp, ag_sum, t.n - U + 1)
                    for j in range(J):
                        sp.dma_start(ag[:, t.r, j, :], agg_dram[j][ds(t.n * P, P), :]).then_inc(ag_ld[t.r], 16)

                run_steps(sp, load_sums, 0, NT, U, NT)

                def stage_experts():
                    sp.wait_ge(zero2_rdy, 1)
                    flat = xs_dram.rearrange("(p k) d -> p (k d)", p=P)
                    for k in range(flat.shape[1] // XZ):
                        sp.dma_start(flat[:, k * XZ:(k + 1) * XZ], zeros2[:]).then_inc(staged, 16)
                    for c in range(KC):
                        sp.dma_start(wtab[:, :, c * H:(c + 1) * H], ffn_w1[:, c * P:(c + 1) * P, :]
                                     ).then_inc(staged, 16)
                    for k in range(2):
                        sp.dma_start(wtab[:, k * H:(k + 1) * H, KC * H:KC * H + D], ffn_w2).then_inc(staged, 16)
                        sp.dma_start(wtab[:, k * H:(k + 1) * H, WW - 1], ffn_b1,
                                     allow_slow_non_contiguous=True).then_inc(staged, 16)
                    sp.wait_ge(staged, 16 * (ET * XW // XZ + 6))
                    sp.dma_start(wtab[:, H, KC * H:KC * H + D], ffn_b2).then_inc(staged, 16)

                stage_experts()
                sp.wait_ge(staged, 16 * (ET * XW // XZ + 7))
                sp.wait_ge(ex_rdy, 1)

                def load_expert(t):
                    e = sp.value_load(expert[0:1, ds(t.n, 1)], min_val=0, max_val=NX - 1)
                    wait(sp, l2_done, t.n - UE + 1)
                    sp.dma_start(we[:, t.r, :], wtab[ds(e, 1)].rearrange("a p w -> p (a w)")).then_inc(ex_ld[t.r], 16)

                run_steps(sp, load_expert, 0, ET, UE, ET)

                for b in range(UE):
                    sp.wait_ge(y_out[b], 16 * len(range(b, ET, UE)))

            @block.gpsimd
            def _(pool):
                nc.gpsimd.memset(zeros2[:], 0.0).then_inc(zero2_rdy, 1)
                nc.gpsimd.iota(rank_w[:], pattern=[[-1, NX]], base=NX, channel_multiplier=0,
                               allow_small_or_imprecise_dtypes=True).then_inc(consts2, 1)
                nc.gpsimd.iota(tile_no[:], pattern=[[0, 1]], base=0, channel_multiplier=1,
                               allow_small_or_imprecise_dtypes=True).then_inc(consts2, 1)
                nc.gpsimd.iota(back[:], pattern=[[P, NT]], base=-PADDEST, channel_multiplier=1,
                               allow_small_or_imprecise_dtypes=True).then_inc(consts2, 1)
                nc.gpsimd.memset(onesv[:], 1.0).then_inc(consts2, 1)
                nc.gpsimd.affine_select(out=valid[:], in_=neg_ln2[:], compare_op=ALU.is_gt, fill=0.0, base=NLAST,
                                        pattern=[[0, 1]], channel_multiplier=-1).then_inc(consts2, 1)

                def residual(t):
                    pool.wait_ge(soft_rdy, t.n + 1)
                    nc.gpsimd.tensor_tensor(node_row(x_sb, t.n), node_row(x_sb, t.n), soft[:, t.r, :], ALU.add
                                            ).then_inc(x2_rdy, 1)

                run_steps(pool, residual, 0, NT, U, NT)

                def sort_rows(t):
                    wait_apart(pool, pc_rdy, t.n + 1, pool_passed)
                    wait_apart(pool, info_rdy, t.n + 1, pool_passed)
                    wait_apart(pool, row_rdy, t.n + 1, pool_passed)
                    rows = NLAST if isinstance(t.q, int) and t.n == NT - 1 else P
                    nc.gpsimd.indirect_dma_start(
                        out=xs_dram, out_offset=bass.IndirectOffsetOnAxis(ap=place_c[0:rows, t.r, :], axis=0),
                        in_=row_c[0:rows, t.r, :], in_offset=None).then_inc(sorted_in[t.r], 16)

                pool.wait_ge(staged, 16 * (ET * XW // XZ + 7))
                run_steps(pool, sort_rows, 0, NT, U, NT)

                def deliver(t):
                    wait_apart(pool, dest_rdy, t.n + 1, pool_passed)
                    wait_apart(pool, yo_rdy, t.n + 1, pool_passed)
                    nc.gpsimd.indirect_dma_start(
                        out=out, out_offset=bass.IndirectOffsetOnAxis(ap=dest_c[:, t.r, :], axis=0),
                        in_=yo[:, t.r, :], in_offset=None, bounds_check=N - 1, oob_is_err=False
                    ).then_inc(y_out[t.r], 16)

                run_steps(pool, deliver, 0, ET, UE, ET)

            @block.scalar
            def _(act):
                nc.scalar.preload_act_table_set("natural_log_exp_and_others")

                def turned(t):
                    act.wait_ge(agt_done, t.n + 1)
                    wait(act, lin2_done, t.n - U + 1)
                    nc.scalar.copy(aggT[:, t.r, :], PS[:, t.slot, 0:D]).then_inc(agT_rdy, 1)

                def softplus(t):
                    act.wait_ge(lin2_done, t.n + 1)
                    wait(act, soft_rdy, t.n - U + 1)
                    nc.scalar.activation(expn[:, t.r, :], PS[:, 2 + t.r, 0:D], ACT.Abs).then_inc(abs_done, 1)
                    act.wait_ge(abs_done, t.n + 1)
                    nc.scalar.activation(expn[:, t.r, :], expn[:, t.r, :], ACT.Exp, scale=-1.0).then_inc(expn_done, 1)
                    act.wait_ge(expn_done, t.n + 1)
                    nc.scalar.activation(expn[:, t.r, :], expn[:, t.r, :], ACT.Ln, bias=half_c[:],
                                         scale=0.5).then_inc(lnn_done, 1)

                def centre(t):
                    act.wait_ge(mean_rdy, t.n + 1)
                    act.wait_ge(x2_rdy, t.n + 1)
                    wait(act, centt_done, t.n - U + 1)
                    nc.scalar.activation(centred[:, t.r, :], node_row(x_sb, t.n), ACT.Identity,
                                         bias=neg_mean[:, t.r:t.r + 1]).then_inc(cent_rdy, 1)

                def centre_turned(t):
                    act.wait_ge(centt_done, t.n + 1)
                    wait(act, lg_done, t.n - 1)
                    nc.scalar.copy(centT[:, t.slot, :], PS[:, 6, 0:D]).then_inc(centT_rdy, 1)

                def node_step(s):
                    if (s + 1).there():
                        turned(s + 1)
                    if s.there():
                        softplus(s)
                    if (s + -5).there():
                        centre_turned(s + -5)
                    if (s + -4).there():
                        centre(s + -4)

                run_steps(act, node_step, -1, NT + 5, U, NT)

                act.wait_ge(sq_ask, 2)
                nc.scalar.activation(rstd[:], tmp_n[:], ACT.Sqrt).then_inc(sq_rdy, 1)

                def stage_row(t):
                    wait(act, sorted_in[t.r], 16 * t.q)
                    nc.scalar.copy(row_c[:, t.r, 0:D], node_row(x_sb, t.n)).then_inc(row_rdy, 1)

                run_steps(act, stage_row, 0, NT, U, NT)

                def rows_turned(t):
                    act.wait_ge(xet_done, t.n + 1)
                    wait(act, l1_done, t.n - U + 1)
                    nc.scalar.copy(aggT[:, t.r % U, :], PS[:, t.slot, 0:D]).then_inc(xeT_rdy, 1)

                def hidden(t):
                    act.wait_ge(l1_done, t.n + 1)
                    wait(act, l2_done, t.n - U + 1)
                    nc.scalar.activation(he[0:H, t.r % U, :], PS[0:H, 2 + t.slot, 0:P], ACT.Relu,
                                         bias=we[0:H, t.r, WW - 1:WW]).then_inc(he_rdy, 1)

                def load_rows(t):
                    wait(act, yo_rdy, t.n - UE + 1)
                    act.dma_start(xe[:, t.r, :], xs_dram[ds(t.n * P, P), :]).then_inc(ex_ld[t.r], 16)

                act.wait_ge(he_ones, 1)
                for b in range(U):
                    act.wait_ge(sorted_in[b], 16 * len(range(b, NT, U)))

                def expert_step(s):
                    if (s + 5).there():
                        load_rows(s + 5)
                    if (s + 1).there():
                        rows_turned(s + 1)
                    if s.there():
                        hidden(s)

                run_steps(act, expert_step, -5, ET, UE, ET)

            @block.vector
            def _(dve):
                links = [0]

                def link(ins):
                    links[0] += 1
                    ins.then_inc(chain2, 1)
                    dve.wait_ge(chain2, links[0])

                nc.vector.memset(he[:], 1.0).then_inc(he_ones, 1)

                def sum_tables(t):
                    dve.wait_ge(ag_ld[t.r], 16 * J * (t.q + 1))
                    wait(dve, agt_done, t.n - U + 1)
                    nc.vector.tensor_reduce(agsum[:, t.r, :], ag[:, t.r].rearrange("p j d -> p d j"), AX.X,
                                            ALU.add).then_inc(ag_sum, 1)

                def soften(t):
                    dve.wait_ge(lnn_done, t.n + 1)
                    wait(dve, x2_rdy, t.n - U + 1)
                    nc.vector.scalar_tensor_tensor(out=soft[:, t.r, :], in0=PS[:, 2 + t.r, 0:D], scalar=0.0,
                                                   in1=expn[:, t.r, :], op0=ALU.max, op1=ALU.add).then_inc(soft_rdy, 1)

                def statistics(t):
                    dve.wait_ge(x2_rdy, t.n + 1)
                    nc.vector.bn_stats(node_row(stats, t.n), node_row(x_sb, t.n)).then_inc(st2_rdy, 1)

                def mean_of(t):
                    dve.wait_ge(st2_rdy, t.n + 1)
                    wait(dve, cent_rdy, t.n - U + 1)
                    even = stats[:, ds(t.n, 1), 1:2].rearrange("p a d -> p (a d)")
                    odd = stats[:, ds(t.n, 1), 4:5].rearrange("p a d -> p (a d)")
                    nc.vector.tensor_scalar(neg_mean[:, t.r:t.r + 1], even, odd, -0.5, ALU.add, ALU.mult
                                            ).then_inc(mean_rdy, 1)

                def logits(t):
                    dve.wait_ge(lg_done, t.n + 1)
                    nc.vector.tensor_copy(node_row(lg, t.n), PS[:, 7, 0:NX]).then_inc(lg_rdy, 1)

                def node_step(s):
                    if (s + -7).there():
                        logits(s + -7)
                    if (s + -1).there():
                        soften(s + -1)
                    if (s + -3).there():
                        statistics(s + -3)
                    if (s + 2).there():
                        sum_tables(s + 2)
                    if (s + -3).there():
                        mean_of(s + -3)

                run_steps(dve, node_step, -2, NT + 7, U, NT)
                norm_bulk(dve, link, 2)

                dve.wait_ge(lg_rdy, NT)
                dve.wait_ge(consts2, 5)

                def over_experts(a):
                    return a.unsqueeze(2).to_broadcast([P, NT, NX])

                def over_tiles(a):
                    return a.unsqueeze(1).to_broadcast([P, NT, NX])

                link(nc.vector.tensor_tensor(lg[:], lg[:], over_experts(rstd[:]), ALU.mult))
                link(nc.vector.tensor_tensor(lg[:], lg[:], over_tiles(rb_all[:]), ALU.add))
                link(nc.vector.tensor_reduce(best[:], lg[:], AX.X, ALU.max))
                link(nc.vector.tensor_tensor(oh[:], lg[:], over_experts(best[:]), ALU.is_ge))
                link(nc.vector.tensor_tensor(oh[:], oh[:], over_tiles(rank_w[:]), ALU.mult))
                link(nc.vector.tensor_reduce(best[:], oh[:], AX.X, ALU.max))
                nc.vector.tensor_scalar(valid[:], valid[:], 0.0, None, ALU.is_lt).then_inc(chain2, 1)
                links[0] += 1
                link(nc.vector.tensor_tensor(oh_bf[:], over_tiles(rank_w[:]), over_experts(best[:]), ALU.is_equal))
                nc.vector.tensor_scalar(oh_bf[:, NT - 1, :], oh_bf[:, NT - 1, :], valid[:, 0:1], None, ALU.mult
                                        ).then_inc(oh_rdy, 1)
                for k, a in enumerate((mean, rstd, back, back)):
                    nc.vector.tensor_copy(info[:, :, k], a[:]).then_inc(info_made, 1)

                dve.wait_ge(count_done, 1)
                TQ = 512 // NX
                for k in range(4):
                    t0, t1 = k * TQ, min(NT, (k + 1) * TQ)
                    if t0 < NT:
                        nc.vector.tensor_copy(tot[:, :, t0:t1], PS[:, 4 + k, 0:(t1 - t0) * NX].rearrange(
                            "p (t e) -> p e t", e=NX)).then_inc(chain2, 1)
                        links[0] += 1
                dve.wait_ge(chain2, links[0])
                flat_tot, flat_off = tot[:].rearrange("p e t -> p (e t)"), off[:].rearrange("p e t -> p (e t)")
                link(nc.vector.tensor_reduce(cnt[:], tot[:], AX.X, ALU.add))
                link(nc.vector.tensor_scalar(pad_i[:], cnt[:], float(P - 1), None, ALU.add))
                link(nc.vector.tensor_scalar(pad_i[:], pad_i[:], 7, 7, ALU.arith_shift_right, ALU.logical_shift_left))
                link(nc.vector.tensor_copy(padded[:], pad_i[:]))
                link(nc.vector.tensor_tensor_scan(pend[:], onesv[:, 0:NX], padded[:], 0.0, ALU.mult, ALU.add))
                nc.vector.tensor_scalar(pend[:], pend[:], 1.0 / P, None, ALU.mult).then_inc(chain2, 1)
                links[0] += 1
                link(nc.vector.tensor_tensor(shift[:], padded[:], cnt[:], ALU.subtract))
                nc.vector.tensor_tensor(tot[:, 1:NX, 0], tot[:, 1:NX, 0], shift[:, 0:NX - 1], ALU.add).then_inc(chain2, 1)
                links[0] += 1
                nc.vector.scalar_tensor_tensor(out=behind[:], in0=pend[0:ET, :], scalar=tile_no[:, 0:1],
                                               in1=onesv[0:ET, 0:NX], op0=ALU.is_le, op1=ALU.mult,
                                               accum_out=expert_f[:]).then_inc(exp_col, 1)
                dve.wait_ge(chain2, links[0])
                link(nc.vector.tensor_tensor_scan(flat_off, onesv[:], flat_tot, 0.0, ALU.mult, ALU.add))
                for k in range(4):
                    t0, t1 = k * TQ, min(NT, (k + 1) * TQ)
                    if t0 < NT:
                        nc.vector.tensor_tensor(lg[:, t0:t1, :], off[:, :, t0:t1].rearrange("p e t -> p t e"),
                                                PS[:, k, 0:(t1 - t0) * NX].rearrange("p (t e) -> p t e", e=NX), ALU.add
                                                ).then_inc(chain2, 1)
                        links[0] += 1
                dve.wait_ge(chain2, links[0])
                link(nc.vector.tensor_tensor(lg[:], lg[:], oh_bf[:], ALU.mult))
                nc.vector.tensor_reduce(place[:], lg[:], AX.X, ALU.add).then_inc(placed, 1)
                dve.wait_ge(exp_row, 1)
                nc.vector.tensor_scalar(expert[:], PS[0:1, 4, 0:ET], float(NX - 1), None, ALU.min).then_inc(ex_rdy, 1)
                dve.wait_ge(placed, 1)
                dve.wait_ge(info_made, 4)

                def stage_place(t):
                    wait(dve, sorted_in[t.r], 16 * t.q)
                    nc.vector.tensor_copy(place_c[:, t.r, :], place[:, ds(t.n, 1)]).then_inc(pc_rdy, 1)
                    nc.vector.tensor_copy(row_c[:, t.r, D:XW], node_row(info, t.n)).then_inc(info_rdy, 1)

                run_steps(dve, stage_place, 0, NT, U, NT)

                def norm_sorted(t):
                    dve.wait_ge(ex_ld[t.r], 32 * (t.q + 1))
                    wait(dve, xet_done, t.n - U + 1)
                    nc.vector.tensor_scalar(xen[:, t.r % U, :], xe[:, t.r, 0:D], xe[:, t.r, D:D + 1],
                                            xe[:, t.r, D + 1:D + 2], ALU.subtract, ALU.mult).then_inc(xen_rdy, 1)
                    wait(dve, y_out[t.r], 16 * t.q)
                    nc.vector.tensor_scalar(dest_c[:, t.r, :], xe[:, t.r, D + 2:D + 3], float(PADDEST), None,
                                            ALU.add).then_inc(dest_rdy, 1)

                def results(t):
                    dve.wait_ge(l2_done, t.n + 1)
                    wait(dve, y_out[t.r], 16 * t.q)
                    nc.vector.scalar_tensor_tensor(out=yo[:, t.r, :], in0=PS[:, 4 + t.r % U, 0:D], scalar=0.0,
                                                   in1=xe[:, t.r, 0:D], op0=ALU.max, op1=ALU.add).then_inc(yo_rdy, 1)

                def expert_step(s):
                    if (s + 3).there():
                        norm_sorted(s + 3)
                    if (s + -2).there():
                        results(s + -2)

                run_steps(dve, expert_step, -3, ET + 2, UE, ET)

            @block.tensor
            def _(pe):
                def turn_rows(source, ready, done, copied, banks):
                    def flip(t):
                        bank = t.r % banks
                        pe.wait_ge(ready, t.n + 1)
                        wait(pe, copied, t.n - banks + 1)
                        for c in range(KC):
                            last = nc.tensor.transpose(PS[:, bank, c * P:(c + 1) * P],
                                                       source[:, t.r % U, c * P:(c + 1) * P], ident[:])
                        last.then_inc(done, 1)
                    return flip

                flip_sums = turn_rows(agsum, ag_sum, agt_done, agT_rdy, 2)

                def lin2(t):
                    pe.wait_ge(agT_rdy, t.n + 1)
                    wait(pe, soft_rdy, t.n - U + 1)
                    nc.tensor.matmul(PS[:, 2 + t.r, 0:D], ones_r[:], lin2b_hl[:], start=True, stop=False)
                    for c in range(KC):
                        last = nc.tensor.matmul(PS[:, 2 + t.r, 0:D], aggT[:, t.r, c * P:(c + 1) * P],
                                                lin2_sb[:, c, :], start=False, stop=(c == KC - 1))
                    last.then_inc(lin2_done, 1)

                def flip_centred(t):
                    pe.wait_ge(cent_rdy, t.n + 1)
                    wait(pe, centT_rdy, t.n)
                    for c in range(KC):
                        last = nc.tensor.transpose(PS[:, 6, c * P:(c + 1) * P],
                                                   centred[:, t.r, c * P:(c + 1) * P], ident[:])
                    last.then_inc(centt_done, 1)

                def router(t):
                    pe.wait_ge(centT_rdy, t.n + 1)
                    wait(pe, lg_rdy, t.n)
                    for c in range(KC):
                        last = nc.tensor.matmul(PS[:, 7, 0:NX], centT[:, t.slot, c * P:(c + 1) * P],
                                                rwT[:, c, :], start=(c == 0), stop=(c == KC - 1))
                    last.then_inc(lg_done, 1)

                def node_step(s):
                    if (s + 1).there():
                        flip_sums(s + 1)
                    if s.there():
                        lin2(s)
                    if (s + -5).there():
                        flip_centred(s + -5)
                    if (s + -6).there():
                        router(s + -6)

                run_steps(pe, node_step, -1, NT + 6, U, NT)

                pe.wait_ge(oh_rdy, 1)
                TQ = 512 // NX
                for half, weights in ((0, minus_from), (4, ones_bf)):
                    for k in range(4):
                        t0, t1 = k * TQ, min(NT, (k + 1) * TQ)
                        if t0 < NT:
                            last = nc.tensor.matmul(PS[:, half + k, 0:(t1 - t0) * NX], weights[:],
                                                    oh_bf[:, t0:t1, :].rearrange("p t e -> p (t e)"), start=True, stop=True)
                last.then_inc(count_done, 1)
                pe.wait_ge(exp_col, 1)
                nc.tensor.matmul(PS[0:1, 4, 0:ET], expert_f[:], ident[0:ET, 0:ET], start=True, stop=True
                                 ).then_inc(exp_row, 1)
                pe.wait_ge(placed, 1)
                pe.wait_ge(ex_rdy, 1)

                flip_expert = turn_rows(xen, xen_rdy, xet_done, xeT_rdy, 2)

                def layer1(t):
                    pe.wait_ge(ex_ld[t.r], 32 * (t.q + 1))
                    pe.wait_ge(xeT_rdy, t.n + 1)
                    wait(pe, he_rdy, t.n - 1)
                    for c in range(KC):
                        last = nc.tensor.matmul(PS[0:H, 2 + t.slot, 0:P], we[:, t.r, c * H:(c + 1) * H],
                                                aggT[:, t.r % U, c * P:(c + 1) * P], start=(c == 0), stop=(c == KC - 1))
                    last.then_inc(l1_done, 1)

                def layer2(t):
                    pe.wait_ge(he_rdy, t.n + 1)
                    wait(pe, yo_rdy, t.n - U + 1)
                    nc.tensor.matmul(PS[:, 4 + t.r % U, 0:D], he[:, t.r % U, :], we[0:H + 1, t.r, KC * H:KC * H + D],
                                     start=True, stop=True).then_inc(l2_done, 1)

                def expert_step(s):
                    if (s + 1).there():
                        flip_expert(s + 1)
                    if s.there():
                        layer1(s)
                    if (s + -1).there():
                        layer2(s + -1)

                run_steps(pe, expert_step, -1, ET + 1, UE, ET)


_INS = ["x", "src", "dst", "edge_attr_3", "edge_attr_50", "L0_gnn_mlp_w1", "L0_gnn_mlp_b1", "L0_gnn_mlp_w2",
        "L0_gnn_mlp_b2", "L0_gnn_lin1_w", "L0_gnn_lin2_w", "L0_gnn_lin2_b", "L0_ffn_router_w", "L0_ffn_router_b",
        "L0_ffn_W1", "L0_ffn_b1", "L0_ffn_W2", "L0_ffn_b2"]


def kernel(**inputs):
    import numpy as _np
    import concourse.bacc as _bacc
    from concourse import mybir as _mybir
    from concourse.bass_utils import run_bass_kernel_spmd as _run

    nc = _bacc.Bacc("TRN2", target_bir_lowering=False, num_devices=1)
    arrays, args = {}, []
    for name in _INS:
        a = _np.ascontiguousarray(inputs[name])
        arrays[f"in_{name}"] = a
        args.append(nc.dram_tensor(f"in_{name}", a.shape, _mybir.dt.from_np(a.dtype), kind="ExternalInput").ap())
    shape = inputs["x"].shape
    result = nc.dram_tensor("out_0", shape, _mybir.dt.float32, kind="ExternalOutput").ap()
    gnn_moe(nc, *args, result)
    r = _run(nc, [arrays], core_ids=[0])
    return r.results[0]["out_0"]
```
